# Optimizing a Trainium2 kernel written in Bass

```python
import numpy as np
import jax
import jax.numpy as jnp

def _softmax(x, axis=-1):
    return jax.nn.softmax(x, axis=axis)

def _gelu(x):
    return jax.nn.gelu(x, approximate=True)

def _silu(x):
    return jax.nn.silu(x)

def _sigmoid(x):
    return jax.nn.sigmoid(x)

def _layernorm(x, axis=-1, eps=1e-05):
    m = jnp.mean(x, axis=axis, keepdims=True)
    v = jnp.var(x, axis=axis, keepdims=True)
    return (x - m) / jnp.sqrt(v + eps)

def _scatter_add(tgt, idx, src, axis=0):
    return tgt.at[idx].add(src)

def _segment_sum(src, seg, n):
    return jax.ops.segment_sum(src, seg, n)
kernel_name = 'mk_seq_postln_d2_jaxref_r4_e60236'

def setup_inputs(seed: int=0):
    np.random.seed(seed)
    _w = jnp.asarray

    def _L0_attn_setup():
        import jax, jax.numpy as jnp
        import numpy as np
        from jax import lax
        D = 256
        E = 2
        DI = D * E
        DS = 16
        DK = 3
        DTR = 64
        B = 2
        L = 1024

        def _silu(v):
            return v * jax.nn.sigmoid(v)

        def _forward(x, W_in, W_conv, W_xproj, W_dt, b_dt, W_out, ln_g, ln_b):
            xz = x @ W_in
            xs, z = jnp.split(xz, 2, axis=-1)
            xc = lax.conv_general_dilated(xs.transpose(0, 2, 1), W_conv, (1,), [(DK // 2, DK // 2)], dimension_numbers=('NCH', 'OIH', 'NCH'), feature_group_count=DI)
            xs = _silu(xc.transpose(0, 2, 1))
            xp = xs @ W_xproj
            dt_lo = xp[..., :DTR]
            Bp = xp[..., DTR:DTR + DS]
            Cp = xp[..., DTR + DS:]
            dt = jax.nn.softplus(dt_lo @ W_dt + b_dt)
            dtm = dt.mean(-1)
            xm = xs.mean(-1)
            decay = jnp.exp(-dtm)
            Bx = Bp * xm[..., None]

            def step(h, inp):
                d, bx = inp
                h = h * d[:, None] + bx
                return (h, h.sum(-1))
            h0 = jnp.zeros((x.shape[0], DS), x.dtype)
            _, S = lax.scan(step, h0, (decay.T, Bx.transpose(1, 0, 2)))
            y = Cp * S.T[..., None]
            y = jnp.tile(y, (1, 1, DI // DS))
            mu = y.mean(-1, keepdims=True)
            var = y.var(-1, keepdims=True)
            y = (y - mu) * lax.rsqrt(var + 1e-05) * ln_g + ln_b
            y = y * _silu(z)
            return y @ W_out
        key = jax.random.key(seed)
        ks = jax.random.split(key, 8)
        s = 0.02
        return {'x': jax.random.normal(ks[0], (B, L, D), jnp.float32), 'W_in': jax.random.normal(ks[1], (D, 2 * DI), jnp.float32) * s, 'W_conv': jax.random.normal(ks[2], (DI, 1, DK), jnp.float32) * s, 'W_xproj': jax.random.normal(ks[3], (DI, DTR + 2 * DS), jnp.float32) * s, 'W_dt': jax.random.normal(ks[4], (DTR, DI), jnp.float32) * s, 'b_dt': jax.random.normal(ks[5], (DI,), jnp.float32) * s, 'W_out': jax.random.normal(ks[6], (DI, D), jnp.float32) * s, 'ln_g': jnp.ones((DI,), jnp.float32), 'ln_b': jnp.zeros((DI,), jnp.float32)}
    _L0_attn_in = _L0_attn_setup()

    def _L0_ffn_setup():
        import jax, jax.numpy as jnp
        import numpy as np
        from jax import lax
        DIM = 256
        INTER = 128
        N_EXPERTS = 16
        TOPK = 4
        ROUTE_SCALE = 2.5
        VOCAB = 8000

        def _silu_and_mul(gu):
            gate, up = jnp.split(gu, 2, axis=-1)
            return jax.nn.silu(gate) * up
        key = jax.random.key(seed)
        ks = jax.random.split(key, 8)
        x = jax.random.normal(ks[0], (2, 128, DIM), dtype=jnp.float32)
        input_ids = jax.random.randint(ks[1], (2, 128), 0, VOCAB)
        s = 0.02
        gate_w = jax.random.normal(ks[2], (N_EXPERTS, DIM), dtype=jnp.float32) * s
        gate_b = jax.random.normal(ks[3], (N_EXPERTS,), dtype=jnp.float32) * s
        w13 = jax.random.normal(ks[4], (N_EXPERTS, 2 * INTER, DIM), dtype=jnp.float32) * s
        w2 = jax.random.normal(ks[5], (N_EXPERTS, DIM, INTER), dtype=jnp.float32) * s
        w13_s = jax.random.normal(ks[6], (2 * INTER, DIM), dtype=jnp.float32) * s
        w2_s = jax.random.normal(ks[7], (DIM, INTER), dtype=jnp.float32) * s
        return {'x': x, 'input_ids': input_ids, 'gate_w': gate_w, 'gate_b': gate_b, 'w13': w13, 'w2': w2, 'w13_s': w13_s, 'w2_s': w2_s}
    _L0_ffn_in = _L0_ffn_setup()

    def _L1_attn_setup():
        import jax, jax.numpy as jnp
        import numpy as np
        import math
        DIM, H, T, B = (256, 16, 512, 1)
        BASE = 15000.0

        def _count_mask(t_len, n_heads):
            idx = jnp.arange(t_len)
            hm = jnp.arange(n_heads)
            count = jnp.zeros((n_heads, t_len, t_len), jnp.float32)
            for X in range(int(math.log2(t_len))):
                S, r = (2 ** (X + 2), 2 ** X)
                same_seg = idx[:, None] // S == idx[None, :] // S
                ok = idx[None, :] % r == hm[:, None] % r
                pat = same_seg[None, :, :] & ok[:, :, None] & ok[:, None, :]
                count = count + pat.astype(jnp.float32)
            return count
        key = jax.random.key(seed)
        ks = jax.random.split(key, 9)
        s = 0.02
        d = DIM
        return {'x': jax.random.normal(ks[0], (B, T, d), jnp.float32), 'Wq': jax.random.normal(ks[1], (d, d), jnp.float32) * s, 'bq': jnp.zeros((d,), jnp.float32), 'Wk': jax.random.normal(ks[2], (d, d), jnp.float32) * s, 'bk': jnp.zeros((d,), jnp.float32), 'Wv': jax.random.normal(ks[3], (d, d), jnp.float32) * s, 'bv': jnp.zeros((d,), jnp.float32), 'Wo': jax.random.normal(ks[4], (d, d), jnp.float32) * s, 'bo': jnp.zeros((d,), jnp.float32)}
    _L1_attn_in = _L1_attn_setup()

    def _L1_ffn_setup():
        import jax, jax.numpy as jnp
        import numpy as np
        IN_DIM = 256
        HIDDEN = 256
        OUT_DIM = 256
        NUM_EXPERTS = 16
        TOP_K = 2
        ROUTER_TEMP = 1.0
        LN_EPS = 1e-05

        def _layernorm(h, g, b):
            mu = jnp.mean(h, axis=-1, keepdims=True)
            var = jnp.mean(jnp.square(h - mu), axis=-1, keepdims=True)
            return (h - mu) * jax.lax.rsqrt(var + LN_EPS) * g + b
        key = jax.random.key(seed)
        ks = jax.random.split(key, 8)
        s_in = 1.0 / np.sqrt(IN_DIM)
        s_h = 1.0 / np.sqrt(HIDDEN)
        x = jax.random.normal(ks[0], (4, 512, IN_DIM), dtype=jnp.float32)
        Wr = jax.random.uniform(ks[1], (IN_DIM, NUM_EXPERTS), jnp.float32, -s_in, s_in)
        br = jax.random.uniform(ks[2], (NUM_EXPERTS,), jnp.float32, -s_in, s_in)
        W1 = jax.random.uniform(ks[3], (NUM_EXPERTS, IN_DIM, HIDDEN), jnp.float32, -s_in, s_in)
        b1 = jax.random.uniform(ks[4], (NUM_EXPERTS, HIDDEN), jnp.float32, -s_in, s_in)
        g1 = jnp.ones((NUM_EXPERTS, HIDDEN), jnp.float32)
        be1 = jnp.zeros((NUM_EXPERTS, HIDDEN), jnp.float32)
        W2 = jax.random.uniform(ks[5], (NUM_EXPERTS, HIDDEN, OUT_DIM), jnp.float32, -s_h, s_h)
        b2 = jax.random.uniform(ks[6], (NUM_EXPERTS, OUT_DIM), jnp.float32, -s_h, s_h)
        return {'x': x, 'Wr': Wr, 'br': br, 'W1': W1, 'b1': b1, 'g1': g1, 'be1': be1, 'W2': W2, 'b2': b2}
    _L1_ffn_in = _L1_ffn_setup()
    _d = {'L0_attn_x': _L0_attn_in['x'], 'L0_attn_W_in': _L0_attn_in['W_in'], 'L0_attn_W_conv': _L0_attn_in['W_conv'], 'L0_attn_W_xproj': _L0_attn_in['W_xproj'], 'L0_attn_W_dt': _L0_attn_in['W_dt'], 'L0_attn_b_dt': _L0_attn_in['b_dt'], 'L0_attn_W_out': _L0_attn_in['W_out'], 'L0_attn_ln_g': _L0_attn_in['ln_g'], 'L0_attn_ln_b': _L0_attn_in['ln_b'], 'L0_ffn_input_ids': _L0_ffn_in['input_ids'], 'L0_ffn_gate_w': _L0_ffn_in['gate_w'], 'L0_ffn_gate_b': _L0_ffn_in['gate_b'], 'L0_ffn_w13': _L0_ffn_in['w13'], 'L0_ffn_w2': _L0_ffn_in['w2'], 'L0_ffn_w13_s': _L0_ffn_in['w13_s'], 'L0_ffn_w2_s': _L0_ffn_in['w2_s'], 'L1_attn_Wq': _L1_attn_in['Wq'], 'L1_attn_bq': _L1_attn_in['bq'], 'L1_attn_Wk': _L1_attn_in['Wk'], 'L1_attn_bk': _L1_attn_in['bk'], 'L1_attn_Wv': _L1_attn_in['Wv'], 'L1_attn_bv': _L1_attn_in['bv'], 'L1_attn_Wo': _L1_attn_in['Wo'], 'L1_attn_bo': _L1_attn_in['bo'], 'L1_ffn_Wr': _L1_ffn_in['Wr'], 'L1_ffn_br': _L1_ffn_in['br'], 'L1_ffn_W1': _L1_ffn_in['W1'], 'L1_ffn_b1': _L1_ffn_in['b1'], 'L1_ffn_g1': _L1_ffn_in['g1'], 'L1_ffn_be1': _L1_ffn_in['be1'], 'L1_ffn_W2': _L1_ffn_in['W2'], 'L1_ffn_b2': _L1_ffn_in['b2']}
    _x0 = _d['L0_attn_x']
    _d['L0_attn_x'] = jax.random.normal(jax.random.fold_in(jax.random.key(seed), 1), (4, 1024, 256), dtype=_x0.dtype)
    del _x0
    return _d

def reference(L0_attn_x, L0_attn_W_in, L0_attn_W_conv, L0_attn_W_xproj, L0_attn_W_dt, L0_attn_b_dt, L0_attn_W_out, L0_attn_ln_g, L0_attn_ln_b, L0_ffn_input_ids, L0_ffn_gate_w, L0_ffn_gate_b, L0_ffn_w13, L0_ffn_w2, L0_ffn_w13_s, L0_ffn_w2_s, L1_attn_Wq, L1_attn_bq, L1_attn_Wk, L1_attn_bk, L1_attn_Wv, L1_attn_bv, L1_attn_Wo, L1_attn_bo, L1_ffn_Wr, L1_ffn_br, L1_ffn_W1, L1_ffn_b1, L1_ffn_g1, L1_ffn_be1, L1_ffn_W2, L1_ffn_b2):

    def _L0_attn_ref(x, W_in, W_conv, W_xproj, W_dt, b_dt, W_out, ln_g, ln_b):
        import jax, jax.numpy as jnp
        import numpy as np
        from jax import lax
        D = 256
        E = 2
        DI = D * E
        DS = 16
        DK = 3
        DTR = 64
        B = 2
        L = 1024

        def _silu(v):
            return v * jax.nn.sigmoid(v)

        def _forward(x, W_in, W_conv, W_xproj, W_dt, b_dt, W_out, ln_g, ln_b):
            xz = x @ W_in
            xs, z = jnp.split(xz, 2, axis=-1)
            xc = lax.conv_general_dilated(xs.transpose(0, 2, 1), W_conv, (1,), [(DK // 2, DK // 2)], dimension_numbers=('NCH', 'OIH', 'NCH'), feature_group_count=DI)
            xs = _silu(xc.transpose(0, 2, 1))
            xp = xs @ W_xproj
            dt_lo = xp[..., :DTR]
            Bp = xp[..., DTR:DTR + DS]
            Cp = xp[..., DTR + DS:]
            dt = jax.nn.softplus(dt_lo @ W_dt + b_dt)
            dtm = dt.mean(-1)
            xm = xs.mean(-1)
            decay = jnp.exp(-dtm)
            Bx = Bp * xm[..., None]

            def step(h, inp):
                d, bx = inp
                h = h * d[:, None] + bx
                return (h, h.sum(-1))
            h0 = jnp.zeros((x.shape[0], DS), x.dtype)
            _, S = lax.scan(step, h0, (decay.T, Bx.transpose(1, 0, 2)))
            y = Cp * S.T[..., None]
            y = jnp.tile(y, (1, 1, DI // DS))
            mu = y.mean(-1, keepdims=True)
            var = y.var(-1, keepdims=True)
            y = (y - mu) * lax.rsqrt(var + 1e-05) * ln_g + ln_b
            y = y * _silu(z)
            return y @ W_out
        return _forward(x, W_in, W_conv, W_xproj, W_dt, b_dt, W_out, ln_g, ln_b)

    def _L0_ffn_ref(x, input_ids, gate_w, gate_b, w13, w2, w13_s, w2_s):
        import jax, jax.numpy as jnp
        import numpy as np
        from jax import lax
        DIM = 256
        INTER = 128
        N_EXPERTS = 16
        TOPK = 4
        ROUTE_SCALE = 2.5
        VOCAB = 8000

        def _silu_and_mul(gu):
            gate, up = jnp.split(gu, 2, axis=-1)
            return jax.nn.silu(gate) * up
        B, S, D = x.shape
        xt = x.reshape(-1, D)
        T = xt.shape[0]
        scores = jax.nn.sigmoid(xt.astype(jnp.float32) @ gate_w.T)
        biased = scores + gate_b
        _, idx = lax.top_k(biased, TOPK)
        w = jnp.take_along_axis(scores, idx, axis=-1)
        w = w / jnp.sum(w, axis=-1, keepdims=True)
        w = w * ROUTE_SCALE
        comb = jnp.zeros((T, N_EXPERTS), jnp.float32)
        comb = comb.at[jnp.arange(T)[:, None], idx].add(w)
        comb = comb.astype(x.dtype)

        def expert_body(y, args):
            w13_e, w2_e, c_e = args
            h = _silu_and_mul(xt @ w13_e.T)
            return (y + c_e[:, None] * (h @ w2_e.T), None)
        y, _ = lax.scan(expert_body, jnp.zeros_like(xt), (w13, w2, comb.T))
        y = y + _silu_and_mul(xt @ w13_s.T) @ w2_s.T
        return y.astype(x.dtype).reshape(B, S, D)

    def _L1_attn_ref(x, Wq, bq, Wk, bk, Wv, bv, Wo, bo):
        import jax, jax.numpy as jnp
        import numpy as np
        import math
        DIM, H, T, B = (256, 16, 512, 1)
        BASE = 15000.0

        def _count_mask(t_len, n_heads):
            idx = jnp.arange(t_len)
            hm = jnp.arange(n_heads)
            count = jnp.zeros((n_heads, t_len, t_len), jnp.float32)
            for X in range(int(math.log2(t_len))):
                S, r = (2 ** (X + 2), 2 ** X)
                same_seg = idx[:, None] // S == idx[None, :] // S
                ok = idx[None, :] % r == hm[:, None] % r
                pat = same_seg[None, :, :] & ok[:, :, None] & ok[:, None, :]
                count = count + pat.astype(jnp.float32)
            return count
        Bsz, t_len, d = x.shape
        dh = d // H
        q = x @ Wq.T + bq
        k = x @ Wk.T + bk
        v = x @ Wv.T + bv
        inv_freq = 1.0 / BASE ** (jnp.arange(0, d, 2, dtype=jnp.float32) / d)
        tpos = jnp.arange(t_len, dtype=jnp.float32)
        freqs = tpos[:, None] * inv_freq[None, :]
        emb = jnp.concatenate([freqs, freqs], axis=-1)
        cos, sin = (jnp.cos(emb), jnp.sin(emb))

        def rot_half(u):
            return jnp.concatenate([-u[..., d // 2:], u[..., :d // 2]], axis=-1)
        q = q * cos + rot_half(q) * sin
        k = k * cos + rot_half(k) * sin
        Q = q.reshape(Bsz, t_len, H, dh).transpose(0, 2, 1, 3)
        K = k.reshape(Bsz, t_len, H, dh).transpose(0, 2, 1, 3)
        V = v.reshape(Bsz, t_len, H, dh).transpose(0, 2, 1, 3)
        scores = jnp.einsum('bhtd,bhsd->bhts', Q, K)
        count = _count_mask(t_len, H)
        causal = jnp.tril(jnp.ones((t_len, t_len), bool))
        valid = (count > 0) & causal
        att = jnp.where(valid, scores * count, -jnp.inf)
        att = jax.nn.softmax(att, axis=-1)
        out = jnp.einsum('bhts,bhsd->bhtd', att, V)
        out = out.transpose(0, 2, 1, 3).reshape(Bsz, t_len, d)
        return out @ Wo.T + bo

    def _L1_ffn_ref(x, Wr, br, W1, b1, g1, be1, W2, b2):
        import jax, jax.numpy as jnp
        import numpy as np
        IN_DIM = 256
        HIDDEN = 256
        OUT_DIM = 256
        NUM_EXPERTS = 16
        TOP_K = 2
        ROUTER_TEMP = 1.0
        LN_EPS = 1e-05

        def _layernorm(h, g, b):
            mu = jnp.mean(h, axis=-1, keepdims=True)
            var = jnp.mean(jnp.square(h - mu), axis=-1, keepdims=True)
            return (h - mu) * jax.lax.rsqrt(var + LN_EPS) * g + b
        orig_shape = x.shape[:-1]
        x_flat = x.reshape(-1, x.shape[-1])
        logits = (x_flat @ Wr + br) / max(ROUTER_TEMP, 1e-06)
        probs = jax.nn.softmax(logits, axis=-1)
        topk_w, topk_idx = jax.lax.top_k(probs, TOP_K)
        topk_w = topk_w / jnp.clip(jnp.sum(topk_w, axis=-1, keepdims=True), 1e-09)
        h = jnp.einsum('nc,ech->neh', x_flat, W1) + b1
        h = _layernorm(h, g1, be1)
        h = jax.nn.gelu(h, approximate=False)
        expert_out = jnp.einsum('neh,eho->neo', h, W2) + b2
        sel = jnp.take_along_axis(expert_out, topk_idx[:, :, None], axis=1)
        y_flat = jnp.sum(sel * topk_w[:, :, None], axis=1)
        return y_flat.reshape(*orig_shape, y_flat.shape[-1])
    x = L0_attn_x
    x = _layernorm(x + _L0_attn_ref(x, L0_attn_W_in, L0_attn_W_conv, L0_attn_W_xproj, L0_attn_W_dt, L0_attn_b_dt, L0_attn_W_out, L0_attn_ln_g, L0_attn_ln_b), axis=-1)
    x = _layernorm(x + _L0_ffn_ref(x, L0_ffn_input_ids, L0_ffn_gate_w, L0_ffn_gate_b, L0_ffn_w13, L0_ffn_w2, L0_ffn_w13_s, L0_ffn_w2_s), axis=-1)
    x = _layernorm(x + _L1_attn_ref(x, L1_attn_Wq, L1_attn_bq, L1_attn_Wk, L1_attn_bk, L1_attn_Wv, L1_attn_bv, L1_attn_Wo, L1_attn_bo), axis=-1)
    x = _layernorm(x + _L1_ffn_ref(x, L1_ffn_Wr, L1_ffn_br, L1_ffn_W1, L1_ffn_b1, L1_ffn_g1, L1_ffn_be1, L1_ffn_W2, L1_ffn_b2), axis=-1)
    return x

_drawn_inputs = setup_inputs


def setup_inputs(seed=0):
    import zlib

    import numpy as np

    out = dict(_drawn_inputs(seed))
    spreads = {'L0_attn_ln_g': (1.0, 0.6),
     'L0_attn_ln_b': (0.0, 0.309),
     'L1_attn_bq': (0.0, 0.271),
     'L1_attn_bk': (0.0, 0.388),
     'L1_attn_bv': (0.0, 0.1),
     'L1_attn_bo': (0.0, 0.1),
     'L1_ffn_g1': (1.0, 0.2),
     'L1_ffn_be1': (0.0, 0.301)}
    factors = {'L0_attn_W_conv': 8.0,
     'L0_attn_W_xproj': 8.0,
     'L0_attn_W_dt': 8.0,
     'L0_attn_b_dt': 8.0,
     'L1_ffn_b1': 3.202}
    for name, (base, spread) in spreads.items():
        noise = np.random.default_rng([zlib.crc32(name.encode()), seed]).standard_normal(out[name].shape)
        drawn = base * np.exp(spread * noise) if base else spread * noise
        out[name] = jnp.asarray(drawn.astype(out[name].dtype))
    for name, factor in factors.items():
        out[name] = (out[name] * factor).astype(out[name].dtype)
    return out
```

```python
from contextlib import ExitStack

import concourse.bass as bass
import numpy as np
from concourse import mybir


ALU = mybir.AluOpType
ACT = mybir.ActivationFunctionType
AX = mybir.AxisListType
F32 = mybir.dt.float32
F16 = mybir.dt.float16
BF16 = mybir.dt.bfloat16
I32 = mybir.dt.int32

P = 128
D = 256
KD = D // P
B, L = 4, 1024
N = B * L
NT = N // P
TB = L // P
DI, DS, DTR = 512, 16, 64
CI = DI // P
G = L // 512
EPS = 1e-5


class Chain:

    def __init__(self, eng, sem, it=0, per=0):
        self.eng, self.sem, self.it, self.per, self.n = eng, sem, it, per, 0

    def mark(self, ins):
        ins.then_inc(self.sem, 1)
        self.n += 1

    def settle(self):
        self.eng.wait_ge(self.sem, self.it * self.per + self.n)

    def step(self, ins):
        self.mark(ins)
        self.settle()

    def close(self):
        assert self.n == self.per, (self.n, self.per)


def hold(eng, T):
    eng.sem_inc(T["held"], 1)


def mixer(nc, T, W):
    with ExitStack() as ctx:
        def sb(name, shape, dt=F32):
            return ctx.enter_context(nc.sbuf_tensor("mx_" + name, shape, dt))

        def sem(name):
            return ctx.enter_context(nc.semaphore("mx_" + name))

        ident = T["ident"]
        x1 = T["x1"]
        xin = x1[:, :, :].rearrange("p t d -> p (t d)").rearrange("p (k n) -> p k n", k=KD)
        w_in = sb("w_in", [P, KD, 2 * DI])
        w_conv = sb("w_conv", [P, CI, 3])
        w_x = sb("w_x", [P, CI, DTR + 2 * DS])
        w_small = sb("w_small", [P, CI, DS + 2])
        w_dt = sb("w_dt", [DTR + 1, DI])
        w_dtsum = sb("w_dtsum", [DTR + 1, 1])
        w_out = sb("w_out", [P, CI, D])
        ln_g = sb("ln_g", [P, CI])
        ln_b = sb("ln_b", [P, CI])
        xs_pad = [sb(f"xs_pad{i}", [P, L + 2]) for i in range(2)]
        convs = sb("conv", [P, 2, L])
        conv = [convs[:, i, :] for i in range(2)]
        xs = sb("xs", [P, CI, L])
        zs = T["zs"]
        zsil = sb("zsil", [P, CI, L])
        yz = xs
        dtl = sb("dtl", [DTR + 1, L])
        small = sb("small", [P, NT, DS + 2])
        absu = sb("absu", [P, DI])
        expu = sb("expu", [P, DI])
        lnu = sb("lnu", [P, DI])
        sum_abs = sb("sum_abs", [P, TB])
        sum_ln = sb("sum_ln", [P, TB])
        sum_ua = sb("sum_ua", [P, TB])
        sum_dt = sb("sum_dt", [P, NT])
        dec_bx = sb("dec_bx", [P, 2, NT])
        dec_bxT = sb("dec_bxT", [NT, 2, P])
        rows = sb("rows", [B, 2, L])
        s_rows = sb("s_rows", [B, L])
        s_blk = sb("s_blk", [NT, P])
        s_tok = sb("s_tok", [P, NT])
        c_sum = sb("c_sum", [P, NT])
        cc = sb("cc", [P, NT, DS])
        csq = sb("csq", [P, NT, DS])
        c_var = sb("c_var", [P, NT])
        y_var = sb("y_var", [P, NT])
        y_rs = sb("y_rs", [P, NT])
        y_f = sb("y_f", [P, NT])
        yn = sb("yn", [P, NT, DS])
        yrep = sb("yrep", [P, TB, 8, DS])
        res = convs[:, :, :].rearrange("p a n -> p (a n)").rearrange("p (t d) -> p t d", t=TB)
        stats = sb("stats", [P, TB, 6])
        mv = sb("mv", [P, TB, 2])
        x_var = sb("x_var", [P, TB])
        x_rs = sb("x_rs", [P, TB])
        SUMU = TB * (DS + 2)

        consts = sem("consts")
        x_in = [sem(f"x_in{b}") for b in range(B)]
        prep = sem("prep")
        xs_full = sem("xs_full")
        xs_evac = sem("xs_evac")
        z_full = sem("z_full")
        z_evac = sem("z_evac")
        conv_done = sem("conv_done")
        xs_done = sem("xs_done")
        rank_done = sem("rank_done")
        lo_full = sem("lo_full")
        lo_done = sem("lo_done")
        small_done = sem("small_done")
        u_full = sem("u_full")
        u_free = sem("u_free")
        ln_done = sem("ln_done")
        dsum_done = sem("dsum_done")
        act_own = sem("act_own")
        dve_own = sem("dve_own")
        decay_done = sem("decay_done")
        bx_done = sem("bx_done")
        turned = sem("turned")
        turned_out = sem("turned_out")
        to_dram = sem("to_dram")
        rows_in = sem("rows_in")
        scanned = sem("scanned")
        s_dram = sem("s_dram")
        s_in = sem("s_in")
        s_turned = sem("s_turned")
        y_var_done = sem("y_var_done")
        y_rs_done = sem("y_rs_done")
        x_res = sem("x_res")

        mixed = T["mixed"]
        states = T["states"]

        with ExitStack() as pctx, nc.Block() as block:
            def ps(name):
                return pctx.enter_context(nc.psum_tensor("mx_" + name, [P, 512], F32))

            pA = [ps(f"pA{i}") for i in range(2)]
            pZ = [ps(f"pZ{i}") for i in range(2)]
            pU = [ps(f"pU{i}") for i in range(2)]
            pL = ps("pL")
            pS = ps("pS")

            @block.sync
            def _(sp):
                xT = W["xT"].rearrange("(k p) n -> p k n", p=P)
                sp.dma_start(w_in[:], W["W_in"].rearrange("(k p) n -> p k n", p=P)).then_inc(consts, 16)
                sp.dma_start(xin[:, :, 0:L], xT[:, :, 0:L]).then_inc(x_in[0], 16)
                for dst, src in ((w_conv[:], W["W_conv"].rearrange("(c p) a k -> p c (a k)", p=P)),
                                 (w_x[:], W["W_xproj"].rearrange("(c p) n -> p c n", p=P)),
                                 (w_dt[0:DTR, :], W["W_dt"]),
                                 (w_dt[DTR:DTR + 1, :], W["b_dt"].rearrange("(a n) -> a n", a=1)),
                                 (ident[:], W["ident"]),
                                 (ln_g[:], W["ln_g"]),
                                 (ln_b[:], W["ln_b"]),
                                 (w_out[:], W["W_out"].rearrange("(c p) n -> p c n", p=P))):
                    sp.dma_start(dst, src).then_inc(consts, 16)
                for b in range(1, B):
                    sp.dma_start(xin[:, :, b * L:(b + 1) * L], xT[:, :, b * L:(b + 1) * L]).then_inc(x_in[b], 16)
                sp.wait_ge(turned_out, 1)
                sp.dma_start(mixed.rearrange("a (q p) -> q a p", p=P), dec_bxT[:, :, :]).then_inc(to_dram, 16)
                sp.wait_ge(to_dram, 16)
                sp.dma_start(rows[:, :, :], mixed.rearrange("a (b l) -> b a l", b=B)).then_inc(rows_in, 16)
                sp.wait_ge(z_full, B * CI * G)
                sp.dma_start(x1[:, :, :], W["x"].rearrange("(t p) d -> p t d", p=P)).then_inc(x_res, 16)
                sp.wait_ge(scanned, 1)
                sp.dma_start(states.rearrange("(b l) -> b l", b=B), s_rows[:, :]).then_inc(s_dram, 16)
                sp.wait_ge(s_dram, 16)
                sp.dma_start(s_blk[:, :], states.rearrange("(q p) -> q p", p=P)).then_inc(s_in, 16)
                sp.wait_ge(x_res, 16)

            @block.tensor
            def _(pe):
                pe.sem_inc(rank_done, 1)
                pe.sem_inc(lo_full, 1)
                pe.wait_ge(consts, 16 * 9)
                pe.wait_ge(prep, 9)
                for b in range(B):
                    pe.wait_ge(x_in[b], 16)
                with pe.Fori(0, B) as b:
                    def proj(j, ring, full, evac, n):
                        m, g = j // G, j % G
                        pe.wait_ge(evac, b * 8 + n + 1)
                        for k in range(KD):
                            mm = pe.matmul(ring[n % 2][:, :], w_in[:, k, m * P:(m + 1) * P],
                                           xin[:, k, bass.ds(b * L + g * 512, 512)],
                                           start=k == 0, stop=k == KD - 1)
                        mm.then_inc(full, 1)

                    for j in range(8):
                        proj(j, pA, xs_full, xs_evac, j)
                    for j in range(2):
                        proj(8 + j, pZ, z_full, z_evac, j)
                    pe.wait_ge(xs_done, b * CI + 2 + CI)
                    for g in range(G):
                        pe.wait_ge(lo_done, b * G + g + 1)
                        for c in range(CI):
                            mm = pe.matmul(pL[0:DTR, :], w_x[:, c, 0:DTR], xs[:, c, g * 512:(g + 1) * 512],
                                           start=c == 0, stop=c == CI - 1)
                        mm.then_inc(lo_full, 1)
                        if g == 0:
                            pe.wait_ge(dsum_done, b + 1)
                            for t in range(TB):
                                for c in range(CI):
                                    mm = pe.matmul(pS[:, t * (DS + 2):(t + 1) * (DS + 2)],
                                                   xs[:, c, t * P:(t + 1) * P], w_small[:, c, :],
                                                   start=c == 0, stop=c == CI - 1)
                            mm.then_inc(rank_done, 1)
                    pe.wait_ge(lo_done, b * G + G + 1)
                    pe.wait_ge(small_done, b + 1)
                    for t in range(TB):
                        pe.wait_ge(u_free, b * TB + t + 1)
                        pe.matmul(pS[:, SUMU + t:SUMU + t + 1], dtl[:, t * P:(t + 1) * P], w_dtsum[:, :],
                                  start=True, stop=True)
                        pe.matmul(pU[t % 2][:, :], dtl[:, t * P:(t + 1) * P], w_dt[:, :],
                                  start=True, stop=True).then_inc(u_full, 1)
                        if t < 6:
                            proj(10 + t, pZ, z_full, z_evac, 2 + t)
                pe.wait_ge(decay_done, 1)
                pe.wait_ge(bx_done, 1)
                pe.wait_ge(small_done, B)
                pe.wait_ge(lo_done, B * G + 1)
                for a in range(2):
                    mm = pe.transpose(pL[0:NT, a * P:(a + 1) * P], dec_bx[:, a, :], ident[:, :])
                mm.then_inc(turned, 1)
                pe.wait_ge(s_in, 16)
                pe.wait_ge(turned_out, 1)
                pe.transpose(pL[:, 256:256 + NT], s_blk[:, :], ident[0:NT, 0:NT]).then_inc(s_turned, 1)

            @block.scalar
            def _(act):
                act.sem_inc(xs_evac, 2)
                act.sem_inc(xs_done, 2)
                act.sem_inc(u_free, 2)
                with act.Fori(0, B) as b:
                    def copy_xs(m):
                        act.wait_ge(conv_done, b * CI + m + 1)
                        for g in range(G):
                            act.wait_ge(xs_full, b * 8 + m * G + g + 1)
                            act.activation(xs_pad[m % 2][:, 1 + g * 512:1 + (g + 1) * 512],
                                           pA[g][:, :], ACT.Identity).then_inc(xs_evac, 1)

                    def silu_xs(m):
                        if m == 0:
                            act.wait_ge(lo_full, b * G + 1)
                            act.wait_ge(rank_done, b + 1)
                        act.wait_ge(conv_done, b * CI + 2 + m + 1)
                        act.activation(xs[:, m, :], conv[m % 2][:, :], ACT.Silu).then_inc(xs_done, 1)

                    copy_xs(0)
                    for m in range(1, CI):
                        copy_xs(m)
                        silu_xs(m - 1)
                    silu_xs(CI - 1)
                    act.wait_ge(dsum_done, b + 1)
                    hold(act, T)
                    act.preload_act_table_set("natural_log_exp_and_others")
                    own = Chain(act, act_own, b, TB)
                    for t in range(TB):
                        act.wait_ge(u_full, b * TB + t + 1)
                        act.activation(absu[:, :], pU[t % 2][:, :], ACT.Abs,
                                       accum_out=sum_abs[:, t:t + 1]).then_inc(u_free, 1)
                        act.wait_ge(u_free, b * TB + t + 1 + 2)
                        own.step(act.activation(expu[:, :], absu[:, :], ACT.Exp, scale=-1.0))
                        act.activation(lnu[:, :], expu[:, :], ACT.Ln, bias=1.0,
                                       accum_out=sum_ln[:, t:t + 1]).then_inc(ln_done, 1)
                        act.wait_ge(ln_done, b * TB + t + 1)
                    own.close()
                act.wait_ge(dsum_done, B + 1)
                act.activation(dec_bx[:, 0, :], sum_dt[:, :], ACT.Exp, scale=-1.0 / DI).then_inc(decay_done, 1)

            @block.vector
            def _(dve):
                dve.sem_inc(z_evac, 2)
                dve.sem_inc(conv_done, 2)
                dve.sem_inc(lo_done, 1)
                dve.sem_inc(dsum_done, 1)
                dve.wait_ge(consts, 16 * 9)
                for i in range(2):
                    dve.memset(xs_pad[i][:, 0:1], 0.0).then_inc(prep, 1)
                    dve.memset(xs_pad[i][:, L + 1:L + 2], 0.0).then_inc(prep, 1)
                dve.memset(dtl[DTR:DTR + 1, :], 1.0).then_inc(prep, 1)
                dve.memset(w_small[:, :, DS + 1:DS + 2], 1.0).then_inc(prep, 1)
                dve.tensor_copy(w_small[:, :, 0:DS], w_x[:, :, DTR + DS:DTR + 2 * DS]).then_inc(prep, 1)
                dve.tensor_reduce(w_small[:, :, DS], w_x[:, :, DTR:DTR + DS], AX.X, ALU.add).then_inc(prep, 1)
                dve.tensor_reduce(w_dtsum[:, 0:1], w_dt[:, :], AX.X, ALU.add).then_inc(prep, 1)
                dve.wait_ge(prep, 9)
                with dve.Fori(0, B) as b:
                    own = Chain(dve, dve_own, b, 2 * CI + 1)

                    def copy_z(n):
                        c, g = n // G, n % G
                        dve.wait_ge(z_full, b * 8 + n + 1)
                        hold(dve, T)
                        dve.tensor_copy(zs[:, c, bass.ds(b * L + g * 512, 512)], pZ[n % 2][:, :]).then_inc(z_evac, 1)

                    for m in range(CI):
                        pad, out = xs_pad[m % 2], conv[m % 2]
                        dve.wait_ge(xs_evac, b * 8 + 2 + (m + 1) * G)
                        dve.wait_ge(xs_done, b * CI + m + 1)
                        own.step(dve.tensor_scalar(out[:, :], pad[:, 1:L + 1], w_conv[:, m, 1:2], None, ALU.mult))
                        own.step(dve.scalar_tensor_tensor(out=out[:, :], in0=pad[:, 0:L], scalar=w_conv[:, m, 0:1],
                                                          in1=out[:, :], op0=ALU.mult, op1=ALU.add))
                        dve.scalar_tensor_tensor(out=out[:, :], in0=pad[:, 2:L + 2], scalar=w_conv[:, m, 2:3],
                                                 in1=out[:, :], op0=ALU.mult, op1=ALU.add).then_inc(conv_done, 1)
                    copy_z(0)
                    copy_z(1)
                    for g in range(G):
                        dve.wait_ge(lo_full, b * G + g + 2)
                        dve.tensor_copy(dtl[0:DTR, g * 512:(g + 1) * 512], pL[0:DTR, :]).then_inc(lo_done, 1)
                        if g == 0:
                            dve.wait_ge(rank_done, b + 2)
                            hold(dve, T)
                            dve.tensor_copy(small[:, bass.ds(b * TB, TB), :],
                                            pS[:, 0:SUMU].rearrange("p (t c) -> p t c", t=TB)).then_inc(small_done, 1)
                    for n in range(2, 8):
                        copy_z(n)
                    dve.wait_ge(u_full, b * TB + TB)
                    dve.wait_ge(ln_done, b * TB + TB)
                    own.step(dve.tensor_tensor(sum_ua[:, :], pS[:, SUMU:SUMU + TB], sum_abs[:, :], ALU.add))
                    dve.scalar_tensor_tensor(out=sum_dt[:, bass.ds(b * TB, TB)], in0=sum_ua[:, :], scalar=0.5,
                                             in1=sum_ln[:, :], op0=ALU.mult, op1=ALU.add).then_inc(dsum_done, 1)
                    own.close()
                own = Chain(dve, dve_own, B, 2 * CI + 1)
                dve.wait_ge(small_done, B)
                dve.scalar_tensor_tensor(out=dec_bx[:, 1, :], in0=small[:, :, DS], scalar=1.0 / DI,
                                         in1=small[:, :, DS + 1], op0=ALU.mult, op1=ALU.mult).then_inc(bx_done, 1)
                own.step(dve.tensor_reduce(c_sum[:, :], small[:, :, 0:DS], AX.X, ALU.add))
                own.step(dve.scalar_tensor_tensor(out=cc[:, :, :], in0=c_sum[:, :].unsqueeze(2).broadcast_to([P, NT, DS]),
                                                  scalar=-1.0 / DS, in1=small[:, :, 0:DS],
                                                  op0=ALU.mult, op1=ALU.add))
                own.step(dve.tensor_tensor(csq[:, :, :], cc[:, :, :], cc[:, :, :], ALU.mult))
                own.step(dve.tensor_reduce(c_var[:, :], csq[:, :, :], AX.X, ALU.add))
                dve.wait_ge(turned, 1)
                dve.tensor_copy(dec_bxT[:, :, :], pL[0:NT, 0:2 * P].rearrange("q (a p) -> q a p", a=2)).then_inc(turned_out, 1)
                dve.wait_ge(rows_in, 16)
                dve.tensor_tensor_scan(s_rows[:, :], rows[:, 0, :], rows[:, 1, :], 0.0,
                                       ALU.mult, ALU.add).then_inc(scanned, 1)
                dve.wait_ge(s_turned, 1)
                own.step(dve.tensor_copy(s_tok[:, :], pL[:, 256:256 + NT]))
                own.step(dve.tensor_tensor(y_var[:, :], s_tok[:, :], s_tok[:, :], ALU.mult))
                own.step(dve.tensor_tensor(y_var[:, :], y_var[:, :], c_var[:, :], ALU.mult))
                dve.tensor_scalar(y_var[:, :], y_var[:, :], 1.0 / DS, EPS, ALU.mult, ALU.add).then_inc(y_var_done, 1)
                dve.wait_ge(y_rs_done, 1)
                own.step(dve.tensor_tensor(y_f[:, :], s_tok[:, :], y_rs[:, :], ALU.mult))
                own.step(dve.tensor_tensor(yn[:, :, :], cc[:, :, :],
                                           y_f[:, :].unsqueeze(2).broadcast_to([P, NT, DS]), ALU.mult))

            @block.gpsimd
            def _(pool):
                pool.wait_ge(y_var_done, 1)
                pool.tensor_tensor(y_rs[:, :], y_var[:, :], T["half"][:, 0:NT], ALU.pow).then_inc(y_rs_done, 1)

        mixer_out(nc, T, ctx, sem, x1, ident, zs, zsil, yz, yn, yrep, w_out, ln_g, ln_b,
                  res, stats, mv, x_var, x_rs)


def mixer_out(nc, T, ctx, sem, x1, ident, zs, zsil, yz, yn, yrep, w_out, ln_g, ln_b, res, stats, mv, x_var, x_rs):
    yrep_done = sem("yrep_done")
    y_turned = sem("y_turned")
    y_scaled = sem("y_scaled")
    z_silu = sem("z_silu")
    yz_done = sem("yz_done")
    o_full = sem("o_full")
    o_evac = sem("o_evac")
    x_var_done = sem("x_var_done")
    x_rs_done = sem("x_rs_done")
    x1_done = sem("x1_done")
    x1_stored = sem("x1_stored")
    own_sem = sem("own2")
    with ExitStack() as pctx, nc.Block() as block:
        pY = [pctx.enter_context(nc.psum_tensor(f"mx_pY{i}", [P, 512], F32)) for i in range(2)]
        pO = [pctx.enter_context(nc.psum_tensor(f"mx_pO{i}", [P, 512], F32)) for i in range(2)]

        @block.tensor
        def _(pe):
            pe.sem_inc(o_full, 1)
            with pe.Fori(0, B) as b:
                pe.wait_ge(yrep_done, b + 1)
                for t in range(TB):
                    mm = pe.transpose(pY[t // 4][:, (t % 4) * P:(t % 4 + 1) * P],
                                      yrep[:, t, :, :].rearrange("p a s -> p (a s)"), ident[:, :])
                    if t % 4 == 3:
                        mm.then_inc(y_turned, 1)
                for t in range(TB):
                    if t % 4 == 0:
                        pe.wait_ge(yz_done, b * G + t // 4 + 2)
                    pe.wait_ge(o_evac, b * TB + t + 1)
                    for c in range(CI):
                        mm = pe.matmul(pO[t % 2][:, 0:D], yz[:, c, t * P:(t + 1) * P], w_out[:, c, :],
                                       start=c == 0, stop=c == CI - 1)
                    mm.then_inc(o_full, 1)

        @block.scalar
        def _(act):
            act.sem_inc(y_scaled, 1)
            with act.Fori(0, B) as b:
                for c in range(CI):
                    act.wait_ge(yz_done, b * G + 1)
                    hold(act, T)
                    act.activation(zsil[:, c, :], zs[:, c, bass.ds(b * L, L)], ACT.Silu).then_inc(z_silu, 1)
                for g in range(G):
                    act.wait_ge(y_turned, b * G + g + 1)
                    act.wait_ge(o_full, b * TB + 1)
                    for c in range(CI):
                        act.activation(yz[:, c, g * 512:(g + 1) * 512], pY[g][:, :], ACT.Identity,
                                       scale=ln_g[:, c:c + 1], bias=ln_b[:, c:c + 1]).then_inc(y_scaled, 1)

        @block.vector
        def _(dve):
            dve.sem_inc(o_evac, 2)
            dve.sem_inc(yz_done, 1)
            with dve.Fori(0, B) as b:
                own = Chain(dve, own_sem, b, TB + TB)
                dve.wait_ge(y_scaled, b * G * CI + 1)
                hold(dve, T)
                dve.tensor_copy(yrep[:, :, :, :],
                                yn[:, bass.ds(b * TB, TB), :].unsqueeze(2).broadcast_to([P, TB, 8, DS])).then_inc(yrep_done, 1)
                for g in range(G):
                    dve.wait_ge(z_silu, b * CI + CI)
                    dve.wait_ge(y_scaled, b * G * CI + (g + 1) * CI + 1)
                    dve.tensor_tensor(yz[:, :, g * 512:(g + 1) * 512], yz[:, :, g * 512:(g + 1) * 512],
                                      zsil[:, :, g * 512:(g + 1) * 512], ALU.mult).then_inc(yz_done, 1)
                for t in range(TB):
                    dve.wait_ge(o_full, b * TB + t + 2)
                    dve.tensor_tensor(res[:, t, :], pO[t % 2][:, 0:D],
                                      x1[:, bass.ds(b * TB + t, 1), :].rearrange("p a d -> p (a d)"),
                                      ALU.add).then_inc(o_evac, 1)
                    dve.wait_ge(o_evac, b * TB + 2 + t + 1)
                    own.mark(dve.bn_stats(stats[:, t, :], res[:, t, :]))
                own.settle()
                hold(dve, T)
                for t in range(TB):
                    own.mark(dve.bn_aggr(mv[:, t, :], stats[:, t, :]))
                own.settle()
                dve.tensor_scalar(x_var[:, :], mv[:, :, 1], EPS, None, ALU.add).then_inc(x_var_done, 1)
                dve.wait_ge(x_rs_done, b + 1)
                for t in range(TB):
                    ins = dve.tensor_scalar(x1[:, bass.ds(b * TB + t, 1), :].rearrange("p a d -> p (a d)"),
                                            res[:, t, :], mv[:, t, 0:1], x_rs[:, t:t + 1],
                                            ALU.subtract, ALU.mult)
                    ins.then_inc(x1_done, 1)
                dve.wait_ge(x1_done, b * TB + TB)
                own.close()

        @block.gpsimd
        def _(pool):
            with pool.Fori(0, B) as b:
                pool.wait_ge(x_var_done, b + 1)
                pool.tensor_tensor(x_rs[:, :], x_var[:, :], T["half"][:, 0:TB], ALU.pow).then_inc(x_rs_done, 1)

        @block.sync
        def _(sp):
            with sp.Fori(0, B) as b:
                sp.wait_ge(x1_done, b * TB + TB)
                sp.dma_start(T["x1_d"].rearrange("(t p) d -> p t d", p=P)[:, bass.ds(b * TB, TB), :],
                             x1[:, bass.ds(b * TB, TB), :]).then_inc(x1_stored, 16)
            sp.wait_ge(x1_stored, 16 * B)


E_ = 16
IN0 = 128
MID_ID = N // 2


def steps(eng, n, depth, unroll, body):
    first = -(-depth // unroll)
    loops = n // unroll - first
    for s in range(first * unroll):
        body(s, s // unroll, s % unroll, lambda k: 0 <= s - k < n)
    with eng.Fori(first, first + loops) as h:
        for q in range(unroll):
            body(h * unroll + q, h, q, lambda k: True)
    for s in range((first + loops) * unroll, n + depth):
        body(s, s // unroll, s % unroll, lambda k: 0 <= s - k < n)


class Sems:

    def __init__(self, nc, ctx, prefix):
        self.make = lambda name: ctx.enter_context(nc.semaphore(prefix + name))
        self.made = {}

    def __call__(self, name):
        if name not in self.made:
            self.made[name] = self.make(name)
        return self.made[name]


def experts0(nc, T, routed, n, pre):
    with ExitStack() as ctx:
        S = Sems(nc, ctx, pre)
        sb = lambda name, shape, dt=F32: ctx.enter_context(nc.sbuf_tensor(pre + name, shape, dt))
        xT = [sb(f"xT{i}", [P, KD, P]) for i in range(2)]
        sg = [sb(f"sg{i}", [P, IN0]) for i in range(2)]
        hh = [sb(f"hh{i}", [P, IN0]) for i in range(2)]
        hT = [sb(f"hT{i}", [P, P]) for i in range(2)]
        xg = [sb(f"xg{i}", [P, D]) for i in range(4)]
        if routed:
            ix = [sb(f"ix{i}", [P, 1], I32) for i in range(4)]
            yo = [sb(f"yo{i}", [P, D]) for i in range(2)]
        x1, ident = T["x1"], T["ident"]
        w13, w2, w_in, w_n = (T[k + ("0" if routed else "s")] for k in ("w13", "w2", "w_in", "w_n"))
        xT_full, xT_done = S("xT_full"), S("xT_done")
        h_full, sg_done, hh_done = S("h_full"), S("sg_done"), S("hh_done")
        ht_full, ht_done = S("ht_full"), S("ht_done")
        y_full, y_done = S("y_full"), S("y_done")
        x_in = [S(f"x_in{i}") for i in range(4)]
        y_stored = [S(f"y_stored{i}") for i in range(2)]
        ix_done = S("ix_done")

        with ExitStack() as pctx, nc.Block() as block:
            pX, pH, pHT, pY = ([pctx.enter_context(nc.psum_tensor(f"{pre}{nm}{i}", [P, 512], F32))
                                for i in range(2)] for nm in ("pX", "pH", "pHT", "pY"))

            @block.gpsimd
            def _(pool):
                def body(s, h, q, on):
                    pool.wait_ge(xT_full, s + 1)
                    hold(pool, T)
                    if not routed:
                        pool.tensor_copy(xg[q][:, :],
                                         x1[:, bass.ds(s, 1), :].rearrange("p a d -> p (a d)")).then_inc(x_in[q], 16)
                        return
                    pool.tensor_copy(ix[q][:, :], T["slot_tok"][:, bass.ds(s, 1)]).then_inc(ix_done, 1)
                    pool.wait_ge(ix_done, s + 1)
                    hold(pool, T)
                    pool.indirect_dma_start(xg[q][:, :], None, T["x1_d"],
                                            bass.IndirectOffsetOnAxis(ap=ix[q][:, 0:1], axis=0)).then_inc(x_in[q], 16)
                steps(pool, n, 0, 4, body)

            if routed:
                @block.sync
                def _(sp):
                    def body(s, h, q, on):
                        sp.wait_ge(y_done, s + 3)
                        sp.dma_start(T["y_d"][bass.ds(s * P, P), :], yo[q % 2][:, :]).then_inc(y_stored[q % 2], 16)
                    steps(sp, n, 0, 4, body)
                    for i in range(2):
                        sp.wait_ge(y_stored[i], 16 * (n // 2 + 1))

            @block.tensor
            def _(pe):
                pe.sem_inc(xT_full, 4)
                pe.sem_inc(h_full, 2)
                pe.sem_inc(ht_full, 2)
                pe.sem_inc(y_full, 2)
                pe.wait_ge(w_in, w_n)
                def body(s, h, q, on):
                    if on(0):
                        t = s
                        pe.wait_ge(x_in[q], (h + 1) * 16)
                        pe.wait_ge(xT_done, t + 1)
                        for k in range(KD):
                            mm = pe.transpose(pX[q % 2][:, k * P:(k + 1) * P], xg[q][:, k * P:(k + 1) * P],
                                              ident[:, :])
                        mm.then_inc(xT_full, 1)
                    if on(1):
                        t, r = s - 1, (q - 1) % 2
                        if routed:
                            e = pe.value_load(T["tile_exp"][0:1, bass.ds(t, 1)], min_val=0, max_val=E_ - 1)
                        pe.wait_ge(xT_done, t + 3)
                        pe.wait_ge(hh_done, t + 1)
                        for k in range(KD):
                            w = w13[:, bass.ds(e, 1), k, :].rearrange("p a n -> p (a n)") if routed else w13[:, k, :]
                            mm = pe.matmul(pH[r][:, 0:D], xT[r][:, k, :], w, start=k == 0, stop=k == KD - 1)
                        if not routed:
                            for k in range(KD):
                                mm = pe.matmul(pH[r][:, D:D + E_], xT[r][:, k, :], T["w_gate"][:, k, :],
                                               start=k == 0, stop=k == KD - 1)
                        mm.then_inc(h_full, 1)
                    if on(2):
                        t, r = s - 2, q % 2
                        pe.wait_ge(hh_done, t + 3)
                        pe.wait_ge(ht_done, t + 1)
                        pe.transpose(pHT[r][:, 0:P], hh[r][:, :], ident[:, :]).then_inc(ht_full, 1)
                    if on(3):
                        t, r = s - 3, (q - 3) % 2
                        if routed:
                            e = pe.value_load(T["tile_exp"][0:1, bass.ds(t, 1)], min_val=0, max_val=E_ - 1)
                        pe.wait_ge(ht_done, t + 3)
                        pe.wait_ge(y_done, t + 1)
                        w = w2[:, bass.ds(e, 1), :].rearrange("p a n -> p (a n)") if routed else w2[:, :]
                        pe.matmul(pY[r][:, 0:D], hT[r][:, :], w, start=True, stop=True).then_inc(y_full, 1)
                steps(pe, n, 3, 4, body)

            @block.scalar
            def _(act):
                act.sem_inc(sg_done, 2)
                act.sem_inc(ht_done, 2)
                if routed:
                    act.sem_inc(y_done, 2)
                    for i in range(2):
                        act.sem_inc(y_stored[i], 16)

                def body(s, h, q, on):
                    if on(1):
                        t, r = s - 1, (q - 1) % 2
                        act.wait_ge(h_full, t + 3)
                        act.wait_ge(hh_done, t + 1)
                        act.activation(sg[r][:, :], pH[r][:, 0:IN0], ACT.Silu).then_inc(sg_done, 1)
                    if on(2):
                        t, r = s - 2, q % 2
                        act.wait_ge(ht_full, t + 3)
                        act.wait_ge(y_full, t + 1)
                        act.activation(hT[r][:, :], pHT[r][:, 0:P], ACT.Identity).then_inc(ht_done, 1)
                    if on(3) and routed:
                        t, r = s - 3, (q - 3) % 2
                        act.wait_ge(y_full, t + 3)
                        act.wait_ge(y_stored[r], (h * 2 + (q - 3) // 2 + 1) * 16)
                        act.activation(yo[r][:, :], pY[r][:, 0:D], ACT.Identity).then_inc(y_done, 1)
                steps(act, n, 3, 4, body)

            @block.vector
            def _(dve):
                dve.sem_inc(xT_done, 2)
                dve.sem_inc(hh_done, 2)
                if not routed:
                    dve.sem_inc(y_done, 2)

                def body(s, h, q, on):
                    if on(0):
                        t, r = s, q % 2
                        dve.wait_ge(xT_full, t + 5)
                        dve.wait_ge(h_full, t + 1)
                        dve.tensor_copy(xT[r][:, :, :].rearrange("p k n -> p (k n)"),
                                        pX[r][:, 0:D]).then_inc(xT_done, 1)
                    if on(1):
                        t, r = s - 1, (q - 1) % 2
                        if not routed:
                            dve.wait_ge(h_full, t + 3)
                            dve.wait_ge(sg_done, t + 3)
                            hold(dve, T)
                            dve.tensor_copy(T["logits"][:, bass.ds(t, 1), :].rearrange("p a e -> p (a e)"),
                                            pH[r][:, D:D + E_]).then_inc(S("lg_done"), 1)
                        dve.wait_ge(sg_done, t + 3)
                        dve.wait_ge(ht_full, t + 1)
                        dve.tensor_tensor(hh[r][:, :], sg[r][:, :], pH[r][:, IN0:2 * IN0], ALU.mult).then_inc(hh_done, 1)
                    if on(3) and not routed:
                        t, r = s - 3, (q - 3) % 2
                        dve.wait_ge(y_full, t + 3)
                        xt = x1[:, bass.ds(t, 1), :].rearrange("p a d -> p (a d)")
                        dve.tensor_tensor(xt, pY[r][:, 0:D], xt, ALU.add).then_inc(y_done, 1)
                steps(dve, n, 3, 4, body)
                if not routed:
                    dve.wait_ge(S("lg_done"), n)
                    dve.wait_ge(y_done, n + 2)


def dispatch(nc, T, K, n_tiles, sigmoid, tok_id, pre):
    with ExitStack() as ctx:
        sb = lambda name, shape, dt=F32: ctx.enter_context(nc.sbuf_tensor(pre + name, shape, dt))
        sem = lambda name: ctx.enter_context(nc.semaphore(pre + name))
        TE = [P, NT, E_]
        score = sb("score", TE)
        work = sb("work", TE)
        cand = sb("cand", TE)
        oh = [sb(f"oh{k}", TE) for k in range(K)]
        top = sb("top", [P, NT])
        wsum = sb("wsum", [P, NT])
        mask = sb("mask", TE, F16)
        tot = sb("tot", [P, E_, NT])
        incl = sb("incl", [P, E_, NT])
        excl = sb("excl", [P, E_, NT])
        ones = sb("ones", [P, E_ * NT])
        cnt = sb("cnt", [P, E_])
        full = sb("full", [P, E_, NT])
        ntile = sb("ntile", [P, E_])
        tile_end = sb("tile_end", [P, E_])
        base = sb("base", [P, E_])
        place = sb("place", TE)
        pos = sb("pos", [P, NT, K])
        pos_lo = sb("pos_lo", [P, NT, K], I32)
        pos_hi = sb("pos_hi", [P, NT, K], I32)
        lo = sb("lo", [P, NT, K])
        hi = sb("hi", [P, NT, K])
        before = sb("before", [P, n_tiles, E_])
        texp = sb("texp", [P, n_tiles])
        oh_lo = [sb(f"oh_lo{k}", [P, P], F16) for k in range(K)]
        oh_hi = [sb(f"oh_hi{k}", [P, n_tiles], F16) for k in range(K)]
        c32, c16 = T["c32"], T["c16"]
        rev, thr, iota = c32["rev"], c32["thr"], c32["iota"]
        io_lo, io_hi, tri, one16 = c16["iota"], c16["iota"], c16["tri"], c16["ones"]
        slot_w = T["slot_w"]

        dve_own, sig, mask_done, counted = sem("dve_own"), sem("sig"), sem("mask_done"), sem("counted")
        cent_done, exp_done = sem("cent_done"), sem("exp_done")
        oh_done, oh_used, inv_done = sem("oh_done"), sem("oh_used"), sem("inv_done")

        bcE = lambda ap: ap.unsqueeze(2).broadcast_to(TE)
        bcT = lambda ap: ap.unsqueeze(1).broadcast_to(TE)

        with ExitStack() as pctx, nc.Block() as block:
            pW, pN, pI = (pctx.enter_context(nc.psum_tensor(pre + nm, [P, 512], F32)) for nm in ("pW", "pN", "pI"))

            @block.scalar
            def _(act):
                if sigmoid:
                    act.activation(score[:, :, :], T["logits"][:, :, :], ACT.Sigmoid).then_inc(exp_done, 1)
                else:
                    act.wait_ge(cent_done, 1)
                    act.activation(work[:, :, :], cand[:, :, :], ACT.Exp).then_inc(exp_done, 1)

            @block.vector
            def _(dve):
                own = Chain(dve, dve_own)
                tt = lambda out, a, b, op: own.step(dve.tensor_tensor(out, a, b, op))
                if sigmoid:
                    dve.wait_ge(exp_done, 1)
                    tt(work[:, :, :], score[:, :, :], bcT(T["route_b"][:, :]), ALU.add)
                else:
                    lg = T["logits"]
                    tt(lg[:, :, :], lg[:, :, :], bcT(T["route_b"][:, :]), ALU.add)
                    own.step(dve.tensor_reduce(top[:, :], lg[:, :, :], AX.X, ALU.max))
                    dve.tensor_tensor(cand[:, :, :], lg[:, :, :], bcE(top[:, :]), ALU.subtract).then_inc(cent_done, 1)
                    dve.wait_ge(exp_done, 1)
                    own.step(dve.tensor_reduce(wsum[:, :], work[:, :, :], AX.X, ALU.add))
                    own.step(dve.reciprocal(wsum[:, :], wsum[:, :]))
                    tt(score[:, :, :], work[:, :, :], bcE(wsum[:, :]), ALU.mult)
                    own.step(dve.tensor_copy(work[:, :, :], score[:, :, :]))
                for k in range(K):
                    own.step(dve.tensor_reduce(top[:, :], work[:, :, :], AX.X, ALU.max))
                    tt(cand[:, :, :], work[:, :, :], bcE(top[:, :]), ALU.is_equal)
                    tt(cand[:, :, :], cand[:, :, :], bcT(rev), ALU.mult)
                    own.step(dve.tensor_reduce(top[:, :], cand[:, :, :], AX.X, ALU.max))
                    tt(oh[k][:, :, :], bcT(rev), bcE(top[:, :]), ALU.is_equal)
                    if k < K - 1:
                        own.step(dve.scalar_tensor_tensor(out=work[:, :, :], in0=oh[k][:, :, :], scalar=-1e30,
                                                          in1=work[:, :, :], op0=ALU.mult, op1=ALU.add))
                for k in range(1, K):
                    src = oh[0] if k <= 1 else cand
                    if k == K - 1:
                        dve.tensor_tensor(mask[:, :, :], src[:, :, :], oh[k][:, :, :], ALU.add).then_inc(mask_done, 1)
                    else:
                        tt(cand[:, :, :], src[:, :, :], oh[k][:, :, :], ALU.add)
                dve.wait_ge(mask_done, 1)
                for k in range(K):
                    tt(cand[:, :, :], oh[k][:, :, :], score[:, :, :], ALU.mult)
                    own.step(dve.tensor_reduce(slot_w[:, :, k], cand[:, :, :], AX.X, ALU.add))
                own.step(dve.tensor_reduce(wsum[:, :], slot_w[:, :, 0:K], AX.X, ALU.add))
                if not sigmoid:
                    own.step(dve.tensor_scalar(wsum[:, :], wsum[:, :], 1e-9, None, ALU.max))
                own.step(dve.reciprocal(wsum[:, :], wsum[:, :]))
                if sigmoid:
                    own.step(dve.tensor_scalar(wsum[:, :], wsum[:, :], 2.5, None, ALU.mult))
                tt(slot_w[:, :, 0:K], slot_w[:, :, 0:K], wsum[:, :].unsqueeze(2).broadcast_to([P, NT, K]), ALU.mult)
                own.step(dve.memset(ones[:, :], 1.0))
                dve.wait_ge(counted, 1)
                own.step(dve.tensor_copy(tot[:, :, :], pN[:, :].rearrange("p (t e) -> p e t", e=E_)))
                own.step(dve.tensor_tensor_scan(incl[:, :, :].rearrange("p e t -> p (e t)"), ones[:, :],
                                                tot[:, :, :].rearrange("p e t -> p (e t)"), 0.0, ALU.mult, ALU.add))
                tt(excl[:, :, :], incl[:, :, :], tot[:, :, :], ALU.subtract)
                tt(cnt[:, :], incl[:, :, NT - 1], excl[:, :, 0], ALU.subtract)
                tt(full[:, :, :], cnt[:, :].unsqueeze(2).broadcast_to([P, E_, NT]),
                   thr.unsqueeze(1).broadcast_to([P, E_, NT]), ALU.is_gt)
                own.step(dve.tensor_reduce(ntile[:, :], full[:, :, :], AX.X, ALU.add))
                own.step(dve.tensor_tensor_scan(tile_end[:, :], ones[:, 0:E_], ntile[:, :], 0.0, ALU.mult, ALU.add))
                tt(before[:, :, :], iota[:, 0:n_tiles].unsqueeze(2).broadcast_to([P, n_tiles, E_]),
                   tile_end[:, :].unsqueeze(1).broadcast_to([P, n_tiles, E_]), ALU.is_ge)
                own.step(dve.tensor_reduce(texp[:, :], before[:, :, :], AX.X, ALU.add))
                own.step(dve.tensor_scalar(T["tile_exp"][:, 0:n_tiles], texp[0:1, :], float(E_ - 1), None, ALU.min))
                tt(base[:, :], tile_end[:, :], ntile[:, :], ALU.subtract)
                own.step(dve.scalar_tensor_tensor(out=base[:, :], in0=base[:, :], scalar=float(P),
                                                  in1=excl[:, :, 0], op0=ALU.mult, op1=ALU.subtract))
                tt(place[:, :, :], excl[:, :, :].rearrange("p e t -> p t e"), bcT(base[:, :]), ALU.add)
                tt(place[:, :, :], place[:, :, :], pW[:, :].rearrange("p (t e) -> p t e", e=E_), ALU.add)
                for k in range(K):
                    tt(cand[:, :, :], oh[k][:, :, :], place[:, :, :], ALU.mult)
                    own.step(dve.tensor_reduce(pos[:, :, k], cand[:, :, :], AX.X, ALU.add))
                pi = T["slot_of"][:, :, 0:K]
                own.step(dve.tensor_copy(pi, pos[:, :, :]))
                own.step(dve.tensor_scalar(pos_lo[:, :, :], pi, P - 1, None, ALU.bitwise_and))
                own.step(dve.tensor_scalar(pos_hi[:, :, :], pi, 7, None, ALU.logical_shift_right))
                own.step(dve.tensor_copy(lo[:, :, :], pos_lo[:, :, :]))
                own.step(dve.tensor_copy(hi[:, :, :], pos_hi[:, :, :]))
                with dve.Fori(0, NT) as t:
                    for k in range(K):
                        dve.wait_ge(oh_used, t * K + k + 1)
                        dve.tensor_scalar(oh_lo[k][:, :], io_lo[:, 0:P],
                                          lo[:, bass.ds(t, 1), k:k + 1].rearrange("p a k -> p (a k)"), None,
                                          ALU.is_equal).then_inc(oh_done, 1)
                        dve.tensor_scalar(oh_hi[k][:, :], io_hi[:, 0:n_tiles],
                                          hi[:, bass.ds(t, 1), k:k + 1].rearrange("p a k -> p (a k)"),
                                          tok_id[:, bass.ds(t, 1)], ALU.is_equal, ALU.mult).then_inc(oh_done, 1)
                dve.wait_ge(inv_done, 1)
                own.step(dve.tensor_scalar(T["slot_tok"][:, 0:n_tiles], pI[:, 0:n_tiles], float(MID_ID), None, ALU.add))

            @block.tensor
            def _(pe):
                pe.sem_inc(oh_used, K)
                pe.wait_ge(mask_done, 1)
                m = mask[:, :, :].rearrange("p t e -> p (t e)")
                pe.matmul(pW[:, :], tri, m, start=True, stop=True)
                pe.matmul(pN[:, :], one16, m, start=True, stop=True).then_inc(counted, 1)

                def add(t, first, last):
                    for k in range(K):
                        pe.wait_ge(oh_done, (t * K + k + 1) * 2)
                        mm = pe.matmul(pI[:, 0:n_tiles], oh_lo[k][:, :], oh_hi[k][:, :],
                                       start=first and k == 0, stop=last and k == K - 1)
                        mm.then_inc(inv_done if last and k == K - 1 else oh_used, 1)
                add(0, True, False)
                with pe.Fori(1, NT - 1) as t:
                    add(t, False, False)
                add(NT - 1, False, True)


def combine(nc, T, K, acc, out_rows, transposed, pre):
    with ExitStack() as ctx:
        sb = lambda name, shape, dt=F32: ctx.enter_context(nc.sbuf_tensor(pre + name, shape, dt))
        S = Sems(nc, ctx, pre)
        ix = [[sb(f"ix{i}_{k}", [P, 1], I32) for k in range(K)] for i in range(2)]
        yg = [sb(f"yg{i}", [P, K, D]) for i in range(2)]
        sm = [sb(f"sm{i}", [P, D]) for i in range(2)]
        st = [sb(f"st{i}", [P, 6]) for i in range(2)]
        mv = [sb(f"mv{i}", [P, 2]) for i in range(2)]
        var = [sb(f"var{i}", [P, 1]) for i in range(2)]
        rs = [sb(f"rs{i}", [P, 1]) for i in range(2)]
        xo = [sb(f"xo{i}", [P, D]) for i in range(2)]
        ident = T["ident"]
        own_sem, ix_done, summed = S("own"), S("ix_done"), S("summed")
        y_in = [S(f"y_in{i}") for i in range(2)]
        var_done, rs_done, xo_done, xo_turned, xT_done = S("var"), S("rs"), S("xo"), S("turned"), S("xT")
        stored = [S(f"stored{i}") for i in range(2)]

        with ExitStack() as pctx, nc.Block() as block:
            pX = [pctx.enter_context(nc.psum_tensor(f"{pre}pX{i}", [P, 512], F32)) for i in range(2)]

            @block.gpsimd
            def _(pool):
                def body(s, h, q, on):
                    if on(0):
                        pool.wait_ge(summed, s + 1)
                        hold(pool, T)
                        for k in range(K):
                            pool.tensor_copy(ix[q][k][:, :], T["slot_of"][:, bass.ds(s, 1), k:k + 1]
                                             .rearrange("p a k -> p (a k)")).then_inc(ix_done, 1)
                        pool.wait_ge(ix_done, (s + 1) * K)
                        hold(pool, T)
                        for k in range(K):
                            pool.indirect_dma_start(yg[q][:, k, :], None, T["y_d"],
                                                    bass.IndirectOffsetOnAxis(ap=ix[q][k][:, 0:1], axis=0)).then_inc(y_in[q], 16)
                    if on(1):
                        t, r = s - 1, (q - 1) % 2
                        pool.wait_ge(var_done, t + 1)
                        pool.tensor_tensor(rs[r][:, :], var[r][:, :], T["half"][:, 0:1], ALU.pow).then_inc(rs_done, 1)
                steps(pool, NT, 1, 2, body)

            @block.vector
            def _(dve):
                dve.sem_inc(summed, 2)
                dve.sem_inc(xo_done, 2)

                def body(s, h, q, on):
                    own = Chain(dve, own_sem, s, K + 1)
                    if on(0):
                        dve.wait_ge(y_in[q], (h + 1) * 16 * K)
                        dve.wait_ge(xo_done, s + 1)
                        src = acc[:, bass.ds(s, 1), :].rearrange("p a d -> p (a d)")
                        for k in range(K):
                            ins = dve.scalar_tensor_tensor(
                                out=sm[q][:, :], in0=yg[q][:, k, :],
                                scalar=T["slot_w"][:, bass.ds(s, 1), k:k + 1].rearrange("p a k -> p (a k)"),
                                in1=src, op0=ALU.mult, op1=ALU.add)
                            src = sm[q][:, :]
                            if k < K - 1:
                                own.step(ins)
                            else:
                                ins.then_inc(summed, 1)
                        dve.wait_ge(summed, s + 3)
                        own.step(dve.bn_stats(st[q][:, :], sm[q][:, :]))
                        hold(dve, T)
                        own.step(dve.bn_aggr(mv[q][:, :], st[q][:, :]))
                        dve.tensor_scalar(var[q][:, :], mv[q][:, 1:2], EPS, None, ALU.add).then_inc(var_done, 1)
                    if on(1):
                        t, r = s - 1, (q - 1) % 2
                        dve.wait_ge(rs_done, t + 1)
                        dve.wait_ge(stored[r], (h + (q - 1) // 2 + 1) * 16)
                        if transposed:
                            dve.wait_ge(xo_turned, t + 1)
                        dve.tensor_scalar(xo[r][:, :], sm[r][:, :], mv[r][:, 0:1], rs[r][:, 0:1],
                                          ALU.subtract, ALU.mult).then_inc(xo_done, 1)
                steps(dve, NT, 1, 2, body)

            @block.sync
            def _(sp):
                for i in range(2):
                    sp.sem_inc(stored[i], 16)

                def body(s, h, q, on):
                    sp.wait_ge(xo_done, s + 3)
                    sp.dma_start(out_rows(s), xo[q][:, :]).then_inc(stored[q], 16)
                steps(sp, NT, 0, 2, body)
                for i in range(2):
                    sp.wait_ge(stored[i], 16 * (NT // 2 + 1))

            if transposed:
                @block.tensor
                def _(pe):
                    pe.sem_inc(xo_turned, 2)

                    def body(s, h, q, on):
                        pe.wait_ge(xo_done, s + 3)
                        pe.wait_ge(xT_done, s + 1)
                        for k in range(KD):
                            mm = pe.transpose(pX[q][:, k * P:(k + 1) * P], xo[q][:, k * P:(k + 1) * P], ident[:, :])
                        mm.then_inc(xo_turned, 1)
                    steps(pe, NT, 0, 2, body)

                @block.scalar
                def _(act):
                    act.sem_inc(xT_done, 2)

                    def body(s, h, q, on):
                        act.wait_ge(xo_turned, s + 3)
                        hold(act, T)
                        act.activation(T["x2T"][:, :, bass.ds(s * P, P)],
                                       pX[q][:, 0:D].rearrange("p (k n) -> p k n", k=KD), ACT.Identity).then_inc(xT_done, 1)
                    steps(act, NT, 0, 2, body)
                    act.wait_ge(xT_done, NT + 2)


H, DH = 16, 16
BL = 32
SEG = 4
LOCAL = (1, 2, 3)
FAR = tuple(range(5))
N0 = 10
PAIRS0 = [(a, b) for a in range(SEG) for b in range(a + 1)]


def far_count(t, s, h):
    return sum(1 for x in range(L.bit_length() - 1)
               if t // 2 ** (x + 2) == s // 2 ** (x + 2) and t % 2 ** x == h % 2 ** x == s % 2 ** x)


def local_groups():
    out, first = [], 0
    for lv in LOCAL:
        r = 2 ** lv
        for rho in range(r):
            nh, ns = H // r, BL // (SEG * r)
            out.append((r, rho, nh, ns, first))
            first += ns * 4 * nh
    return out, first


GROUPS, NC = local_groups()


def far_groups():
    out, first = [], 0
    for lv in FAR:
        r = 2 ** lv
        ns = (L // H) // (SEG * r)
        out.append((r, ns, first))
        first += ns * 4
    return out, first


FGROUPS, NF = far_groups()
NJ = L // H


def count_tables():
    c0 = np.zeros((P, BL // SEG, N0, H), np.float32)
    cc = np.zeros((P, NC), np.float32)
    for p in range(L // BL):
        for s in range(BL // SEG):
            for n, (a, b) in enumerate(PAIRS0):
                for h in range(H):
                    t = BL * p + SEG * s
                    c0[p, s, n, h] = far_count(t + a, t + b, h)
        for r, rho, nh, ns, first in GROUPS:
            v = cc[p, first:first + ns * 4 * nh].reshape(ns, 2, 2, nh)
            for s in range(ns):
                for a in range(2):
                    for b in range(2):
                        for k in range(nh):
                            t = BL * p + s * SEG * r + rho
                            v[s, a, b, k] = far_count(t + (2 + a) * r, t + b * r, rho + r * k)
    for q in range(1, B):
        n = L // BL
        c0[q * n:(q + 1) * n], cc[q * n:(q + 1) * n] = c0[:n], cc[:n]
    cf = np.zeros((B * H, NF), np.float32)
    for h in range(H):
        for r, ns, first in FGROUPS:
            v = cf[h, first:first + ns * 4].reshape(ns, 2, 2)
            for s in range(ns):
                for a in range(2):
                    for b in range(2):
                        j = s * SEG * r
                        v[s, a, b] = far_count(H * (j + (2 + a) * r) + h, H * (j + b * r) + h, h)
    for q in range(1, B):
        cf[q * H:(q + 1) * H] = cf[:H]
    return c0.reshape(P, -1), cc, cf


def rope_tables():
    freq = (1.0 / np.float32(15000.0) ** (np.arange(0, D, 2, dtype=np.float32) / np.float32(D))).astype(np.float32)
    ang = np.arange(L, dtype=np.float32)[:, None] * freq[None, :]
    both = np.stack([np.cos(ang), np.sin(ang)], 1).astype(np.float32)
    return np.tile(both.reshape(L // BL, BL, 2, D // 2), (B, 1, 1, 1)).copy()


def project_qkv(nc, T, W):
    with ExitStack() as ctx:
        S = Sems(nc, ctx, "qkv_")
        sb = lambda name, shape, dt=F32: ctx.enter_context(nc.sbuf_tensor("qkv_" + name, shape, dt))
        w = sb("w", [P, KD, 3 * D])
        brow = sb("brow", [1, 3 * D])
        one = sb("one", [1, P])
        lhs = [sb(f"lhs{i}", [P, KD, P]) for i in range(2)]
        raw = [sb(f"raw{i}", [P, 2 * D]) for i in range(2)]
        tc_ = [sb(f"tc{i}", [P, 2 * D]) for i in range(2)]
        ts_ = [sb(f"ts{i}", [P, 2 * D]) for i in range(2)]
        x2T, qk, v, cs = T["x2T"], T["qk"], T["v"], T["rope"]
        w_in, prep, lhs_done, qk_full, v_full = S("w_in"), S("prep"), S("lhs_done"), S("qk_full"), S("v_full")
        raw_done, v_done, tc_done, ts_done, rot0, rot_done = (S("raw_done"), S("v_done"), S("tc_done"),
                                                              S("ts_done"), S("rot0"), S("rot_done"))
        xv = x2T.rearrange("p k (b i) -> p k b i", i=BL)
        halves = lambda ap: ap.rearrange("p (a h n) -> p a h n", a=2, h=2)

        with ExitStack() as pctx, nc.Block() as block:
            pQ, pV = ([pctx.enter_context(nc.psum_tensor(f"qkv_{nm}{i}", [P, 512], F32)) for i in range(2)]
                      for nm in ("pQ", "pV"))

            @block.sync
            def _(sp):
                sp.dma_start(w[:, :, :], W["wqkvT"].rearrange("(k p) n -> p k n", p=P)).then_inc(w_in, 16)
                sp.dma_start(brow[:, :], W["bqkv"].rearrange("(a n) -> a n", a=1)).then_inc(w_in, 16)
                sp.wait_ge(w_in, 32)

            @block.scalar
            def _(act):
                act.sem_inc(raw_done, 2)
                act.sem_inc(v_done, 2)

                def body(s, h, q, on):
                    if on(0):
                        act.wait_ge(v_full, s + 1)
                        hold(act, T)
                        act.activation(lhs[q][:, :, :], xv[:, :, :, bass.ds(s, 1)].rearrange("p k b i -> p k (b i)"),
                                       ACT.Identity).then_inc(lhs_done, 1)
                    if on(2):
                        t = s - 2
                        act.wait_ge(qk_full, t + 3)
                        act.wait_ge(rot0, t + 1)
                        act.wait_ge(ts_done, t + 1)
                        act.activation(raw[q][:, :], pQ[q][:, :], ACT.Identity).then_inc(raw_done, 1)
                        act.wait_ge(v_full, t + 3)
                        hold(act, T)
                        act.activation(v[:, bass.ds(t, 1), :].rearrange("p a d -> p (a d)"), pV[q][:, 0:D],
                                       ACT.Identity).then_inc(v_done, 1)
                steps(act, BL, 2, 2, body)

            @block.tensor
            def _(pe):
                pe.sem_inc(qk_full, 2)
                pe.sem_inc(v_full, 2)
                pe.wait_ge(w_in, 32)
                pe.wait_ge(prep, 1)

                def body(s, h, q, on):
                    if on(1):
                        t, r = s - 1, (q - 1) % 2
                        pe.wait_ge(lhs_done, t + 1)
                        pe.wait_ge(raw_done, t + 1)
                        for k in range(KD):
                            pe.matmul(pQ[r][:, :], lhs[r][:, k, :], w[:, k, 0:2 * D], start=k == 0, stop=False)
                        pe.matmul(pQ[r][:, :], one[:, :], brow[:, 0:2 * D], start=False, stop=True).then_inc(qk_full, 1)
                        pe.wait_ge(v_done, t + 1)
                        for k in range(KD):
                            pe.matmul(pV[r][:, 0:D], lhs[r][:, k, :], w[:, k, 2 * D:3 * D], start=k == 0, stop=False)
                        pe.matmul(pV[r][:, 0:D], one[:, :], brow[:, 2 * D:3 * D], start=False, stop=True).then_inc(v_full, 1)
                steps(pe, BL, 2, 2, body)

            @block.gpsimd
            def _(pool):
                pool.sem_inc(ts_done, 2)
                pool.wait_ge(T["rope_in"], 16)

                def body(s, h, q, on):
                    if on(2):
                        t = s - 2
                        pool.wait_ge(raw_done, t + 3)
                        pool.wait_ge(rot_done, t + 1)
                        hold(pool, T)
                        x, o = halves(raw[q][:, :]), halves(ts_[q][:, :])
                        sin = cs[:, bass.ds(t, 1), 1, :].broadcast_to([P, 2, D // 2])
                        pool.tensor_tensor(o[:, :, 0, :], x[:, :, 1, :], sin, ALU.mult).then_inc(S("ts0"), 1)
                        pool.tensor_tensor(o[:, :, 1, :], x[:, :, 0, :], sin, ALU.mult).then_inc(ts_done, 1)
                        pool.wait_ge(S("ts0"), t + 1)
                        pool.wait_ge(ts_done, t + 3)
                steps(pool, BL, 2, 2, body)

            @block.vector
            def _(dve):
                dve.sem_inc(rot0, 2)
                dve.sem_inc(rot_done, 2)
                dve.memset(one[:, :], 1.0).then_inc(prep, 1)
                dve.wait_ge(T["rope_in"], 16)

                def body(s, h, q, on):
                    if on(2):
                        t = s - 2
                        dve.wait_ge(raw_done, t + 3)
                        dve.wait_ge(rot_done, t + 1)
                        cos = cs[:, bass.ds(t, 1), 0, :].broadcast_to([P, 4, D // 2])
                        dve.tensor_tensor(tc_[q][:, :].rearrange("p (a n) -> p a n", a=4),
                                          raw[q][:, :].rearrange("p (a n) -> p a n", a=4), cos, ALU.mult).then_inc(rot0, 1)
                        dve.wait_ge(rot0, t + 3)
                        dve.wait_ge(ts_done, t + 3)
                        o = qk[:, bass.ds(t, 1), :].rearrange("p b (a h n) -> p (b a) h n", a=2, h=2)
                        c, x = halves(tc_[q][:, :]), halves(ts_[q][:, :])
                        dve.tensor_tensor(o[:, :, 0, :], c[:, :, 0, :], x[:, :, 0, :], ALU.subtract).then_inc(S("rot1"), 1)
                        dve.tensor_tensor(o[:, :, 1, :], c[:, :, 1, :], x[:, :, 1, :], ALU.add).then_inc(rot_done, 1)
                steps(dve, BL, 2, 2, body)
                dve.wait_ge(S("rot1"), BL)
                dve.wait_ge(rot_done, BL + 2)


def attend(nc, T, W):
    with ExitStack() as ctx:
        sb = lambda name, shape, dt=F32: ctx.enter_context(nc.sbuf_tensor("at_" + name, shape, dt))
        sem = lambda name: ctx.enter_context(nc.semaphore("at_" + name))
        NS = BL // SEG
        HR = B * H
        qk, v = T["qk"], T["v"]
        cnt0 = sb("cnt0", [P, NS * N0 * H])
        cntc = sb("cntc", [P, NC])
        cntf = sb("cntf", [HR, NF])
        s0 = sb("s0", [P, NS, N0, H])
        sc = sb("sc", [P, NC])
        scx = sb("scx", [P, NC // 2])
        M = sb("M", [P, BL, H])
        Z = sb("Z", [P, BL, H])
        prod = [sb(f"prod{i}", [P, SEG * D]) for i in range(2)]
        mc = sb("mc", [P, NC // 2])
        far = T["far"]
        fq = T["fq"]
        fs = sb("fs", [HR, NF])
        fx = sb("fx", [HR, NF // 2])
        fm = sb("fm", [HR, NF // 2])
        fo = sb("fo", [HR, NJ, DH + 2])
        fb = sb("fb", [P, 2, H, DH + 2])
        fg = sb("fg", [P, 2, H])
        pc = T["prodc"]
        pf = T["prodf"][0:HR, :]
        o = T["o"]
        tabs, own_sem, pool_own = sem("tabs"), sem("own"), sem("pool_own")
        far_done, far_st, far_in, fo_done, fo_st, fb_in = (sem("far_done"), sem("far_st"), sem("far_in"),
                                                           sem("fo_done"), sem("fo_st"), sem("fb_in"))
        pc_done, pv_go, pv_done = sem("pc_done"), sem("pv_go"), sem("pv_done")
        e_req, e_done = sem("e_req"), sem("e_done")
        fq_, fk_, fv_ = (fq[:, :, i, :] for i in range(3))

        def rows_of(ap, r, rho, ns, nh, a):
            t0 = (2 + a) * r + rho
            return ap[:, t0:t0 + (ns - 1) * SEG * r + 1:SEG * r, rho:H:r]

        with nc.Block() as block:
            @block.sync
            def _(sp):
                for dst, src in ((cnt0[:, :], W["cnt0"]), (cntc[:, :], W["cntc"]), (cntf[:, :], W["cntf"])):
                    sp.dma_start(dst, src).then_inc(tabs, 16)
                sp.wait_ge(far_done, 6)
                sp.dma_start(T["far_d"].rearrange("p a h c d -> p (a h c d)"),
                             far[:, :, :, :, :].rearrange("p a h c d -> p (a h c d)")).then_inc(far_st, 16)
                sp.wait_ge(far_st, 16)
                src = T["far_d"].rearrange("(b n) a h c d -> b h n a (c d)", b=B)
                for b in range(B):
                    sp.dma_start(fq[b * H:(b + 1) * H, :, :, :].rearrange("h (n a) c d -> h n a (c d)", a=2),
                                 src[b]).then_inc(far_in, 16)
                sp.wait_ge(fo_done, 1)
                sp.dma_start(T["fo_d"].rearrange("h j c -> h (j c)"), fo[:, :, :].rearrange("h j c -> h (j c)")).then_inc(fo_st, 16)
                sp.wait_ge(fo_st, 16)
                back = T["fo_d"].rearrange("(b h) (n a) c -> b n a h c", b=B, a=2)
                n = L // BL
                for b in range(B):
                    for a in range(2):
                        sp.dma_start(fb[b * n:(b + 1) * n, a, :, :], back[b][:, a]).then_inc(fb_in, 16)
                sp.wait_ge(fb_in, 16 * B * 2)

            @block.scalar
            def _(act):
                act.wait_ge(e_req, 1)
                act.activation(fs[:, :], fs[:, :], ACT.Exp).then_inc(e_done, 1)
                act.wait_ge(e_req, 2)
                act.activation(s0[:, :, :, :], s0[:, :, :, :], ACT.Exp).then_inc(e_done, 1)
                act.activation(sc[:, :], sc[:, :], ACT.Exp).then_inc(e_done, 1)
                act.activation(fg[:, :, :], fg[:, :, :], ACT.Exp).then_inc(e_done, 1)

            qh = qk[:, :, 0:D].rearrange("p t (h d) -> p t h d", h=H)
            kh = qk[:, :, D:2 * D].rearrange("p t (h d) -> p t h d", h=H)
            vh = v[:, :, :].rearrange("p t (h d) -> p t h d", h=H)

            def key_rows(ap, r, rho, ns, b):
                t0 = b * r + rho
                return ap[:, t0:t0 + (ns - 1) * SEG * r + 1:SEG * r, rho:H:r]

            @block.gpsimd
            def _(pool):
                own = Chain(pool, pool_own)
                for a in range(2):
                    for c, src in enumerate((qk[:, :, 0:D], qk[:, :, D:2 * D], v[:, :, :])):
                        w = 2 * D if c < 2 else D
                        full = qk if c < 2 else v
                        flat = full[:, :, :].rearrange("p t n -> p (t n)")
                        off = a * H * w + (D if c == 1 else 0)
                        diag = flat[:, off:off + (H - 1) * (w + DH) + DH]
                        diag = bass.AP(diag.tensor, diag.offset, [diag.ap[0], [w + DH, H], [1, DH]])
                        pool.tensor_copy(far[:, a, :, c, :], diag).then_inc(far_done, 1)
                for r, rho, nh, ns, first in GROUPS:
                    out = pc[:, first * DH:(first + ns * 4 * nh) * DH].rearrange(
                        "p (s a b h d) -> p s a b h d", s=ns, a=2, b=2, h=nh)
                    for a in range(2):
                        for b in range(2):
                            pool.tensor_tensor(out[:, :, a, b, :, :], rows_of(qh, r, rho, ns, nh, a),
                                               key_rows(kh, r, rho, ns, b), ALU.mult).then_inc(pc_done, 1)
                pool.wait_ge(pc_done, 4 * len(GROUPS))
                pool.wait_ge(pv_go, 1)
                for r, rho, nh, ns, first in GROUPS:
                    out = pc[:, first * DH:(first + ns * 4 * nh) * DH].rearrange(
                        "p (s a b h d) -> p s a b h d", s=ns, a=2, b=2, h=nh)
                    wgt = sc[:, first:first + ns * 4 * nh].rearrange("p (s a b h) -> p s a b h", s=ns, a=2, b=2)
                    for a in range(2):
                        for b in range(2):
                            pool.tensor_tensor(out[:, :, a, b, :, :],
                                               wgt[:, :, a, b, :].unsqueeze(3).broadcast_to([P, ns, nh, DH]),
                                               key_rows(vh, r, rho, ns, b), ALU.mult).then_inc(pv_done, 1)

            @block.vector
            def _(dve):
                own = Chain(dve, own_sem)
                step = own.step
                tt = lambda out, a, b, op: step(dve.tensor_tensor(out, a, b, op))
                for s in range(NS):
                    for a in range(SEG):
                        n = (a + 1)
                        buf = prod[(s * SEG + a) % 2]
                        t = s * SEG
                        pr = buf[:, 0:n * D].rearrange("p (b x) -> p b x", b=n)
                        step(dve.tensor_tensor(pr, qk[:, t + a:t + a + 1, 0:D].broadcast_to([P, n, D]),
                                               qk[:, t:t + n, D:2 * D], ALU.mult))
                        own.mark(dve.tensor_reduce(s0[:, s, a * (a + 1) // 2:a * (a + 1) // 2 + n, :],
                                                   buf[:, 0:n * D].rearrange("p (b h d) -> p b h d", b=n, h=H),
                                                   AX.X, ALU.add))
                own.settle()
                dve.wait_ge(tabs, 48)
                s0f = s0[:, :, :, :].rearrange("p s n h -> p (s n h)")
                tt(s0f, s0f, cnt0[:, :], ALU.mult)
                dve.wait_ge(far_in, 16 * B)
                for r, ns, first in FGROUPS:
                    out = pf[:, first * DH:(first + ns * 4) * DH].rearrange("p (s a b d) -> p s a b d", s=ns, a=2, b=2)
                    for a in range(2):
                        qa = fq_[:, (2 + a) * r:(2 + a) * r + (ns - 1) * SEG * r + 1:SEG * r, :]
                        for b in range(2):
                            kb = fk_[:, b * r:b * r + (ns - 1) * SEG * r + 1:SEG * r, :]
                            own.mark(dve.tensor_tensor(out[:, :, a, b, :], qa, kb, ALU.mult))
                step(dve.memset(fo[:, :, DH:DH + 1], -1e30))
                step(dve.tensor_reduce(fs[:, :], pf[:, 0:NF * DH].rearrange("p (n d) -> p n d", d=DH), AX.X, ALU.add))
                tt(fs[:, :], fs[:, :], cntf[:, :], ALU.mult)
                step(dve.tensor_reduce(fx[:, :], fs[:, :].rearrange("p (n b) -> p n b", b=2), AX.X, ALU.max))

                def frows(c0, c1, r, ns):
                    return fo[:, :, c0:c1].rearrange("p (s q) c -> p s q c", q=SEG * r)[:, :, 2 * r:3 * r + 1:r, :]

                fxs = lambda buf, ns, first: buf[:, first // 2:(first + ns * 4) // 2].rearrange("p (s a c) -> p s a c", a=2, c=1)
                for r, ns, first in FGROUPS:
                    tt(frows(DH, DH + 1, r, ns), frows(DH, DH + 1, r, ns), fxs(fx, ns, first), ALU.max)
                for r, ns, first in FGROUPS:
                    own.mark(dve.tensor_copy(fxs(fm, ns, first), frows(DH, DH + 1, r, ns)))
                own.settle()
                dve.tensor_tensor(fs[:, :].rearrange("p (n b) -> p n b", b=2), fs[:, :].rearrange("p (n b) -> p n b", b=2),
                                  fm[:, :].unsqueeze(2).broadcast_to([HR, NF // 2, 2]), ALU.subtract).then_inc(e_req, 1)
                step(dve.memset(fo[:, :, 0:DH], 0.0))
                step(dve.memset(fo[:, :, DH + 1:DH + 2], 0.0))
                dve.wait_ge(e_done, 1)
                step(dve.tensor_reduce(fx[:, :], fs[:, :].rearrange("p (n b) -> p n b", b=2), AX.X, ALU.add))
                for r, ns, first in FGROUPS:
                    tt(frows(DH + 1, DH + 2, r, ns), frows(DH + 1, DH + 2, r, ns), fxs(fx, ns, first), ALU.add)
                for r, ns, first in FGROUPS:
                    out = pf[:, first * DH:(first + ns * 4) * DH].rearrange("p (s a b d) -> p s a b d", s=ns, a=2, b=2)
                    w = fs[:, first:first + ns * 4].rearrange("p (s a b) -> p s a b", a=2, b=2)
                    for a in range(2):
                        for b in range(2):
                            vb = fv_[:, b * r:b * r + (ns - 1) * SEG * r + 1:SEG * r, :]
                            own.mark(dve.tensor_tensor(out[:, :, a, b, :],
                                                       w[:, :, a, b].unsqueeze(2).broadcast_to([HR, ns, DH]), vb, ALU.mult))
                own.settle()
                pfh = pf[:, 0:NF * DH].rearrange("p (n b d) -> p n b d", b=2, d=DH)
                tt(pfh[:, :, 0, :], pfh[:, :, 0, :], pfh[:, :, 1, :], ALU.add)
                for i, (r, ns, first) in enumerate(FGROUPS):
                    part = pf[:, first * DH:(first + ns * 4) * DH].rearrange("p (s a b d) -> p s a b d", s=ns, a=2, b=2)
                    for a in range(2):
                        view = fo[:, :, 0:DH].rearrange("p (s q) c -> p s q c", q=SEG * r)[:, :, (2 + a) * r, :]
                        ins = dve.tensor_tensor(view, view, part[:, :, a, 0, :], ALU.add)
                        if i == len(FGROUPS) - 1 and a == 1:
                            ins.then_inc(fo_done, 1)
                        else:
                            step(ins)
                dve.wait_ge(pc_done, 4 * len(GROUPS))
                step(dve.tensor_reduce(sc[:, :], pc[:, 0:NC * DH].rearrange("p (n d) -> p n d", d=DH), AX.X, ALU.add))
                tt(sc[:, :], sc[:, :], cntc[:, :], ALU.mult)
                for a in range(SEG):
                    f = a * (a + 1) // 2
                    own.mark(dve.tensor_reduce(M[:, a:BL:SEG, :],
                                               s0[:, :, f:f + a + 1, :].rearrange("p s b h -> p s h b"), AX.X, ALU.max))
                own.settle()

                def parts(buf, r, rho, nh, ns, first):
                    return buf[:, first:first + ns * 4 * nh].rearrange("p (s a b h) -> p s a b h", s=ns, a=2, b=2)

                def halves(buf, r, rho, nh, ns, first):
                    return buf[:, first // 2:(first + ns * 4 * nh) // 2].rearrange("p (s a h) -> p s a h", s=ns, a=2)

                for g in GROUPS:
                    sp_ = parts(sc, *g)
                    hx = halves(scx, *g)
                    for a in range(2):
                        own.mark(dve.tensor_tensor(hx[:, :, a, :], sp_[:, :, a, 0, :], sp_[:, :, a, 1, :], ALU.max))
                own.settle()
                for gi, g in enumerate(GROUPS):
                    r, rho, nh, ns, first = g
                    if rho == 0:
                        own.settle()
                    for a in range(2):
                        m = rows_of(M, r, rho, ns, nh, a)
                        own.mark(dve.tensor_tensor(m, m, halves(scx, *g)[:, :, a, :], ALU.max))
                own.settle()
                dve.wait_ge(fb_in, 16 * B * 2)
                Mf = M[:, :, :].rearrange("p (a t) h -> p a (t h)", a=2)[:, :, 0:H * H:H + 1]
                Zf = Z[:, :, :].rearrange("p (a t) h -> p a (t h)", a=2)[:, :, 0:H * H:H + 1]
                tt(Mf, Mf, fb[:, :, :, DH], ALU.max)
                own.mark(dve.tensor_tensor(fg[:, :, :], fb[:, :, :, DH], Mf, ALU.subtract))
                for a in range(SEG):
                    f = a * (a + 1) // 2
                    for b in range(a + 1):
                        own.mark(dve.tensor_tensor(s0[:, :, f + b, :], s0[:, :, f + b, :], M[:, a:BL:SEG, :], ALU.subtract))
                for g in GROUPS:
                    r, rho, nh, ns, first = g
                    for a in range(2):
                        own.mark(dve.tensor_copy(halves(mc, *g)[:, :, a, :], rows_of(M, r, rho, ns, nh, a)))
                own.settle()
                for g in GROUPS:
                    for b in range(2):
                        own.mark(dve.tensor_tensor(parts(sc, *g)[:, :, :, b, :], parts(sc, *g)[:, :, :, b, :],
                                                   halves(mc, *g), ALU.subtract))
                own.settle()
                step(dve.tensor_copy(scx[:, 0:1], mc[:, 0:1]))
                dve.sem_inc(e_req, 1)
                dve.wait_ge(e_done, 4)
                for a in range(SEG):
                    f = a * (a + 1) // 2
                    own.mark(dve.tensor_reduce(Z[:, a:BL:SEG, :],
                                               s0[:, :, f:f + a + 1, :].rearrange("p s b h -> p s h b"), AX.X, ALU.add))
                for g in GROUPS:
                    sp_ = parts(sc, *g)
                    hx = halves(scx, *g)
                    for a in range(2):
                        own.mark(dve.tensor_tensor(hx[:, :, a, :], sp_[:, :, a, 0, :], sp_[:, :, a, 1, :], ALU.add))
                own.settle()
                for gi, g in enumerate(GROUPS):
                    r, rho, nh, ns, first = g
                    if rho == 0:
                        own.settle()
                    for a in range(2):
                        z = rows_of(Z, r, rho, ns, nh, a)
                        own.mark(dve.tensor_tensor(z, z, halves(scx, *g)[:, :, a, :], ALU.add))
                own.settle()
                fsum = fb[:, :, :, DH + 1]
                tt(fsum, fsum, fg[:, :, :], ALU.mult)
                tt(Zf, Zf, fsum, ALU.add)
                step(dve.reciprocal(Z[:, :, :], Z[:, :, :]))
                own.mark(dve.tensor_tensor(fg[:, :, :], fg[:, :, :], Zf, ALU.mult))
                for g in GROUPS:
                    r, rho, nh, ns, first = g
                    for a in range(2):
                        own.mark(dve.tensor_copy(halves(mc, *g)[:, :, a, :], rows_of(Z, r, rho, ns, nh, a)))
                own.settle()
                for gi, g in enumerate(GROUPS):
                    for b in range(2):
                        own.mark(dve.tensor_tensor(parts(sc, *g)[:, :, :, b, :], parts(sc, *g)[:, :, :, b, :],
                                                   halves(mc, *g), ALU.mult))
                own.settle()
                dve.tensor_copy(scx[:, 0:1], mc[:, 0:1]).then_inc(pv_go, 1)
                for a in range(SEG):
                    f = a * (a + 1) // 2
                    for b in range(a + 1):
                        own.mark(dve.tensor_tensor(s0[:, :, f + b, :], s0[:, :, f + b, :], Z[:, a:BL:SEG, :], ALU.mult))
                own.settle()
                for s in range(NS):
                    t = s * SEG
                    for a in range(SEG):
                        f, n = a * (a + 1) // 2, a + 1
                        buf = prod[(s * SEG + a) % 2]
                        if a == 0:
                            own.mark(dve.tensor_tensor(o[:, t, :].rearrange("p (h d) -> p h d", h=H),
                                                       s0[:, s, 0, :].unsqueeze(2).broadcast_to([P, H, DH]),
                                                       vh[:, t, :, :], ALU.mult))
                            continue
                        own.settle()
                        step(dve.tensor_tensor(buf[:, 0:n * D].rearrange("p (n d) -> p n d", d=DH),
                                               s0[:, s, f:f + n, :].rearrange("p b h -> p (b h)").unsqueeze(2).broadcast_to([P, n * H, DH]),
                                               v[:, t:t + n, :].rearrange("p b (h d) -> p (b h) d", h=H), ALU.mult))
                        own.mark(dve.tensor_reduce(o[:, t + a, :], buf[:, 0:n * D].rearrange("p (b x) -> p x b", b=n),
                                                   AX.X, ALU.add))
                own.settle()
                oh = o.rearrange("p t (h d) -> p t h d", h=H)
                dve.wait_ge(pv_done, 4 * len(GROUPS))
                for gi, g in enumerate(GROUPS):
                    r, rho, nh, ns, first = g
                    part = pc[:, first * DH:(first + ns * 4 * nh) * DH].rearrange(
                        "p (s a b h d) -> p s a b h d", s=ns, a=2, b=2, h=nh)
                    if rho == 0:
                        own.settle()
                    for a in range(2):
                        x = rows_of(oh, r, rho, ns, nh, a)
                        step(dve.tensor_tensor(x, x, part[:, :, a, 0, :, :], ALU.add))
                        own.mark(dve.tensor_tensor(x, x, part[:, :, a, 1, :, :], ALU.add))
                own.settle()
                tt(fb[:, :, :, 0:DH], fb[:, :, :, 0:DH], fg[:, :, :].unsqueeze(3).broadcast_to([P, 2, H, DH]), ALU.mult)
                for a in range(2):
                    x = T["o_diag"](a)
                    own.mark(dve.tensor_tensor(x, x, fb[:, a, :, 0:DH], ALU.add))
                own.settle()


def attend_out(nc, T, W):
    with ExitStack() as ctx:
        S = Sems(nc, ctx, "ao_")
        sb = lambda name, shape, dt=F32: ctx.enter_context(nc.sbuf_tensor("ao_" + name, shape, dt))
        w = sb("w", [P, KD, D])
        brow = sb("brow", [1, D])
        one = sb("one", [1, P])
        oc = [sb(f"oc{i}", [P, D]) for i in range(2)]
        oT = [sb(f"oT{i}", [P, KD, P]) for i in range(2)]
        rs_ = [sb(f"res{i}", [P, D]) for i in range(2)]
        xo = [sb(f"xo{i}", [P, D]) for i in range(2)]
        xT = [sb(f"xT{i}", [P, KD, P]) for i in range(2)]
        st = [sb(f"st{i}", [P, 6]) for i in range(2)]
        mv = [sb(f"mv{i}", [P, 2]) for i in range(2)]
        var = [sb(f"var{i}", [P, 1]) for i in range(2)]
        rs = [sb(f"rs{i}", [P, 1]) for i in range(2)]
        o, x2b, x3, ident = T["o"], T["x2b"], T["x1"], T["ident"]
        x2_in, w_in, prep = S("x2_in"), S("w_in"), S("prep")
        oc_done, oT_full, oT_done, y_full, res_done, own_sem = (S("oc"), S("oT_full"), S("oT"), S("y_full"), S("res"), S("own"))
        var_done, rs_done, xo_done, xT_full, xT_done, g_full, lg_done = (S("var"), S("rs"), S("xo"), S("xT_full"),
                                                                       S("xT"), S("g_full"), S("lg"))
        x3_done, stored = S("x3"), [S(f"stored{i}") for i in range(2)]

        with ExitStack() as pctx, nc.Block() as block:
            pT, pO, pX, pG = ([pctx.enter_context(nc.psum_tensor(f"ao_{nm}{i}", [P, 512], F32)) for i in range(2)]
                              for nm in ("pT", "pO", "pX", "pG"))

            @block.sync
            def _(sp):
                sp.dma_start(w[:, :, :], W["woT"].rearrange("(k p) n -> p k n", p=P)).then_inc(w_in, 16)
                sp.dma_start(brow[:, :], W["bo"].rearrange("(a n) -> a n", a=1)).then_inc(w_in, 16)
                sp.dma_start(x2b, T["x2_d"].rearrange("(p i) d -> p i d", i=BL)).then_inc(x2_in, 16)
                for i in range(2):
                    sp.sem_inc(stored[i], 16)

                def body(s, h, q, on):
                    sp.wait_ge(xo_done, s + 3)
                    sp.dma_start(T["x3_d"].rearrange("(p i) d -> p i d", i=BL)[:, bass.ds(s, 1), :]
                                 .rearrange("p i d -> p (i d)"), xo[q][:, :]).then_inc(stored[q], 16)
                steps(sp, BL, 0, 2, body)
                for i in range(2):
                    sp.wait_ge(stored[i], 16 * (BL // 2 + 1))

            @block.gpsimd
            def _(pool):
                def body(s, h, q, on):
                    if on(0):
                        pool.wait_ge(oT_full, s + 1)
                        hold(pool, T)
                        pool.tensor_copy(oc[q][:, :], o[:, bass.ds(s, 1), :].rearrange("p a d -> p (a d)")).then_inc(oc_done, 1)
                    if on(3):
                        t, r = s - 3, (q - 3) % 2
                        pool.wait_ge(var_done, t + 1)
                        pool.tensor_tensor(rs[r][:, :], var[r][:, :], T["half"][:, 0:1], ALU.pow).then_inc(rs_done, 1)
                steps(pool, BL, 3, 2, body)

            @block.tensor
            def _(pe):
                pe.sem_inc(oT_full, 2)
                pe.sem_inc(y_full, 2)
                pe.sem_inc(xT_full, 2)
                pe.sem_inc(g_full, 2)
                pe.wait_ge(w_in, 32)
                pe.wait_ge(prep, 1)

                def body(s, h, q, on):
                    if on(1):
                        t, r = s - 1, (q - 1) % 2
                        pe.wait_ge(oc_done, t + 1)
                        pe.wait_ge(oT_done, t + 1)
                        for k in range(KD):
                            mm = pe.transpose(pT[r][:, k * P:(k + 1) * P], oc[r][:, k * P:(k + 1) * P], ident[:, :])
                        mm.then_inc(oT_full, 1)
                    if on(2):
                        t, r = s - 2, q
                        pe.wait_ge(oT_done, t + 3)
                        pe.wait_ge(res_done, t + 1)
                        for k in range(KD):
                            pe.matmul(pO[r][:, 0:D], oT[r][:, k, :], w[:, k, :], start=k == 0, stop=False)
                        pe.matmul(pO[r][:, 0:D], one[:, :], brow[:, :], start=False, stop=True).then_inc(y_full, 1)
                    if on(5):
                        t, r = s - 5, (q - 5) % 2
                        pe.wait_ge(xo_done, t + 3)
                        pe.wait_ge(xT_done, t + 1)
                        for k in range(KD):
                            mm = pe.transpose(pX[r][:, k * P:(k + 1) * P], xo[r][:, k * P:(k + 1) * P], ident[:, :])
                        mm.then_inc(xT_full, 1)
                    if on(6):
                        t, r = s - 6, q
                        pe.wait_ge(xT_done, t + 3)
                        pe.wait_ge(lg_done, t + 1)
                        for k in range(KD):
                            mm = pe.matmul(pG[r][:, 0:E_], xT[r][:, k, :], T["w_route"][:, k, :], start=k == 0, stop=k == KD - 1)
                        mm.then_inc(g_full, 1)
                steps(pe, BL, 6, 2, body)

            @block.scalar
            def _(act):
                act.sem_inc(oT_done, 2)
                act.sem_inc(xT_done, 2)

                def body(s, h, q, on):
                    if on(1):
                        t, r = s - 1, (q - 1) % 2
                        act.wait_ge(oT_full, t + 3)
                        act.wait_ge(y_full, t + 1)
                        act.activation(oT[r][:, :, :].rearrange("p k n -> p (k n)"), pT[r][:, 0:D], ACT.Identity).then_inc(oT_done, 1)
                    if on(5):
                        t, r = s - 5, (q - 5) % 2
                        act.wait_ge(xT_full, t + 3)
                        act.wait_ge(g_full, t + 1)
                        act.activation(xT[r][:, :, :].rearrange("p k n -> p (k n)"), pX[r][:, 0:D], ACT.Identity).then_inc(xT_done, 1)
                steps(act, BL, 6, 2, body)

            @block.vector
            def _(dve):
                dve.sem_inc(res_done, 2)
                dve.sem_inc(xo_done, 2)
                dve.sem_inc(lg_done, 2)
                dve.memset(one[:, :], 1.0).then_inc(prep, 1)
                dve.wait_ge(x2_in, 16)

                def body(s, h, q, on):
                    if on(2):
                        t, r = s - 2, q
                        own = Chain(dve, own_sem, t, 2)
                        dve.wait_ge(y_full, t + 3)
                        dve.wait_ge(xo_done, t + 1)
                        dve.tensor_tensor(rs_[r][:, :], pO[r][:, 0:D],
                                          x2b[:, bass.ds(t, 1), :].rearrange("p a d -> p (a d)"), ALU.add).then_inc(res_done, 1)
                        dve.wait_ge(res_done, t + 3)
                        own.step(dve.bn_stats(st[r][:, :], rs_[r][:, :]))
                        hold(dve, T)
                        own.step(dve.bn_aggr(mv[r][:, :], st[r][:, :]))
                        dve.tensor_scalar(var[r][:, :], mv[r][:, 1:2], EPS, None, ALU.add).then_inc(var_done, 1)
                        own.close()
                    if on(3):
                        t, r = s - 3, (q - 3) % 2
                        dve.wait_ge(rs_done, t + 1)
                        dve.wait_ge(stored[r], (h + (q - 3) // 2 + 1) * 16)
                        dve.wait_ge(xT_full, t + 1)
                        dve.wait_ge(x3_done, t + 1)
                        dve.tensor_scalar(xo[r][:, :], rs_[r][:, :], mv[r][:, 0:1], rs[r][:, 0:1],
                                          ALU.subtract, ALU.mult).then_inc(xo_done, 1)
                        dve.wait_ge(xo_done, t + 3)
                        hold(dve, T)
                        dve.tensor_copy(x3[:, bass.ds(t, 1), :].rearrange("p a d -> p (a d)"), xo[r][:, :]).then_inc(x3_done, 1)
                    if on(6):
                        t, r = s - 6, q
                        dve.wait_ge(g_full, t + 3)
                        hold(dve, T)
                        dve.tensor_copy(T["logits"][:, bass.ds(t, 1), :].rearrange("p a e -> p (a e)"),
                                        pG[r][:, 0:E_]).then_inc(lg_done, 1)
                dve.sem_inc(x3_done, 2)
                steps(dve, BL, 6, 2, body)
                dve.wait_ge(lg_done, BL + 2)
                dve.wait_ge(x3_done, BL + 2)


def experts1(nc, T, n, pre):
    with ExitStack() as ctx:
        S = Sems(nc, ctx, pre)
        sb = lambda name, shape, dt=F32: ctx.enter_context(nc.sbuf_tensor(pre + name, shape, dt))
        ix = [sb(f"ix{i}", [P, 1], I32) for i in range(4)]
        xg = [sb(f"xg{i}", [P, D]) for i in range(4)]
        xT = [sb(f"xT{i}", [P, KD, P]) for i in range(2)]
        hb = [sb(f"hb{i}", [P, D]) for i in range(2)]
        hn = [sb(f"hn{i}", [P, D]) for i in range(2)]
        hT = [sb(f"hT{i}", [P, KD, P]) for i in range(2)]
        yo = [sb(f"yo{i}", [P, D]) for i in range(2)]
        st = [sb(f"st{i}", [P, 6]) for i in range(2)]
        mv = [sb(f"mv{i}", [P, 2]) for i in range(2)]
        var = [sb(f"var{i}", [P, 1]) for i in range(2)]
        rs = [sb(f"rs{i}", [P, 1]) for i in range(2)]
        ident, w1, w2, b1, b2, g1, be1 = (T[k] for k in ("ident", "w1", "w2b", "b1", "b2", "g1", "be1"))
        ix_done, xT_full, xT_done, h_full, hb_done = S("ix_done"), S("xT_full"), S("xT_done"), S("h_full"), S("hb_done")
        own_sem, var_done, rs_done, hn_done = S("own"), S("var_done"), S("rs_done"), S("hn_done")
        hT_full, hT_done, y_full, y_done = S("hT_full"), S("hT_done"), S("y_full"), S("y_done")
        x_in = [S(f"x_in{i}") for i in range(4)]
        y_stored = [S(f"y_stored{i}") for i in range(2)]
        expert = lambda eng, t: eng.value_load(T["tile_exp"][0:1, bass.ds(t, 1)], min_val=0, max_val=E_ - 1)
        row = lambda ap, e: ap[:, bass.ds(e, 1), :].rearrange("p a n -> p (a n)")

        with ExitStack() as pctx, nc.Block() as block:
            pX, pH, pHT, pY = ([pctx.enter_context(nc.psum_tensor(f"{pre}{nm}{i}", [P, 512], F32))
                                for i in range(2)] for nm in ("pX", "pH", "pHT", "pY"))

            @block.gpsimd
            def _(pool):
                def body(s, h, q, on):
                    if on(0):
                        pool.wait_ge(xT_full, s + 1)
                        hold(pool, T)
                        pool.tensor_copy(ix[q][:, :], T["slot_tok"][:, bass.ds(s, 1)]).then_inc(ix_done, 1)
                        pool.wait_ge(ix_done, s + 1)
                        hold(pool, T)
                        pool.indirect_dma_start(xg[q][:, :], None, T["x3_d"],
                                                bass.IndirectOffsetOnAxis(ap=ix[q][:, 0:1], axis=0)).then_inc(x_in[q], 16)
                    if on(2):
                        t, r = s - 2, q % 2
                        pool.wait_ge(var_done, t + 1)
                        pool.tensor_tensor(rs[r][:, :], var[r][:, :], T["half"][:, 0:1], ALU.pow).then_inc(rs_done, 1)
                steps(pool, n, 4, 4, body)

            @block.sync
            def _(sp):
                for i in range(2):
                    sp.sem_inc(y_stored[i], 16)

                def body(s, h, q, on):
                    sp.wait_ge(y_done, s + 3)
                    sp.dma_start(T["y_d"][bass.ds(s * P, P), :], yo[q % 2][:, :]).then_inc(y_stored[q % 2], 16)
                steps(sp, n, 0, 4, body)
                for i in range(2):
                    sp.wait_ge(y_stored[i], 16 * (n // 2 + 1))

            @block.tensor
            def _(pe):
                pe.sem_inc(xT_full, 4)
                pe.sem_inc(h_full, 2)
                pe.sem_inc(hT_full, 2)
                pe.sem_inc(y_full, 2)
                pe.wait_ge(T["w1_in"], T["w1_n"])

                def body(s, h, q, on):
                    if on(0):
                        pe.wait_ge(x_in[q], (h + 1) * 16)
                        pe.wait_ge(xT_done, s + 1)
                        for k in range(KD):
                            mm = pe.transpose(pX[q % 2][:, k * P:(k + 1) * P], xg[q][:, k * P:(k + 1) * P], ident[:, :])
                        mm.then_inc(xT_full, 1)
                    if on(1):
                        t, r = s - 1, (q - 1) % 2
                        e = expert(pe, t)
                        pe.wait_ge(xT_done, t + 3)
                        pe.wait_ge(hb_done, t + 1)
                        for k in range(KD):
                            mm = pe.matmul(pH[r][:, 0:D], xT[r][:, k, :], row(w1[:, :, k, :], e),
                                           start=k == 0, stop=k == KD - 1)
                        mm.then_inc(h_full, 1)
                    if on(3):
                        t, r = s - 3, (q - 3) % 2
                        pe.wait_ge(hn_done, t + 3)
                        pe.wait_ge(hT_done, t + 1)
                        for k in range(KD):
                            mm = pe.transpose(pHT[r][:, k * P:(k + 1) * P], hn[r][:, k * P:(k + 1) * P], ident[:, :])
                        mm.then_inc(hT_full, 1)
                    if on(4):
                        t, r = s - 4, q % 2
                        e = expert(pe, t)
                        pe.wait_ge(hT_done, t + 3)
                        pe.wait_ge(y_done, t + 1)
                        for k in range(KD):
                            mm = pe.matmul(pY[r][:, 0:D], hT[r][:, k, :], row(w2[:, :, k, :], e),
                                           start=k == 0, stop=k == KD - 1)
                        mm.then_inc(y_full, 1)
                steps(pe, n, 4, 4, body)

            @block.scalar
            def _(act):
                act.sem_inc(xT_done, 2)
                act.sem_inc(hT_done, 2)
                act.wait_ge(T["w1_in"], T["w1_n"])

                def body(s, h, q, on):
                    if on(0):
                        act.wait_ge(xT_full, s + 5)
                        act.wait_ge(h_full, s + 1)
                        act.activation(xT[q % 2][:, :, :].rearrange("p k n -> p (k n)"), pX[q % 2][:, 0:D],
                                       ACT.Identity).then_inc(xT_done, 1)
                    if on(3):
                        t, r = s - 3, (q - 3) % 2
                        e = expert(act, t)
                        act.wait_ge(hT_full, t + 3)
                        act.wait_ge(y_full, t + 1)
                        hold(act, T)
                        for k in range(KD):
                            ins = act.activation(hT[r][:, k, :], pHT[r][:, k * P:(k + 1) * P], ACT.Gelu,
                                                 scale=g1[:, k, bass.ds(e, 1)], bias=be1[:, k, bass.ds(e, 1)])
                        ins.then_inc(hT_done, 1)
                steps(act, n, 4, 4, body)

            @block.vector
            def _(dve):
                dve.sem_inc(hb_done, 2)
                dve.sem_inc(hn_done, 2)
                dve.sem_inc(y_done, 2)
                dve.wait_ge(T["w1_in"], T["w1_n"])

                def body(s, h, q, on):
                    if on(1):
                        t, r = s - 1, (q - 1) % 2
                        own = Chain(dve, own_sem, t, 2)
                        e = expert(dve, t)
                        dve.wait_ge(h_full, t + 3)
                        dve.wait_ge(hn_done, t + 1)
                        dve.tensor_tensor(hb[r][:, :], pH[r][:, 0:D], row(b1, e), ALU.add).then_inc(hb_done, 1)
                        dve.wait_ge(hb_done, t + 3)
                        own.step(dve.bn_stats(st[r][:, :], hb[r][:, :]))
                        hold(dve, T)
                        own.step(dve.bn_aggr(mv[r][:, :], st[r][:, :]))
                        dve.tensor_scalar(var[r][:, :], mv[r][:, 1:2], EPS, None, ALU.add).then_inc(var_done, 1)
                        own.close()
                    if on(2):
                        t, r = s - 2, q % 2
                        dve.wait_ge(rs_done, t + 1)
                        dve.wait_ge(hT_full, t + 1)
                        dve.tensor_scalar(hn[r][:, :], hb[r][:, :], mv[r][:, 0:1], rs[r][:, 0:1],
                                          ALU.subtract, ALU.mult).then_inc(hn_done, 1)
                    if on(4):
                        t, r = s - 4, q % 2
                        e = expert(dve, t)
                        dve.wait_ge(y_full, t + 3)
                        dve.wait_ge(y_stored[r], (h * 2 + (q - 4) // 2 + 1) * 16)
                        dve.tensor_tensor(yo[r][:, :], pY[r][:, 0:D], row(b2, e), ALU.add).then_inc(y_done, 1)
                steps(dve, n, 4, 4, body)


SLOTS0 = 4 * NT + E_
SLOTS1 = 2 * NT + E_


def shape_tables():
    p, t = np.arange(P), np.arange(NT)
    c32 = np.zeros((P, 256), np.float32)
    c32[:, 0:E_] = E_ - np.arange(E_)
    c32[:, 16:48] = P * t
    c32[:, 48:192] = np.arange(SLOTS0)
    c32[:, 192:224] = P * t[None, :] + p[:, None] - MID_ID
    c32[:, 224:256] = BL * p[:, None] + t[None, :] - MID_ID
    c16 = np.zeros((P, SLOTS0 + 2 * P), np.float16)
    c16[:, 0:SLOTS0] = np.arange(SLOTS0)
    c16[:, SLOTS0:SLOTS0 + P] = p[:, None] < p[None, :]
    c16[:, SLOTS0 + P:] = 1.0
    return c32, c16


def network(nc, W):
    with ExitStack() as ctx:
        def sb(name, shape, dt=F32):
            return ctx.enter_context(nc.sbuf_tensor(name, shape, dt))

        def sem(name):
            return ctx.enter_context(nc.semaphore(name))

        def dram(name, shape):
            return nc.dram_tensor(name, shape, F32, kind="Internal").ap()

        x = sb("x", [P, NT, D])
        R = sb("R", [P, CI * N])
        ident = sb("ident_sb", [P, P])
        half = sb("half", [P, NT])
        c32 = sb("c32_sb", [P, 256])
        c16 = sb("c16_sb", [P, SLOTS0 + 2 * P], F16)
        T = {
            "x1": x, "v": x, "ident": ident, "half": half, "zs": R[:, :].rearrange("p (c n) -> p c n", c=CI),
            "held": sem("held"), "w_ins": sem("ws_in"), "w_in0": sem("w0_in"), "w1_in": sem("w1_in"),
            "rope_in": sem("rope_in"), "w_ns": 32, "w_n0": 32, "w1_n": 96,
            "mixed": dram("mixed", [2, N]), "states": dram("states", [N]),
            "x1_d": dram("x1_d", [N, D]), "x2_d": dram("x2_d", [N, D]), "x3_d": dram("x3_d", [N, D]),
            "y_d": dram("y_d", [SLOTS0 * P, D]),
            "far_d": dram("far_d", [P, 2, H, 3, DH]), "fo_d": dram("fo_d", [B * H, NJ, DH + 2]),
            "w13s": sb("w13s", [P, KD, 2 * IN0]), "w2s": sb("w2s", [P, D]),
            "w_gate": sb("w_gate", [P, KD, E_]), "w_route": sb("w_route", [P, KD, E_]),
            "w130": R[:, 0:E_ * KD * 2 * IN0].rearrange("p (e k n) -> p e k n", e=E_, k=KD),
            "w20": R[:, E_ * KD * 2 * IN0:E_ * KD * 2 * IN0 + E_ * D].rearrange("p (e n) -> p e n", e=E_),
            "x2T": R[:, 0:KD * N].rearrange("p (k n) -> p k n", k=KD),
            "rope": R[:, KD * N:KD * N + BL * D].rearrange("p (t a n) -> p t a n", t=BL, a=2),
            "logits": sb("logits", [P, NT, E_]),
            "tile_exp": sb("tile_exp", [1, SLOTS0], I32), "slot_tok": sb("slot_tok", [P, SLOTS0], I32),
            "slot_of": sb("slot_of", [P, NT, 4], I32), "slot_w": sb("slot_w", [P, NT, 4]),
            "c32": {"rev": c32[:, 0:16], "thr": c32[:, 16:48], "iota": c32[:, 48:192]},
            "c16": {"iota": c16[:, 0:SLOTS0], "tri": c16[:, SLOTS0:SLOTS0 + P], "ones": c16[:, SLOTS0 + P:]},
        }
        route_b = [sb(f"route_b{i}", [P, E_]) for i in range(2)]
        T["route_b"] = route_b[0]
        early, half_done = sem("early"), sem("half_done")
        stage_sems = range(half_done.num + 1, 256)

        with nc.Block() as block:
            @block.gpsimd
            def _(pool):
                pool.memset(half[:, :], -0.5).then_inc(half_done, 1)
                for dst, src, s in (
                        (T["w13s"][:, :, :], W["w13s"].rearrange("(k p) n -> p k n", p=P), T["w_ins"]),
                        (T["w2s"][:, :], W["w2s"], T["w_ins"]),
                        (T["w_gate"][:, :, :], W["gateT"].rearrange("(k p) e -> p k e", p=P), early),
                        (T["w_route"][:, :, :], W["Wr"].rearrange("(k p) e -> p k e", p=P), early),
                        (route_b[0][:, :], W["gate_b"].partition_broadcast(P), early),
                        (route_b[1][:, :], W["br"].partition_broadcast(P), early),
                        (c32[:, :], W["c32"], early),
                        (c16[:, :], W["c16"], early)):
                    pool.dma_start(dst, src).then_inc(s, 16)
                pool.wait_ge(half_done, 1)

        mixer(nc, T, W)

        with nc.Block() as block:
            @block.sync
            def _(sp):
                sp.wait_ge(early, 16 * 6)
                sp.dma_start(T["w130"], W["w13T"].rearrange("e (k p) n -> p e k n", p=P)).then_inc(T["w_in0"], 16)
                sp.dma_start(T["w20"], W["w2T"].rearrange("e p n -> p e n")).then_inc(T["w_in0"], 16)

        experts0(nc, T, False, NT, "sh_")
        dispatch(nc, T, 4, SLOTS0, True, c32[:, 192:224], "d0_")
        experts0(nc, T, True, SLOTS0, "e0_")

        with nc.Block() as block:
            @block.sync
            def _(sp):
                sp.dma_start(T["rope"], W["rope"]).then_inc(T["rope_in"], 16)

        combine(nc, T, 4, x, lambda s: T["x2_d"][bass.ds(s * P, P), :], True, "c0_")

        with ExitStack() as actx:
            qk = actx.enter_context(nc.sbuf_tensor("qk", [P, BL, 2 * D], F32))
            flat = qk[:, :, :].rearrange("p t n -> p (t n)")
            n_c, n_f, n_far = NC * DH, NF * DH, 2 * H * 3 * DH
            T.update({
                "qk": qk, "o": qk[:, :, 0:D], "x2b": qk[:, :, D:2 * D],
                "o_diag": lambda a: bass.AP(flat.tensor, a * H * 2 * D, [flat.ap[0], [2 * D + DH, H], [1, DH]]),
                "prodc": R[:, 0:n_c], "prodf": R[:, n_c:n_c + n_f],
                "far": R[:, n_c + n_f:n_c + n_f + n_far].rearrange("p (a h c d) -> p a h c d", a=2, h=H, c=3),
                "fq": R[0:B * H, n_c + n_f + n_far:n_c + n_f + n_far + NJ * 3 * DH]
                .rearrange("p (j c d) -> p j c d", j=NJ, c=3),
            })
            project_qkv(nc, T, W)
            attend(nc, T, W)
            T["w1"] = R[:, 0:E_ * KD * D].rearrange("p (e k n) -> p e k n", e=E_, k=KD)
            T["w2b"] = R[:, E_ * KD * D:2 * E_ * KD * D].rearrange("p (e k n) -> p e k n", e=E_, k=KD)
            with nc.Block() as block:
                @block.scalar
                def _(act):
                    for dst, src in ((T["w1"], W["W1"]), (T["w2b"], W["W2"])):
                        act.dma_start(dst, src.rearrange("e (k p) n -> p e k n", p=P)).then_inc(T["w1_in"], 16)
            attend_out(nc, T, W)

        T["b1"], T["b2"] = sb("b1", [P, E_, D]), sb("b2", [P, E_, D])
        T["g1"], T["be1"] = sb("g1", [P, KD, E_]), sb("be1", [P, KD, E_])
        T["route_b"] = route_b[1]
        with nc.Block() as block:
            @block.gpsimd
            def _(pool):
                pool.sem_clear(stage_sems)

            @block.sync
            def _(sp):
                for dst, src in ((T["b1"], W["b1"]), (T["b2"], W["b2"])):
                    sp.dma_start(dst[:, :, :].rearrange("p e n -> p (e n)"),
                                 src.rearrange("e n -> (e n)").partition_broadcast(P)).then_inc(T["w1_in"], 16)
                for dst, src in ((T["g1"], W["g1T"]), (T["be1"], W["be1T"])):
                    sp.dma_start(dst[:, :, :], src.rearrange("(k p) e -> p k e", p=P)).then_inc(T["w1_in"], 16)

        dispatch(nc, T, 2, SLOTS1, False, c32[:, 224:256], "d1_")
        experts1(nc, T, SLOTS1, "e1_")
        out = W["out"].rearrange("(p i) d -> p i d", i=BL)
        combine(nc, T, 2, x, lambda s: out[:, bass.ds(s, 1), :].rearrange("p i d -> p (i d)"), False, "c1_")


def layouts(inputs):
    a = {k: np.asarray(v) for k, v in inputs.items()}
    m, f, t, g = (lambda n, p=p: a[p + n] for p in ("L0_attn_", "L0_ffn_", "L1_attn_", "L1_ffn_"))
    cnt0, cntc, cntf = count_tables()
    c32, c16 = shape_tables()
    out = {"x": m("x").reshape(N, D), "xT": m("x").reshape(N, D).T}
    for n in ("W_in", "W_conv", "W_xproj", "W_dt", "b_dt", "W_out"):
        out[n] = m(n)
    out.update({
        "ln_g": m("ln_g").reshape(CI, P).T, "ln_b": m("ln_b").reshape(CI, P).T, "ident": np.eye(P, dtype=np.float32),
        "gateT": f("gate_w").T, "gate_b": f("gate_b"), "w13T": f("w13").transpose(0, 2, 1),
        "w2T": f("w2").transpose(0, 2, 1), "w13s": f("w13_s").T, "w2s": f("w2_s").T,
        "wqkvT": np.concatenate([t("Wq"), t("Wk"), t("Wv")]).T, "bqkv": np.concatenate([t("bq"), t("bk"), t("bv")]),
        "woT": t("Wo").T, "bo": t("bo"), "rope": rope_tables(), "cnt0": cnt0, "cntc": cntc, "cntf": cntf,
        "Wr": g("Wr"), "br": g("br"), "W1": g("W1"), "b1": g("b1"), "W2": g("W2"), "b2": g("b2"),
        "g1T": g("g1").T, "be1T": g("be1").T, "c32": c32, "c16": c16})
    return {k: np.ascontiguousarray(v) for k, v in out.items()}


def kernel(**inputs):
    import concourse.bacc as bacc
    from concourse.bass_utils import run_bass_kernel_spmd

    nc = bacc.Bacc("TRN2", target_bir_lowering=False, num_devices=1)
    arrays = layouts(inputs)
    W = {name: nc.dram_tensor("in_" + name, a.shape, mybir.dt.from_np(a.dtype), kind="ExternalInput").ap()
         for name, a in arrays.items()}
    W["out"] = nc.dram_tensor("out_x", (N, D), F32, kind="ExternalOutput").ap()
    network(nc, W)
    r = run_bass_kernel_spmd(nc, [{"in_" + name: a for name, a in arrays.items()}], core_ids=[0])
    return r.results[0]["out_x"].reshape(B, L, D)
```

```python
from contextlib import ExitStack

import concourse.bass as bass
import numpy as np
from concourse import mybir


ALU = mybir.AluOpType
ACT = mybir.ActivationFunctionType
AX = mybir.AxisListType
F32 = mybir.dt.float32
F16 = mybir.dt.float16
BF16 = mybir.dt.bfloat16
I32 = mybir.dt.int32

P = 128
D = 256
KD = D // P
B, L = 4, 1024
N = B * L
NT = N // P
TB = L // P
DI, DS, DTR = 512, 16, 64
CI = DI // P
G = L // 512
EPS = 1e-5


class Chain:

    def __init__(self, eng, sem, it=0, per=0):
        self.eng, self.sem, self.it, self.per, self.n = eng, sem, it, per, 0

    def mark(self, ins):
        ins.then_inc(self.sem, 1)
        self.n += 1

    def settle(self):
        self.eng.wait_ge(self.sem, self.it * self.per + self.n)

    def step(self, ins):
        self.mark(ins)
        self.settle()

    def close(self):
        assert self.n == self.per, (self.n, self.per)


def hold(eng, T):
    eng.sem_inc(T["held"], 1)


def mixer(nc, T, W):
    with ExitStack() as ctx:
        def sb(name, shape, dt=F32):
            return ctx.enter_context(nc.sbuf_tensor("mx_" + name, shape, dt))

        def sem(name):
            return ctx.enter_context(nc.semaphore("mx_" + name))

        ident = T["ident"]
        x1 = T["x1"]
        xin = x1[:, :, :].rearrange("p t d -> p (t d)").rearrange("p (k n) -> p k n", k=KD)
        w_in = sb("w_in", [P, KD, 2 * DI])
        w_conv = sb("w_conv", [P, CI, 3])
        w_x = sb("w_x", [P, CI, DTR + 2 * DS])
        w_small = sb("w_small", [P, CI, DS + 2])
        w_dt = sb("w_dt", [DTR + 1, DI])
        w_dtsum = sb("w_dtsum", [DTR + 1, 1])
        w_out = sb("w_out", [P, CI, D])
        ln_g = sb("ln_g", [P, CI])
        ln_b = sb("ln_b", [P, CI])
        xs_pad = [sb(f"xs_pad{i}", [P, L + 2]) for i in range(2)]
        convs = sb("conv", [P, 2, L])
        conv = [convs[:, i, :] for i in range(2)]
        xs = sb("xs", [P, CI, L])
        zs = T["zs"]
        zsil = sb("zsil", [P, CI, L])
        yz = xs
        dtl = sb("dtl", [DTR + 1, L])
        small = sb("small", [P, NT, DS + 2])
        absu = sb("absu", [P, DI])
        expu = sb("expu", [P, DI])
        lnu = sb("lnu", [P, DI])
        sum_abs = sb("sum_abs", [P, TB])
        sum_ln = sb("sum_ln", [P, TB])
        sum_ua = sb("sum_ua", [P, TB])
        sum_dt = sb("sum_dt", [P, NT])
        dec_bx = sb("dec_bx", [P, 2, NT])
        dec_bxT = sb("dec_bxT", [NT, 2, P])
        rows = sb("rows", [B, 2, L])
        s_rows = sb("s_rows", [B, L])
        s_blk = sb("s_blk", [NT, P])
        s_tok = sb("s_tok", [P, NT])
        c_sum = sb("c_sum", [P, NT])
        cc = sb("cc", [P, NT, DS])
        csq = sb("csq", [P, NT, DS])
        c_var = sb("c_var", [P, NT])
        y_var = sb("y_var", [P, NT])
        y_rs = sb("y_rs", [P, NT])
        y_f = sb("y_f", [P, NT])
        yn = sb("yn", [P, NT, DS])
        yrep = sb("yrep", [P, TB, 8, DS])
        res = convs[:, :, :].rearrange("p a n -> p (a n)").rearrange("p (t d) -> p t d", t=TB)
        stats = sb("stats", [P, TB, 6])
        mv = sb("mv", [P, TB, 2])
        x_var = sb("x_var", [P, TB])
        x_rs = sb("x_rs", [P, TB])
        SUMU = TB * (DS + 2)

        consts = sem("consts")
        x_in = [sem(f"x_in{b}") for b in range(B)]
        prep = sem("prep")
        xs_full = sem("xs_full")
        xs_evac = sem("xs_evac")
        z_full = sem("z_full")
        z_evac = sem("z_evac")
        conv_done = sem("conv_done")
        xs_done = sem("xs_done")
        rank_done = sem("rank_done")
        lo_full = sem("lo_full")
        lo_done = sem("lo_done")
        small_done = sem("small_done")
        u_full = sem("u_full")
        u_free = sem("u_free")
        ln_done = sem("ln_done")
        dsum_done = sem("dsum_done")
        act_own = sem("act_own")
        dve_own = sem("dve_own")
        decay_done = sem("decay_done")
        bx_done = sem("bx_done")
        turned = sem("turned")
        turned_out = sem("turned_out")
        to_dram = sem("to_dram")
        rows_in = sem("rows_in")
        scanned = sem("scanned")
        s_dram = sem("s_dram")
        s_in = sem("s_in")
        s_turned = sem("s_turned")
        y_var_done = sem("y_var_done")
        y_rs_done = sem("y_rs_done")
        x_res = sem("x_res")

        mixed = T["mixed"]
        states = T["states"]

        with ExitStack() as pctx, nc.Block() as block:
            def ps(name):
                return pctx.enter_context(nc.psum_tensor("mx_" + name, [P, 512], F32))

            pA = [ps(f"pA{i}") for i in range(2)]
            pZ = [ps(f"pZ{i}") for i in range(2)]
            pU = [ps(f"pU{i}") for i in range(2)]
            pL = ps("pL")
            pS = ps("pS")

            @block.sync
            def _(sp):
                xT = W["xT"].rearrange("(k p) n -> p k n", p=P)
                sp.dma_start(w_in[:], W["W_in"].rearrange("(k p) n -> p k n", p=P)).then_inc(consts, 16)
                sp.dma_start(xin[:, :, 0:L], xT[:, :, 0:L]).then_inc(x_in[0], 16)
                for dst, src in ((w_conv[:], W["W_conv"].rearrange("(c p) a k -> p c (a k)", p=P)),
                                 (w_x[:], W["W_xproj"].rearrange("(c p) n -> p c n", p=P)),
                                 (w_dt[0:DTR, :], W["W_dt"]),
                                 (w_dt[DTR:DTR + 1, :], W["b_dt"].rearrange("(a n) -> a n", a=1)),
                                 (ident[:], W["ident"]),
                                 (ln_g[:], W["ln_g"]),
                                 (ln_b[:], W["ln_b"]),
                                 (w_out[:], W["W_out"].rearrange("(c p) n -> p c n", p=P))):
                    sp.dma_start(dst, src).then_inc(consts, 16)
                for b in range(1, B):
                    sp.dma_start(xin[:, :, b * L:(b + 1) * L], xT[:, :, b * L:(b + 1) * L]).then_inc(x_in[b], 16)
                sp.wait_ge(turned_out, 1)
                sp.dma_start(mixed.rearrange("a (q p) -> q a p", p=P), dec_bxT[:, :, :]).then_inc(to_dram, 16)
                sp.wait_ge(to_dram, 16)
                sp.dma_start(rows[:, :, :], mixed.rearrange("a (b l) -> b a l", b=B)).then_inc(rows_in, 16)
                sp.wait_ge(z_full, B * CI * G)
                sp.dma_start(x1[:, :, :], W["x"].rearrange("(t p) d -> p t d", p=P)).then_inc(x_res, 16)
                sp.wait_ge(scanned, 1)
                sp.dma_start(states.rearrange("(b l) -> b l", b=B), s_rows[:, :]).then_inc(s_dram, 16)
                sp.wait_ge(s_dram, 16)
                sp.dma_start(s_blk[:, :], states.rearrange("(q p) -> q p", p=P)).then_inc(s_in, 16)
                sp.wait_ge(x_res, 16)

            @block.tensor
            def _(pe):
                pe.sem_inc(rank_done, 1)
                pe.sem_inc(lo_full, 1)
                pe.wait_ge(consts, 16 * 9)
                pe.wait_ge(prep, 9)
                for b in range(B):
                    pe.wait_ge(x_in[b], 16)
                with pe.Fori(0, B) as b:
                    def proj(j, ring, full, evac, n):
                        m, g = j // G, j % G
                        pe.wait_ge(evac, b * 8 + n + 1)
                        for k in range(KD):
                            mm = pe.matmul(ring[n % 2][:, :], w_in[:, k, m * P:(m + 1) * P],
                                           xin[:, k, bass.ds(b * L + g * 512, 512)],
                                           start=k == 0, stop=k == KD - 1)
                        mm.then_inc(full, 1)

                    for j in range(8):
                        proj(j, pA, xs_full, xs_evac, j)
                    for j in range(2):
                        proj(8 + j, pZ, z_full, z_evac, j)
                    pe.wait_ge(xs_done, b * CI + 2 + CI)
                    for g in range(G):
                        pe.wait_ge(lo_done, b * G + g + 1)
                        for c in range(CI):
                            mm = pe.matmul(pL[0:DTR, :], w_x[:, c, 0:DTR], xs[:, c, g * 512:(g + 1) * 512],
                                           start=c == 0, stop=c == CI - 1)
                        mm.then_inc(lo_full, 1)
                        if g == 0:
                            pe.wait_ge(dsum_done, b + 1)
                            for t in range(TB):
                                for c in range(CI):
                                    mm = pe.matmul(pS[:, t * (DS + 2):(t + 1) * (DS + 2)],
                                                   xs[:, c, t * P:(t + 1) * P], w_small[:, c, :],
                                                   start=c == 0, stop=c == CI - 1)
                            mm.then_inc(rank_done, 1)
                    pe.wait_ge(lo_done, b * G + G + 1)
                    pe.wait_ge(small_done, b + 1)
                    for t in range(TB):
                        pe.wait_ge(u_free, b * TB + t + 1)
                        pe.matmul(pS[:, SUMU + t:SUMU + t + 1], dtl[:, t * P:(t + 1) * P], w_dtsum[:, :],
                                  start=True, stop=True)
                        pe.matmul(pU[t % 2][:, :], dtl[:, t * P:(t + 1) * P], w_dt[:, :],
                                  start=True, stop=True).then_inc(u_full, 1)
                        if t < 6:
                            proj(10 + t, pZ, z_full, z_evac, 2 + t)
                pe.wait_ge(decay_done, 1)
                pe.wait_ge(bx_done, 1)
                pe.wait_ge(small_done, B)
                pe.wait_ge(lo_done, B * G + 1)
                for a in range(2):
                    mm = pe.transpose(pL[0:NT, a * P:(a + 1) * P], dec_bx[:, a, :], ident[:, :])
                mm.then_inc(turned, 1)
                pe.wait_ge(s_in, 16)
                pe.wait_ge(turned_out, 1)
                pe.transpose(pL[:, 256:256 + NT], s_blk[:, :], ident[0:NT, 0:NT]).then_inc(s_turned, 1)

            @block.scalar
            def _(act):
                act.sem_inc(xs_evac, 2)
                act.sem_inc(xs_done, 2)
                act.sem_inc(u_free, 2)
                with act.Fori(0, B) as b:
                    def copy_xs(m):
                        act.wait_ge(conv_done, b * CI + m + 1)
                        for g in range(G):
                            act.wait_ge(xs_full, b * 8 + m * G + g + 1)
                            act.activation(xs_pad[m % 2][:, 1 + g * 512:1 + (g + 1) * 512],
                                           pA[g][:, :], ACT.Identity).then_inc(xs_evac, 1)

                    def silu_xs(m):
                        if m == 0:
                            act.wait_ge(lo_full, b * G + 1)
                            act.wait_ge(rank_done, b + 1)
                        act.wait_ge(conv_done, b * CI + 2 + m + 1)
                        act.activation(xs[:, m, :], conv[m % 2][:, :], ACT.Silu).then_inc(xs_done, 1)

                    copy_xs(0)
                    for m in range(1, CI):
                        copy_xs(m)
                        silu_xs(m - 1)
                    silu_xs(CI - 1)
                    act.wait_ge(dsum_done, b + 1)
                    hold(act, T)
                    act.preload_act_table_set("natural_log_exp_and_others")
                    own = Chain(act, act_own, b, TB)
                    for t in range(TB):
                        act.wait_ge(u_full, b * TB + t + 1)
                        act.activation(absu[:, :], pU[t % 2][:, :], ACT.Abs,
                                       accum_out=sum_abs[:, t:t + 1]).then_inc(u_free, 1)
                        act.wait_ge(u_free, b * TB + t + 1 + 2)
                        own.step(act.activation(expu[:, :], absu[:, :], ACT.Exp, scale=-1.0))
                        act.activation(lnu[:, :], expu[:, :], ACT.Ln, bias=1.0,
                                       accum_out=sum_ln[:, t:t + 1]).then_inc(ln_done, 1)
                        act.wait_ge(ln_done, b * TB + t + 1)
                    own.close()
                act.wait_ge(dsum_done, B + 1)
                act.activation(dec_bx[:, 0, :], sum_dt[:, :], ACT.Exp, scale=-1.0 / DI).then_inc(decay_done, 1)

            @block.vector
            def _(dve):
                dve.sem_inc(z_evac, 2)
                dve.sem_inc(conv_done, 2)
                dve.sem_inc(lo_done, 1)
                dve.sem_inc(dsum_done, 1)
                dve.wait_ge(consts, 16 * 9)
                for i in range(2):
                    dve.memset(xs_pad[i][:, 0:1], 0.0).then_inc(prep, 1)
                    dve.memset(xs_pad[i][:, L + 1:L + 2], 0.0).then_inc(prep, 1)
                dve.memset(dtl[DTR:DTR + 1, :], 1.0).then_inc(prep, 1)
                dve.memset(w_small[:, :, DS + 1:DS + 2], 1.0).then_inc(prep, 1)
                dve.tensor_copy(w_small[:, :, 0:DS], w_x[:, :, DTR + DS:DTR + 2 * DS]).then_inc(prep, 1)
                dve.tensor_reduce(w_small[:, :, DS], w_x[:, :, DTR:DTR + DS], AX.X, ALU.add).then_inc(prep, 1)
                dve.tensor_reduce(w_dtsum[:, 0:1], w_dt[:, :], AX.X, ALU.add).then_inc(prep, 1)
                dve.wait_ge(prep, 9)
                with dve.Fori(0, B) as b:
                    own = Chain(dve, dve_own, b, 2 * CI + 1)

                    def copy_z(n):
                        c, g = n // G, n % G
                        dve.wait_ge(z_full, b * 8 + n + 1)
                        hold(dve, T)
                        dve.tensor_copy(zs[:, c, bass.ds(b * L + g * 512, 512)], pZ[n % 2][:, :]).then_inc(z_evac, 1)

                    for m in range(CI):
                        pad, out = xs_pad[m % 2], conv[m % 2]
                        dve.wait_ge(xs_evac, b * 8 + 2 + (m + 1) * G)
                        dve.wait_ge(xs_done, b * CI + m + 1)
                        own.step(dve.tensor_scalar(out[:, :], pad[:, 1:L + 1], w_conv[:, m, 1:2], None, ALU.mult))
                        own.step(dve.scalar_tensor_tensor(out=out[:, :], in0=pad[:, 0:L], scalar=w_conv[:, m, 0:1],
                                                          in1=out[:, :], op0=ALU.mult, op1=ALU.add))
                        dve.scalar_tensor_tensor(out=out[:, :], in0=pad[:, 2:L + 2], scalar=w_conv[:, m, 2:3],
                                                 in1=out[:, :], op0=ALU.mult, op1=ALU.add).then_inc(conv_done, 1)
                    copy_z(0)
                    copy_z(1)
                    for g in range(G):
                        dve.wait_ge(lo_full, b * G + g + 2)
                        dve.tensor_copy(dtl[0:DTR, g * 512:(g + 1) * 512], pL[0:DTR, :]).then_inc(lo_done, 1)
                        if g == 0:
                            dve.wait_ge(rank_done, b + 2)
                            hold(dve, T)
                            dve.tensor_copy(small[:, bass.ds(b * TB, TB), :],
                                            pS[:, 0:SUMU].rearrange("p (t c) -> p t c", t=TB)).then_inc(small_done, 1)
                    for n in range(2, 8):
                        copy_z(n)
                    dve.wait_ge(u_full, b * TB + TB)
                    dve.wait_ge(ln_done, b * TB + TB)
                    own.step(dve.tensor_tensor(sum_ua[:, :], pS[:, SUMU:SUMU + TB], sum_abs[:, :], ALU.add))
                    dve.scalar_tensor_tensor(out=sum_dt[:, bass.ds(b * TB, TB)], in0=sum_ua[:, :], scalar=0.5,
                                             in1=sum_ln[:, :], op0=ALU.mult, op1=ALU.add).then_inc(dsum_done, 1)
                    own.close()
                own = Chain(dve, dve_own, B, 2 * CI + 1)
                dve.wait_ge(small_done, B)
                dve.scalar_tensor_tensor(out=dec_bx[:, 1, :], in0=small[:, :, DS], scalar=1.0 / DI,
                                         in1=small[:, :, DS + 1], op0=ALU.mult, op1=ALU.mult).then_inc(bx_done, 1)
                own.step(dve.tensor_reduce(c_sum[:, :], small[:, :, 0:DS], AX.X, ALU.add))
                own.step(dve.scalar_tensor_tensor(out=cc[:, :, :], in0=c_sum[:, :].unsqueeze(2).broadcast_to([P, NT, DS]),
                                                  scalar=-1.0 / DS, in1=small[:, :, 0:DS],
                                                  op0=ALU.mult, op1=ALU.add))
                own.step(dve.tensor_tensor(csq[:, :, :], cc[:, :, :], cc[:, :, :], ALU.mult))
                own.step(dve.tensor_reduce(c_var[:, :], csq[:, :, :], AX.X, ALU.add))
                dve.wait_ge(turned, 1)
                dve.tensor_copy(dec_bxT[:, :, :], pL[0:NT, 0:2 * P].rearrange("q (a p) -> q a p", a=2)).then_inc(turned_out, 1)
                dve.wait_ge(rows_in, 16)
                dve.tensor_tensor_scan(s_rows[:, :], rows[:, 0, :], rows[:, 1, :], 0.0,
                                       ALU.mult, ALU.add).then_inc(scanned, 1)
                dve.wait_ge(s_turned, 1)
                own.step(dve.tensor_copy(s_tok[:, :], pL[:, 256:256 + NT]))
                own.step(dve.tensor_tensor(y_var[:, :], s_tok[:, :], s_tok[:, :], ALU.mult))
                own.step(dve.tensor_tensor(y_var[:, :], y_var[:, :], c_var[:, :], ALU.mult))
                dve.tensor_scalar(y_var[:, :], y_var[:, :], 1.0 / DS, EPS, ALU.mult, ALU.add).then_inc(y_var_done, 1)
                dve.wait_ge(y_rs_done, 1)
                own.step(dve.tensor_tensor(y_f[:, :], s_tok[:, :], y_rs[:, :], ALU.mult))
                own.step(dve.tensor_tensor(yn[:, :, :], cc[:, :, :],
                                           y_f[:, :].unsqueeze(2).broadcast_to([P, NT, DS]), ALU.mult))

            @block.gpsimd
            def _(pool):
                pool.wait_ge(y_var_done, 1)
                pool.tensor_tensor(y_rs[:, :], y_var[:, :], T["half"][:, 0:NT], ALU.pow).then_inc(y_rs_done, 1)

        mixer_out(nc, T, ctx, sem, x1, ident, zs, zsil, yz, yn, yrep, w_out, ln_g, ln_b,
                  res, stats, mv, x_var, x_rs)


def steps(eng, n, depth, unroll, body):
    first = -(-depth // unroll)
    loops = n // unroll - first
    for s in range(first * unroll):
        body(s, s // unroll, s % unroll, lambda k: 0 <= s - k < n)
    with eng.Fori(first, first + loops) as h:
        for q in range(unroll):
            body(h * unroll + q, h, q, lambda k: True)
    for s in range((first + loops) * unroll, n + depth):
        body(s, s // unroll, s % unroll, lambda k: 0 <= s - k < n)


GT = 4
NG = NT // GT


def mixer_out(nc, T, ctx, sem, x1, ident, zs, zsil, yz, yn, yrep, w_out, ln_g, ln_b, res, stats, mv, x_var, x_rs):
    yrep_done = sem("yrep_done")
    y_turned = sem("y_turned")
    y_scaled = sem("y_scaled")
    z_silu = sem("z_silu")
    yz_done = sem("yz_done")
    o_full = sem("o_full")
    o_evac = sem("o_evac")
    x_var_done = sem("x_var_done")
    x_rs_done = sem("x_rs_done")
    x1_done = sem("x1_done")
    x1_stored = sem("x1_stored")
    own_sem = sem("own2")
    GW = GT * P
    with ExitStack() as pctx, nc.Block() as block:
        pY = [pctx.enter_context(nc.psum_tensor(f"mx_pY{i}", [P, 512], F32)) for i in range(2)]
        pO = [pctx.enter_context(nc.psum_tensor(f"mx_pO{i}", [P, 512], F32)) for i in range(2)]

        @block.tensor
        def _(pe):
            pe.sem_inc(y_turned, 2)
            pe.sem_inc(o_full, 2 * GT)

            def body(s, h, q, on):
                if on(0):
                    pe.wait_ge(yrep_done, s + 1)
                    pe.wait_ge(y_scaled, (s + 1) * CI)
                    for t in range(GT):
                        mm = pe.transpose(pY[q][:, t * P:(t + 1) * P],
                                          yrep[:, q * GT + t, :, :].rearrange("p a s -> p (a s)"), ident[:, :])
                    mm.then_inc(y_turned, 1)
                if on(2):
                    g = s - 2
                    pe.wait_ge(yz_done, g + 3)
                    for t in range(GT):
                        pe.wait_ge(o_evac, g * GT + t + 1)
                        for c in range(CI):
                            mm = pe.matmul(pO[t % 2][:, 0:D], yz[:, c, q * GW + t * P:q * GW + (t + 1) * P], w_out[:, c, :],
                                           start=c == 0, stop=c == CI - 1)
                        mm.then_inc(o_full, 1)
            steps(pe, NG, 3, 2, body)

        @block.scalar
        def _(act):
            act.sem_inc(y_scaled, 2 * CI)

            def body(s, h, q, on):
                if on(0):
                    act.wait_ge(yz_done, s + 1)
                    hold(act, T)
                    act.activation(zsil[:, :, q * GW:(q + 1) * GW], zs[:, :, bass.ds(s * GW, GW)],
                                   ACT.Silu).then_inc(z_silu, 1)
                if on(1):
                    g, r = s - 1, (q - 1) % 2
                    act.wait_ge(y_turned, g + 3)
                    act.wait_ge(o_full, (g + 1) * GT)
                    for c in range(CI):
                        act.activation(yz[:, c, r * GW:(r + 1) * GW], pY[r][:, :], ACT.Identity,
                                       scale=ln_g[:, c:c + 1], bias=ln_b[:, c:c + 1]).then_inc(y_scaled, 1)
            steps(act, NG, 3, 2, body)

        @block.vector
        def _(dve):
            dve.sem_inc(o_evac, 2)
            dve.sem_inc(yz_done, 2)
            dve.sem_inc(x1_done, 2 * GT)

            def body(s, h, q, on):
                def gate():
                    g, r = s - 1, (q - 1) % 2
                    dve.wait_ge(z_silu, g + 1)
                    dve.wait_ge(y_scaled, (g + 3) * CI)
                    half = slice(r * GW, (r + 1) * GW)
                    dve.tensor_tensor(yz[:, :, half], yz[:, :, half], zsil[:, :, half], ALU.mult).then_inc(yz_done, 1)

                if on(1) and not on(2):
                    gate()
                if on(2):
                    g = s - 2
                    own = Chain(dve, own_sem, g, 2 * GT)
                    dve.wait_ge(x1_done, (g + 1) * GT)
                    for t in range(GT):
                        dve.wait_ge(o_full, (g + 2) * GT + t + 1)
                        dve.tensor_tensor(res[:, q * GT + t, :], pO[t % 2][:, 0:D],
                                          x1[:, bass.ds(g * GT + t, 1), :].rearrange("p a d -> p (a d)"),
                                          ALU.add).then_inc(o_evac, 1)
                        if t > 0:
                            dve.wait_ge(o_evac, g * GT + 2 + t)
                            own.mark(dve.bn_stats(stats[:, q * GT + t - 1, :], res[:, q * GT + t - 1, :]))
                        if t == 1 and on(1):
                            gate()
                    dve.wait_ge(o_evac, g * GT + 2 + GT)
                    own.mark(dve.bn_stats(stats[:, q * GT + GT - 1, :], res[:, q * GT + GT - 1, :]))
                    own.settle()
                    hold(dve, T)
                    for t in range(GT):
                        own.mark(dve.bn_aggr(mv[:, q * GT + t, :], stats[:, q * GT + t, :]))
                    own.settle()
                    dve.tensor_scalar(x_var[:, q * GT:(q + 1) * GT], mv[:, q * GT:(q + 1) * GT, 1], EPS, None,
                                      ALU.add).then_inc(x_var_done, 1)
                    own.close()
                if on(3):
                    g, r = s - 3, (q - 3) % 2
                    dve.wait_ge(x_rs_done, g + 1)
                    for t in range(GT):
                        i = r * GT + t
                        dve.tensor_scalar(x1[:, bass.ds(g * GT + t, 1), :].rearrange("p a d -> p (a d)"),
                                          res[:, i, :], mv[:, i, 0:1], x_rs[:, i:i + 1],
                                          ALU.subtract, ALU.mult).then_inc(x1_done, 1)
            steps(dve, NG, 3, 2, body)
            dve.wait_ge(x1_done, (NG + 2) * GT)

        @block.gpsimd
        def _(pool):
            def body(s, h, q, on):
                if on(0):
                    pool.wait_ge(y_turned, s + 1)
                    hold(pool, T)
                    pool.tensor_copy(yrep[:, q * GT:(q + 1) * GT, :, :],
                                     yn[:, bass.ds(s * GT, GT), :].unsqueeze(2).broadcast_to([P, GT, 8, DS])
                                     ).then_inc(yrep_done, 1)
                if on(3):
                    g, r = s - 3, (q - 3) % 2
                    pool.wait_ge(x_var_done, g + 1)
                    pool.tensor_tensor(x_rs[:, r * GT:(r + 1) * GT], x_var[:, r * GT:(r + 1) * GT], T["half"][:, 0:GT],
                                       ALU.pow).then_inc(x_rs_done, 1)
            steps(pool, NG, 3, 2, body)

        @block.sync
        def _(sp):
            def body(s, h, q, on):
                sp.wait_ge(x1_done, (s + 3) * GT)
                sp.dma_start(T["x1_d"].rearrange("(t p) d -> p t d", p=P)[:, bass.ds(s * GT, GT), :],
                             x1[:, bass.ds(s * GT, GT), :]).then_inc(x1_stored, 16)
            steps(sp, NG, 0, 2, body)
            sp.wait_ge(x1_stored, 16 * NG)


E_ = 16
IN0 = 128
MID_ID = N // 2


class Experts:

    def __init__(self, eng, T, n):
        self.eng, self.words, self.n, self.loaded = eng, T["tile_exp"], n // 4, {}

    def load(self, h, i):
        if not isinstance(h, int) or 0 <= 2 * h + i < self.n:
            self.loaded[i] = self.eng.value_load(self.words[0:1, bass.ds(h * 2 + i, 1)], min_val=0, max_val=65535)

    def before(self, h, q):
        if q == 0:
            self.load(h, -1)

    def after(self, h, q):
        if q in (0, 3):
            self.load(h, q // 3)

    def of(self, q, k):
        return (self.loaded[(q - k) // 4] >> (4 * ((q - k) % 4))) & (E_ - 1)


class Sems:

    def __init__(self, nc, ctx, prefix):
        self.make = lambda name: ctx.enter_context(nc.semaphore(prefix + name))
        self.made = {}

    def __call__(self, name):
        if name not in self.made:
            self.made[name] = self.make(name)
        return self.made[name]


def experts0(nc, T, routed, n, pre):
    with ExitStack() as ctx:
        S = Sems(nc, ctx, pre)
        sb = lambda name, shape, dt=F32: ctx.enter_context(nc.sbuf_tensor(pre + name, shape, dt))
        xT = [sb(f"xT{i}", [P, KD, P]) for i in range(2)]
        sg = [sb(f"sg{i}", [P, IN0]) for i in range(2)]
        hh = [sb(f"hh{i}", [P, IN0]) for i in range(2)]
        hT = [sb(f"hT{i}", [P, P]) for i in range(2)]
        xg = [sb(f"xg{i}", [P, D]) for i in range(8)]
        if routed:
            ix = [sb(f"ix{i}", [P, 4], I32) for i in range(2)]
            yo = [sb(f"yo{i}", [P, D]) for i in range(2)]
        x1, ident = T["x1"], T["ident"]
        w13, w2, w_in, w_n = (T[k + ("0" if routed else "s")] for k in ("w13", "w2", "w_in", "w_n"))
        xT_full, xT_done = S("xT_full"), S("xT_done")
        h_full, sg_done, hh_done = S("h_full"), S("sg_done"), S("hh_done")
        ht_full, ht_done = S("ht_full"), S("ht_done")
        y_full, y_done = S("y_full"), S("y_done")
        x_in = [S(f"x_in{i}") for i in range(8)]
        y_stored = [S(f"y_stored{i}") for i in range(2)]
        ix_done = S("ix_done")

        with ExitStack() as pctx, nc.Block() as block:
            pX, pH, pHT, pY = ([pctx.enter_context(nc.psum_tensor(f"{pre}{nm}{i}", [P, 512], F32))
                                for i in range(2)] for nm in ("pX", "pH", "pHT", "pY"))

            @block.gpsimd
            def _(pool):
                def body(s, h, q, on):
                    if not routed:
                        pool.wait_ge(xT_full, s + 1)
                        hold(pool, T)
                        pool.tensor_copy(xg[q][:, :],
                                         x1[:, bass.ds(s, 1), :].rearrange("p a d -> p (a d)")).then_inc(x_in[q], 16)
                        return
                    if q % 4 == 0:
                        pool.wait_ge(xT_full, s + 4)
                        hold(pool, T)
                        pool.tensor_copy(ix[q // 4][:, :], T["slot_tok"][:, bass.ds(s, 4)]).then_inc(ix_done, 1)
                        pool.wait_ge(ix_done, h * 2 + q // 4 + 1)
                        hold(pool, T)
                    pool.indirect_dma_start(xg[q][:, :], None, T["x1_d"],
                                            bass.IndirectOffsetOnAxis(ap=ix[q // 4][:, q % 4:q % 4 + 1], axis=0)).then_inc(x_in[q], 16)
                steps(pool, n, 0, 8, body)

            if routed:
                @block.sync
                def _(sp):
                    def body(s, h, q, on):
                        sp.wait_ge(y_done, s + 3)
                        sp.dma_start(T["y_d"][bass.ds(s * P, P), :], yo[q % 2][:, :]).then_inc(y_stored[q % 2], 16)
                    steps(sp, n, 0, 4, body)
                    for i in range(2):
                        sp.wait_ge(y_stored[i], 16 * (n // 2 + 1))

            @block.tensor
            def _(pe):
                pe.sem_inc(xT_full, 8)
                pe.sem_inc(h_full, 2)
                pe.sem_inc(ht_full, 2)
                pe.sem_inc(y_full, 2)
                pe.wait_ge(w_in, w_n)
                experts = Experts(pe, T, n)

                def body(s, h, q, on):
                    if on(0):
                        t = s
                        pe.wait_ge(x_in[q], (h + 1) * 16)
                        pe.wait_ge(xT_done, t + 1)
                        for k in range(KD):
                            mm = pe.transpose(pX[q % 2][:, k * P:(k + 1) * P], xg[q][:, k * P:(k + 1) * P],
                                              ident[:, :])
                        mm.then_inc(xT_full, 1)
                    if routed:
                        experts.before(h, q)
                    if on(1):
                        t, r = s - 1, (q - 1) % 2
                        if routed:
                            e = experts.of(q, 1)
                        pe.wait_ge(xT_done, t + 3)
                        pe.wait_ge(hh_done, t + 1)
                        for k in range(KD):
                            w = w13[:, bass.ds(e, 1), k, :].rearrange("p a n -> p (a n)") if routed else w13[:, k, :]
                            mm = pe.matmul(pH[r][:, 0:D], xT[r][:, k, :], w, start=k == 0, stop=k == KD - 1)
                        if not routed:
                            for k in range(KD):
                                mm = pe.matmul(pH[r][:, D:D + E_], xT[r][:, k, :], T["w_gate"][:, k, :],
                                               start=k == 0, stop=k == KD - 1)
                        mm.then_inc(h_full, 1)
                    if routed:
                        experts.after(h, q)
                    if on(2):
                        t, r = s - 2, q % 2
                        pe.wait_ge(hh_done, t + 3)
                        pe.wait_ge(ht_done, t + 1)
                        pe.transpose(pHT[r][:, 0:P], hh[r][:, :], ident[:, :]).then_inc(ht_full, 1)
                    if on(3):
                        t, r = s - 3, (q - 3) % 2
                        if routed:
                            e = experts.of(q, 3)
                        pe.wait_ge(ht_done, t + 3)
                        pe.wait_ge(y_done, t + 1)
                        w = w2[:, bass.ds(e, 1), :].rearrange("p a n -> p (a n)") if routed else w2[:, :]
                        pe.matmul(pY[r][:, 0:D], hT[r][:, :], w, start=True, stop=True).then_inc(y_full, 1)
                steps(pe, n, 3, 8, body)

            @block.scalar
            def _(act):
                act.sem_inc(sg_done, 2)
                act.sem_inc(ht_done, 2)
                if routed:
                    act.sem_inc(y_done, 2)
                    for i in range(2):
                        act.sem_inc(y_stored[i], 16)

                def body(s, h, q, on):
                    if on(1):
                        t, r = s - 1, (q - 1) % 2
                        act.wait_ge(h_full, t + 3)
                        act.wait_ge(hh_done, t + 1)
                        act.activation(sg[r][:, :], pH[r][:, 0:IN0], ACT.Silu).then_inc(sg_done, 1)
                    if on(2):
                        t, r = s - 2, q % 2
                        act.wait_ge(ht_full, t + 3)
                        act.wait_ge(y_full, t + 1)
                        act.activation(hT[r][:, :], pHT[r][:, 0:P], ACT.Identity).then_inc(ht_done, 1)
                    if on(3) and routed:
                        t, r = s - 3, (q - 3) % 2
                        act.wait_ge(y_full, t + 3)
                        act.wait_ge(y_stored[r], (h * 2 + (q - 3) // 2 + 1) * 16)
                        act.activation(yo[r][:, :], pY[r][:, 0:D], ACT.Identity).then_inc(y_done, 1)
                steps(act, n, 3, 4, body)

            @block.vector
            def _(dve):
                dve.sem_inc(xT_done, 2)
                dve.sem_inc(hh_done, 2)
                if not routed:
                    dve.sem_inc(y_done, 2)

                def body(s, h, q, on):
                    if on(0):
                        t, r = s, q % 2
                        dve.wait_ge(xT_full, t + 9)
                        dve.wait_ge(h_full, t + 1)
                        dve.tensor_copy(xT[r][:, :, :].rearrange("p k n -> p (k n)"),
                                        pX[r][:, 0:D]).then_inc(xT_done, 1)
                    if on(1):
                        t, r = s - 1, (q - 1) % 2
                        if not routed:
                            dve.wait_ge(h_full, t + 3)
                            dve.wait_ge(sg_done, t + 3)
                            hold(dve, T)
                            dve.tensor_copy(T["logits"][:, bass.ds(t, 1), :].rearrange("p a e -> p (a e)"),
                                            pH[r][:, D:D + E_]).then_inc(S("lg_done"), 1)
                        dve.wait_ge(sg_done, t + 3)
                        dve.wait_ge(ht_full, t + 1)
                        dve.tensor_tensor(hh[r][:, :], sg[r][:, :], pH[r][:, IN0:2 * IN0], ALU.mult).then_inc(hh_done, 1)
                    if on(3) and not routed:
                        t, r = s - 3, (q - 3) % 2
                        dve.wait_ge(y_full, t + 3)
                        xt = x1[:, bass.ds(t, 1), :].rearrange("p a d -> p (a d)")
                        dve.tensor_tensor(xt, pY[r][:, 0:D], xt, ALU.add).then_inc(y_done, 1)
                steps(dve, n, 3, 4, body)
                if not routed:
                    dve.wait_ge(S("lg_done"), n)
                    dve.wait_ge(y_done, n + 2)


def dispatch(nc, T, K, n_tiles, sigmoid, tok_id, pre):
    with ExitStack() as ctx:
        sb = lambda name, shape, dt=F32: ctx.enter_context(nc.sbuf_tensor(pre + name, shape, dt))
        sem = lambda name: ctx.enter_context(nc.semaphore(pre + name))
        TE = [P, NT, E_]
        score = sb("score", TE)
        work = sb("work", TE)
        cand = sb("cand", TE)
        oh = [sb(f"oh{k}", TE) for k in range(K)]
        top = sb("top", [P, NT])
        wsum = sb("wsum", [P, NT])
        mask = sb("mask", TE, F16)
        tot = sb("tot", [P, E_, NT])
        incl = sb("incl", [P, E_, NT])
        excl = sb("excl", [P, E_, NT])
        ones = sb("ones", [P, E_ * NT])
        cnt = sb("cnt", [P, E_])
        full = sb("full", [P, E_, NT])
        ntile = sb("ntile", [P, E_])
        tile_end = sb("tile_end", [P, E_])
        base = sb("base", [P, E_])
        place = sb("place", TE)
        pos = sb("pos", [P, NT, K])
        pos_lo = sb("pos_lo", [P, NT, K], I32)
        pos_hi = sb("pos_hi", [P, NT, K], I32)
        lo = sb("lo", [P, NT, K])
        hi = sb("hi", [P, NT, K])
        before = sb("before", [P, n_tiles, E_])
        texp = sb("texp", [P, n_tiles])
        word = sb("word", [1, n_tiles // 4])
        oh_lo = [sb(f"oh_lo{k}", [P, P], F16) for k in range(K)]
        oh_hi = [sb(f"oh_hi{k}", [P, n_tiles], F16) for k in range(K)]
        c32, c16 = T["c32"], T["c16"]
        rev, thr, iota = c32["rev"], c32["thr"], c32["iota"]
        io_lo, io_hi, tri, one16 = c16["iota"], c16["iota"], c16["tri"], c16["ones"]
        slot_w = T["slot_w"]

        dve_own, sig, mask_done, counted = sem("dve_own"), sem("sig"), sem("mask_done"), sem("counted")
        cent_done, exp_done = sem("cent_done"), sem("exp_done")
        oh_done, oh_used, inv_done = sem("oh_done"), sem("oh_used"), sem("inv_done")

        bcE = lambda ap: ap.unsqueeze(2).broadcast_to(TE)
        bcT = lambda ap: ap.unsqueeze(1).broadcast_to(TE)

        with ExitStack() as pctx, nc.Block() as block:
            pW, pN, pI = (pctx.enter_context(nc.psum_tensor(pre + nm, [P, 512], F32)) for nm in ("pW", "pN", "pI"))

            @block.scalar
            def _(act):
                if sigmoid:
                    act.activation(score[:, :, :], T["logits"][:, :, :], ACT.Sigmoid).then_inc(exp_done, 1)
                else:
                    act.wait_ge(cent_done, 1)
                    act.activation(work[:, :, :], cand[:, :, :], ACT.Exp).then_inc(exp_done, 1)

            @block.vector
            def _(dve):
                own = Chain(dve, dve_own)
                tt = lambda out, a, b, op: own.step(dve.tensor_tensor(out, a, b, op))
                if sigmoid:
                    dve.wait_ge(exp_done, 1)
                    tt(work[:, :, :], score[:, :, :], bcT(T["route_b"][:, :]), ALU.add)
                else:
                    lg = T["logits"]
                    tt(lg[:, :, :], lg[:, :, :], bcT(T["route_b"][:, :]), ALU.add)
                    own.step(dve.tensor_reduce(top[:, :], lg[:, :, :], AX.X, ALU.max))
                    dve.tensor_tensor(cand[:, :, :], lg[:, :, :], bcE(top[:, :]), ALU.subtract).then_inc(cent_done, 1)
                    dve.wait_ge(exp_done, 1)
                    own.step(dve.tensor_reduce(wsum[:, :], work[:, :, :], AX.X, ALU.add))
                    own.step(dve.reciprocal(wsum[:, :], wsum[:, :]))
                    tt(score[:, :, :], work[:, :, :], bcE(wsum[:, :]), ALU.mult)
                    own.step(dve.tensor_copy(work[:, :, :], score[:, :, :]))
                for k in range(K):
                    own.step(dve.tensor_reduce(top[:, :], work[:, :, :], AX.X, ALU.max))
                    tt(cand[:, :, :], work[:, :, :], bcE(top[:, :]), ALU.is_equal)
                    tt(cand[:, :, :], cand[:, :, :], bcT(rev), ALU.mult)
                    own.step(dve.tensor_reduce(top[:, :], cand[:, :, :], AX.X, ALU.max))
                    tt(oh[k][:, :, :], bcT(rev), bcE(top[:, :]), ALU.is_equal)
                    if k < K - 1:
                        own.step(dve.scalar_tensor_tensor(out=work[:, :, :], in0=oh[k][:, :, :], scalar=-1e30,
                                                          in1=work[:, :, :], op0=ALU.mult, op1=ALU.add))
                for k in range(1, K):
                    src = oh[0] if k <= 1 else cand
                    if k == K - 1:
                        dve.tensor_tensor(mask[:, :, :], src[:, :, :], oh[k][:, :, :], ALU.add).then_inc(mask_done, 1)
                    else:
                        tt(cand[:, :, :], src[:, :, :], oh[k][:, :, :], ALU.add)
                dve.wait_ge(mask_done, 1)
                for k in range(K):
                    tt(cand[:, :, :], oh[k][:, :, :], score[:, :, :], ALU.mult)
                    own.step(dve.tensor_reduce(slot_w[:, :, k], cand[:, :, :], AX.X, ALU.add))
                own.step(dve.tensor_reduce(wsum[:, :], slot_w[:, :, 0:K], AX.X, ALU.add))
                if not sigmoid:
                    own.step(dve.tensor_scalar(wsum[:, :], wsum[:, :], 1e-9, None, ALU.max))
                own.step(dve.reciprocal(wsum[:, :], wsum[:, :]))
                if sigmoid:
                    own.step(dve.tensor_scalar(wsum[:, :], wsum[:, :], 2.5, None, ALU.mult))
                tt(slot_w[:, :, 0:K], slot_w[:, :, 0:K], wsum[:, :].unsqueeze(2).broadcast_to([P, NT, K]), ALU.mult)
                own.step(dve.memset(ones[:, :], 1.0))
                dve.wait_ge(counted, 1)
                own.step(dve.tensor_copy(tot[:, :, :], pN[:, :].rearrange("p (t e) -> p e t", e=E_)))
                own.step(dve.tensor_tensor_scan(incl[:, :, :].rearrange("p e t -> p (e t)"), ones[:, :],
                                                tot[:, :, :].rearrange("p e t -> p (e t)"), 0.0, ALU.mult, ALU.add))
                tt(excl[:, :, :], incl[:, :, :], tot[:, :, :], ALU.subtract)
                tt(cnt[:, :], incl[:, :, NT - 1], excl[:, :, 0], ALU.subtract)
                tt(full[:, :, :], cnt[:, :].unsqueeze(2).broadcast_to([P, E_, NT]),
                   thr.unsqueeze(1).broadcast_to([P, E_, NT]), ALU.is_gt)
                own.step(dve.tensor_reduce(ntile[:, :], full[:, :, :], AX.X, ALU.add))
                own.step(dve.tensor_tensor_scan(tile_end[:, :], ones[:, 0:E_], ntile[:, :], 0.0, ALU.mult, ALU.add))
                tt(before[:, :, :], iota[:, 0:n_tiles].unsqueeze(2).broadcast_to([P, n_tiles, E_]),
                   tile_end[:, :].unsqueeze(1).broadcast_to([P, n_tiles, E_]), ALU.is_ge)
                own.step(dve.tensor_reduce(texp[:, :], before[:, :, :], AX.X, ALU.add))
                own.step(dve.tensor_scalar(texp[:, :], texp[:, :], float(E_ - 1), None, ALU.min))
                four = texp[0:1, :].rearrange("p (n j) -> p n j", j=4)
                for j, out in ((2, word[:, :]), (1, word[:, :]), (0, T["tile_exp"][:, 0:n_tiles // 4])):
                    own.step(dve.scalar_tensor_tensor(out=out, in0=four[:, :, 3] if j == 2 else word[:, :], scalar=float(E_),
                                                      in1=four[:, :, j], op0=ALU.mult, op1=ALU.add))
                tt(base[:, :], tile_end[:, :], ntile[:, :], ALU.subtract)
                own.step(dve.scalar_tensor_tensor(out=base[:, :], in0=base[:, :], scalar=float(P),
                                                  in1=excl[:, :, 0], op0=ALU.mult, op1=ALU.subtract))
                tt(place[:, :, :], excl[:, :, :].rearrange("p e t -> p t e"), bcT(base[:, :]), ALU.add)
                tt(place[:, :, :], place[:, :, :], pW[:, :].rearrange("p (t e) -> p t e", e=E_), ALU.add)
                for k in range(K):
                    tt(cand[:, :, :], oh[k][:, :, :], place[:, :, :], ALU.mult)
                    own.step(dve.tensor_reduce(pos[:, :, k], cand[:, :, :], AX.X, ALU.add))
                pi = T["slot_of"][:, :, 0:K]
                own.step(dve.tensor_copy(pi, pos[:, :, :]))
                own.step(dve.tensor_scalar(pos_lo[:, :, :], pi, P - 1, None, ALU.bitwise_and))
                own.step(dve.tensor_scalar(pos_hi[:, :, :], pi, 7, None, ALU.logical_shift_right))
                own.step(dve.tensor_copy(lo[:, :, :], pos_lo[:, :, :]))
                own.step(dve.tensor_copy(hi[:, :, :], pos_hi[:, :, :]))
                with dve.Fori(0, NT) as t:
                    for k in range(K):
                        dve.wait_ge(oh_used, t * K + k + 1)
                        dve.tensor_scalar(oh_lo[k][:, :], io_lo[:, 0:P],
                                          lo[:, bass.ds(t, 1), k:k + 1].rearrange("p a k -> p (a k)"), None,
                                          ALU.is_equal).then_inc(oh_done, 1)
                        dve.tensor_scalar(oh_hi[k][:, :], io_hi[:, 0:n_tiles],
                                          hi[:, bass.ds(t, 1), k:k + 1].rearrange("p a k -> p (a k)"),
                                          tok_id[:, bass.ds(t, 1)], ALU.is_equal, ALU.mult).then_inc(oh_done, 1)
                dve.wait_ge(inv_done, 1)
                own.step(dve.tensor_scalar(T["slot_tok"][:, 0:n_tiles], pI[:, 0:n_tiles], float(MID_ID), None, ALU.add))

            @block.tensor
            def _(pe):
                pe.sem_inc(oh_used, K)
                pe.wait_ge(mask_done, 1)
                m = mask[:, :, :].rearrange("p t e -> p (t e)")
                pe.matmul(pW[:, :], tri, m, start=True, stop=True)
                pe.matmul(pN[:, :], one16, m, start=True, stop=True).then_inc(counted, 1)

                def add(t, first, last):
                    for k in range(K):
                        pe.wait_ge(oh_done, (t * K + k + 1) * 2)
                        mm = pe.matmul(pI[:, 0:n_tiles], oh_lo[k][:, :], oh_hi[k][:, :],
                                       start=first and k == 0, stop=last and k == K - 1)
                        mm.then_inc(inv_done if last and k == K - 1 else oh_used, 1)
                add(0, True, False)
                with pe.Fori(1, NT - 1) as t:
                    add(t, False, False)
                add(NT - 1, False, True)


def combine(nc, T, K, acc, out_rows, transposed, pre):
    LAG = 7
    with ExitStack() as ctx:
        sb = lambda name, shape, dt=F32: ctx.enter_context(nc.sbuf_tensor(pre + name, shape, dt))
        S = Sems(nc, ctx, pre)
        ix = [sb(f"ix{i}", [P, 4, K], I32) for i in range(2)]
        yg = [sb(f"yg{i}", [P, K, D]) for i in range(4)]
        sm = [sb(f"sm{i}", [P, D]) for i in range(8)]
        st = [sb(f"st{i}", [P, 6]) for i in range(2)]
        mv = sb("mv", [P, 8, 2])
        var = [sb(f"var{i}", [P, 4]) for i in range(2)]
        rs = [sb(f"rs{i}", [P, 4]) for i in range(2)]
        xo = [sb(f"xo{i}", [P, D]) for i in range(4)]
        ident = T["ident"]
        own_sem, ix_done, summed = S("own"), S("ix_done"), S("summed")
        y_in = [S(f"y_in{i}") for i in range(4)]
        var_done, rs_done = S("var"), S("rs")
        xo_done, xo_turned, xT_done = S("xo"), S("turned"), S("xT")
        stored = [S(f"stored{i}") for i in range(4)]

        with ExitStack() as pctx, nc.Block() as block:
            pX = [pctx.enter_context(nc.psum_tensor(f"{pre}pX{i}", [P, 512], F32)) for i in range(2)]

            @block.gpsimd
            def _(pool):
                def body(s, h, q, on):
                    g = h * 2 + q // 4
                    if on(0):
                        if q % 4 == 0:
                            pool.wait_ge(summed, s)
                            hold(pool, T)
                            pool.tensor_copy(ix[q // 4][:, :, :], T["slot_of"][:, bass.ds(s, 4), 0:K]).then_inc(ix_done, 1)
                            pool.wait_ge(ix_done, g + 1)
                        pool.wait_ge(summed, s + 1)
                        hold(pool, T)
                        for k in range(K):
                            pool.indirect_dma_start(yg[q % 4][:, k, :], None, T["y_d"],
                                                    bass.IndirectOffsetOnAxis(ap=ix[q // 4][:, q % 4, k:k + 1], axis=0)
                                                    ).then_inc(y_in[q % 4], 16)
                    if q % 4 == 2 and on(4):
                        pool.wait_ge(var_done, g)
                        r = (q // 4 - 1) % 2
                        pool.tensor_tensor(rs[r][:, :], var[r][:, :], T["half"][:, 0:4], ALU.pow).then_inc(rs_done, 1)
                steps(pool, NT, LAG, 8, body)

            @block.vector
            def _(dve):
                dve.sem_inc(summed, 4)
                dve.sem_inc(xo_done, 8)

                def body(s, h, q, on):
                    own = Chain(dve, own_sem, s, K + 1)
                    if on(0):
                        dve.wait_ge(y_in[q % 4], (h * 2 + q // 4 + 1) * 16 * K)
                        dve.wait_ge(xo_done, s + 1)
                        src = acc[:, bass.ds(s, 1), :].rearrange("p a d -> p (a d)")
                        for k in range(K):
                            ins = dve.scalar_tensor_tensor(
                                out=sm[q][:, :], in0=yg[q % 4][:, k, :],
                                scalar=T["slot_w"][:, bass.ds(s, 1), k:k + 1].rearrange("p a k -> p (a k)"),
                                in1=src, op0=ALU.mult, op1=ALU.add)
                            src = sm[q][:, :]
                            if k < K - 1:
                                own.step(ins)
                            else:
                                ins.then_inc(summed, 1)
                        dve.wait_ge(summed, s + 5)
                        own.step(dve.bn_stats(st[q % 2][:, :], sm[q][:, :]))
                        hold(dve, T)
                        own.step(dve.bn_aggr(mv[:, q, :], st[q % 2][:, :]))
                        if q % 4 == 3:
                            g = q // 4
                            dve.tensor_scalar(var[g][:, :], mv[:, g * 4:g * 4 + 4, 1], EPS, None, ALU.add).then_inc(var_done, 1)
                    if on(LAG):
                        t, r, g = s - LAG, (q - LAG) % 8, (q - LAG) // 4
                        dve.wait_ge(rs_done, h * 2 + g + 1)
                        dve.wait_ge(stored[r % 4], (h * 2 + g + 1) * 16)
                        if transposed:
                            dve.wait_ge(xo_turned, t + 1)
                        dve.tensor_scalar(xo[r % 4][:, :], sm[r][:, :], mv[:, r, 0:1], rs[r // 4][:, r % 4:r % 4 + 1],
                                          ALU.subtract, ALU.mult).then_inc(xo_done, 1)
                steps(dve, NT, LAG, 8, body)

            @block.sync
            def _(sp):
                for i in range(4):
                    sp.sem_inc(stored[i], 16)

                def body(s, h, q, on):
                    sp.wait_ge(xo_done, s + 9)
                    sp.dma_start(out_rows(s), xo[q][:, :]).then_inc(stored[q], 16)
                steps(sp, NT, 0, 4, body)
                for i in range(4):
                    sp.wait_ge(stored[i], 16 * (NT // 4 + 1))

            if transposed:
                @block.tensor
                def _(pe):
                    pe.sem_inc(xo_turned, 4)

                    def body(s, h, q, on):
                        pe.wait_ge(xo_done, s + 9)
                        pe.wait_ge(xT_done, s + 1)
                        for k in range(KD):
                            mm = pe.transpose(pX[q % 2][:, k * P:(k + 1) * P], xo[q][:, k * P:(k + 1) * P], ident[:, :])
                        mm.then_inc(xo_turned, 1)
                    steps(pe, NT, 0, 4, body)

                @block.scalar
                def _(act):
                    act.sem_inc(xT_done, 2)

                    def body(s, h, q, on):
                        act.wait_ge(xo_turned, s + 5)
                        hold(act, T)
                        act.activation(T["x2T"][:, :, bass.ds(s * P, P)],
                                       pX[q % 2][:, 0:D].rearrange("p (k n) -> p k n", k=KD), ACT.Identity).then_inc(xT_done, 1)
                    steps(act, NT, 0, 4, body)
                    act.wait_ge(xT_done, NT + 2)


H, DH = 16, 16
BL = 32
SEG = 4
LOCAL = (1, 2, 3)
FAR = tuple(range(5))
N0 = 10
PAIRS0 = [(a, b) for a in range(SEG) for b in range(a + 1)]


def far_count(t, s, h):
    return sum(1 for x in range(L.bit_length() - 1)
               if t // 2 ** (x + 2) == s // 2 ** (x + 2) and t % 2 ** x == h % 2 ** x == s % 2 ** x)


def local_groups():
    out, first = [], 0
    for lv in LOCAL:
        r = 2 ** lv
        for rho in range(r):
            nh, ns = H // r, BL // (SEG * r)
            out.append((r, rho, nh, ns, first))
            first += ns * 4 * nh
    return out, first


GROUPS, NC = local_groups()


def far_groups():
    out, first = [], 0
    for lv in FAR:
        r = 2 ** lv
        ns = (L // H) // (SEG * r)
        out.append((r, ns, first))
        first += ns * 4
    return out, first


FGROUPS, NF = far_groups()
NJ = L // H


def count_tables():
    c0 = np.zeros((P, BL // SEG, N0, H), np.float32)
    cc = np.zeros((P, NC), np.float32)
    for p in range(L // BL):
        for s in range(BL // SEG):
            for n, (a, b) in enumerate(PAIRS0):
                for h in range(H):
                    t = BL * p + SEG * s
                    c0[p, s, n, h] = far_count(t + a, t + b, h)
        for r, rho, nh, ns, first in GROUPS:
            v = cc[p, first:first + ns * 4 * nh].reshape(ns, 2, 2, nh)
            for s in range(ns):
                for a in range(2):
                    for b in range(2):
                        for k in range(nh):
                            t = BL * p + s * SEG * r + rho
                            v[s, a, b, k] = far_count(t + (2 + a) * r, t + b * r, rho + r * k)
    for q in range(1, B):
        n = L // BL
        c0[q * n:(q + 1) * n], cc[q * n:(q + 1) * n] = c0[:n], cc[:n]
    cf = np.zeros((B * H, NF), np.float32)
    for h in range(H):
        for r, ns, first in FGROUPS:
            v = cf[h, first:first + ns * 4].reshape(ns, 2, 2)
            for s in range(ns):
                for a in range(2):
                    for b in range(2):
                        j = s * SEG * r
                        v[s, a, b] = far_count(H * (j + (2 + a) * r) + h, H * (j + b * r) + h, h)
    for q in range(1, B):
        cf[q * H:(q + 1) * H] = cf[:H]
    return c0.reshape(P, -1), cc, cf


def rope_tables():
    freq = (1.0 / np.float32(15000.0) ** (np.arange(0, D, 2, dtype=np.float32) / np.float32(D))).astype(np.float32)
    ang = np.arange(L, dtype=np.float32)[:, None] * freq[None, :]
    both = np.stack([np.cos(ang), np.sin(ang)], 1).astype(np.float32)
    return np.tile(both.reshape(L // BL, BL, 2, D // 2), (B, 1, 1, 1)).copy()


def project_qkv(nc, T, W):
    with ExitStack() as ctx:
        S = Sems(nc, ctx, "qkv_")
        sb = lambda name, shape, dt=F32: ctx.enter_context(nc.sbuf_tensor("qkv_" + name, shape, dt))
        w = sb("w", [P, KD, 3 * D])
        bias = sb("bias", [P, 3 * D])
        lhs = [sb(f"lhs{i}", [P, KD, P]) for i in range(2)]
        raw = [sb(f"raw{i}", [P, 2 * D]) for i in range(2)]
        tc_ = [sb(f"tc{i}", [P, 2 * D]) for i in range(2)]
        ts_ = [sb(f"ts{i}", [P, 2 * D]) for i in range(2)]
        x2T, qk, v, cs = T["x2T"], T["qk"], T["v"], T["rope"]
        w_in, lhs_done, qk_full, v_full = S("w_in"), S("lhs_done"), S("qk_full"), S("v_full")
        raw_done, v_done, tc_done, ts_done, rot0, rot_done = (S("raw_done"), S("v_done"), S("tc_done"),
                                                              S("ts_done"), S("rot0"), S("rot_done"))
        xv = x2T.rearrange("p k (b i) -> p k b i", i=BL)
        halves = lambda ap: ap.rearrange("p (a h n) -> p a h n", a=2, h=2)

        with ExitStack() as pctx, nc.Block() as block:
            pQ, pV = ([pctx.enter_context(nc.psum_tensor(f"qkv_{nm}{i}", [P, 512], F32)) for i in range(2)]
                      for nm in ("pQ", "pV"))

            @block.sync
            def _(sp):
                sp.dma_start(w[:, :, :], W["wqkvT"].rearrange("(k p) n -> p k n", p=P)).then_inc(w_in, 16)
                sp.dma_start(bias[:, :], W["bqkv"].partition_broadcast(P)).then_inc(w_in, 16)
                sp.wait_ge(w_in, 32)

            @block.scalar
            def _(act):
                def body(s, h, q, on):
                    if on(0):
                        act.wait_ge(v_full, s + 1)
                        hold(act, T)
                        act.activation(lhs[q][:, :, :], xv[:, :, :, bass.ds(s, 1)].rearrange("p k b i -> p k (b i)"),
                                       ACT.Identity).then_inc(lhs_done, 1)
                steps(act, BL, 2, 2, body)

            @block.tensor
            def _(pe):
                pe.sem_inc(qk_full, 2)
                pe.sem_inc(v_full, 2)
                pe.wait_ge(w_in, 32)

                def body(s, h, q, on):
                    if on(1):
                        t, r = s - 1, (q - 1) % 2
                        pe.wait_ge(lhs_done, t + 1)
                        pe.wait_ge(raw_done, t + 1)
                        for k in range(KD):
                            mm = pe.matmul(pQ[r][:, :], lhs[r][:, k, :], w[:, k, 0:2 * D], start=k == 0, stop=k == KD - 1)
                        mm.then_inc(qk_full, 1)
                        pe.wait_ge(v_done, t + 1)
                        for k in range(KD):
                            mm = pe.matmul(pV[r][:, 0:D], lhs[r][:, k, :], w[:, k, 2 * D:3 * D], start=k == 0, stop=k == KD - 1)
                        mm.then_inc(v_full, 1)
                steps(pe, BL, 2, 2, body)

            @block.gpsimd
            def _(pool):
                pool.sem_inc(ts_done, 2)
                pool.wait_ge(T["rope_in"], 16)

                def body(s, h, q, on):
                    if on(2):
                        t = s - 2
                        pool.wait_ge(raw_done, t + 3)
                        pool.wait_ge(rot_done, t + 1)
                        hold(pool, T)
                        x, o = halves(raw[q][:, :]), halves(ts_[q][:, :])
                        sin = cs[:, bass.ds(t, 1), 1, :].broadcast_to([P, 2, D // 2])
                        pool.tensor_tensor(o[:, :, 0, :], x[:, :, 1, :], sin, ALU.mult).then_inc(S("ts0"), 1)
                        pool.tensor_tensor(o[:, :, 1, :], x[:, :, 0, :], sin, ALU.mult).then_inc(ts_done, 1)
                        pool.wait_ge(S("ts0"), t + 1)
                        pool.wait_ge(ts_done, t + 3)
                steps(pool, BL, 2, 2, body)

            @block.vector
            def _(dve):
                dve.sem_inc(raw_done, 2)
                dve.sem_inc(v_done, 2)
                dve.sem_inc(rot0, 2)
                dve.sem_inc(rot_done, 2)
                dve.wait_ge(w_in, 32)
                dve.wait_ge(T["rope_in"], 16)

                def body(s, h, q, on):
                    if on(2):
                        t = s - 2
                        dve.wait_ge(qk_full, t + 3)
                        dve.wait_ge(rot0, t + 1)
                        dve.wait_ge(ts_done, t + 1)
                        dve.tensor_tensor(raw[q][:, :], pQ[q][:, :], bias[:, 0:2 * D], ALU.add).then_inc(raw_done, 1)
                        dve.wait_ge(v_full, t + 3)
                        dve.tensor_tensor(v[:, bass.ds(t, 1), :].rearrange("p a d -> p (a d)"), pV[q][:, 0:D],
                                          bias[:, 2 * D:3 * D], ALU.add).then_inc(v_done, 1)
                    if on(3):
                        t, q = s - 3, (q - 3) % 2
                        dve.wait_ge(raw_done, t + 3)
                        dve.wait_ge(rot_done, t + 1)
                        cos = cs[:, bass.ds(t, 1), 0, :].broadcast_to([P, 4, D // 2])
                        dve.tensor_tensor(tc_[q][:, :].rearrange("p (a n) -> p a n", a=4),
                                          raw[q][:, :].rearrange("p (a n) -> p a n", a=4), cos, ALU.mult).then_inc(rot0, 1)
                        dve.wait_ge(rot0, t + 3)
                        dve.wait_ge(ts_done, t + 3)
                        o = qk[:, bass.ds(t, 1), :].rearrange("p b (a h n) -> p (b a) h n", a=2, h=2)
                        c, x = halves(tc_[q][:, :]), halves(ts_[q][:, :])
                        dve.tensor_tensor(o[:, :, 0, :], c[:, :, 0, :], x[:, :, 0, :], ALU.subtract).then_inc(S("rot1"), 1)
                        dve.tensor_tensor(o[:, :, 1, :], c[:, :, 1, :], x[:, :, 1, :], ALU.add).then_inc(rot_done, 1)
                steps(dve, BL, 3, 2, body)
                dve.wait_ge(S("rot1"), BL)
                dve.wait_ge(v_done, BL + 2)
                dve.wait_ge(rot_done, BL + 2)


def attend(nc, T, W):
    with ExitStack() as ctx:
        sb = lambda name, shape, dt=F32: ctx.enter_context(nc.sbuf_tensor("at_" + name, shape, dt))
        sem = lambda name: ctx.enter_context(nc.semaphore("at_" + name))
        NS = BL // SEG
        HR = B * H
        qk, v = T["qk"], T["v"]
        cnt0 = sb("cnt0", [P, NS * N0 * H])
        cntc = sb("cntc", [P, NC])
        cntf = sb("cntf", [HR, NF])
        s0 = sb("s0", [P, NS, N0, H])
        sc = sb("sc", [P, NC])
        scx = sb("scx", [P, NC // 2])
        M = sb("M", [P, BL, H])
        Z = sb("Z", [P, BL, H])
        prod = [sb(f"prod{i}", [P, SEG * D]) for i in range(2)]
        mc = sb("mc", [P, NC // 2])
        far = T["far"]
        fq = T["fq"]
        fs = sb("fs", [HR, NF])
        fx = sb("fx", [HR, NF // 2])
        fm = sb("fm", [HR, NF // 2])
        fo = sb("fo", [HR, NJ, DH + 2])
        fb = sb("fb", [P, 2, H, DH + 2])
        fg = sb("fg", [P, 2, H])
        pc = T["prodc"]
        pf = T["prodf"][0:HR, :]
        o = T["o"]
        tabs, own_sem, pool_own = sem("tabs"), sem("own"), sem("pool_own")
        far_done, far_st, far_in, fo_done, fo_st, fb_in = (sem("far_done"), sem("far_st"), sem("far_in"),
                                                           sem("fo_done"), sem("fo_st"), sem("fb_in"))
        pc_done, pv_go, pv_done = sem("pc_done"), sem("pv_go"), sem("pv_done")
        e_req, e_done = sem("e_req"), sem("e_done")
        fq_, fk_, fv_ = (fq[:, :, i, :] for i in range(3))

        def rows_of(ap, r, rho, ns, nh, a):
            t0 = (2 + a) * r + rho
            return ap[:, t0:t0 + (ns - 1) * SEG * r + 1:SEG * r, rho:H:r]

        with nc.Block() as block:
            @block.sync
            def _(sp):
                for dst, src in ((cnt0[:, :], W["cnt0"]), (cntc[:, :], W["cntc"]), (cntf[:, :], W["cntf"])):
                    sp.dma_start(dst, src).then_inc(tabs, 16)
                sp.wait_ge(far_done, 6)
                sp.dma_start(T["far_d"].rearrange("p a h c d -> p (a h c d)"),
                             far[:, :, :, :, :].rearrange("p a h c d -> p (a h c d)")).then_inc(far_st, 16)
                sp.wait_ge(far_st, 16)
                src = T["far_d"].rearrange("(b n) a h c d -> b h n a (c d)", b=B)
                for b in range(B):
                    sp.dma_start(fq[b * H:(b + 1) * H, :, :, :].rearrange("h (n a) c d -> h n a (c d)", a=2),
                                 src[b]).then_inc(far_in, 16)
                sp.wait_ge(fo_done, 1)
                sp.dma_start(T["fo_d"].rearrange("h j c -> h (j c)"), fo[:, :, :].rearrange("h j c -> h (j c)")).then_inc(fo_st, 16)
                sp.wait_ge(fo_st, 16)
                back = T["fo_d"].rearrange("(b h) (n a) c -> b n a h c", b=B, a=2)
                n = L // BL
                for b in range(B):
                    for a in range(2):
                        sp.dma_start(fb[b * n:(b + 1) * n, a, :, :], back[b][:, a]).then_inc(fb_in, 16)
                sp.wait_ge(fb_in, 16 * B * 2)

            @block.scalar
            def _(act):
                act.wait_ge(e_req, 1)
                act.activation(fs[:, :], fs[:, :], ACT.Exp).then_inc(e_done, 1)
                act.wait_ge(e_req, 2)
                act.activation(s0[:, :, :, :], s0[:, :, :, :], ACT.Exp).then_inc(e_done, 1)
                act.activation(sc[:, :], sc[:, :], ACT.Exp).then_inc(e_done, 1)
                act.activation(fg[:, :, :], fg[:, :, :], ACT.Exp).then_inc(e_done, 1)

            qh = qk[:, :, 0:D].rearrange("p t (h d) -> p t h d", h=H)
            kh = qk[:, :, D:2 * D].rearrange("p t (h d) -> p t h d", h=H)
            vh = v[:, :, :].rearrange("p t (h d) -> p t h d", h=H)

            def key_rows(ap, r, rho, ns, b):
                t0 = b * r + rho
                return ap[:, t0:t0 + (ns - 1) * SEG * r + 1:SEG * r, rho:H:r]

            @block.gpsimd
            def _(pool):
                own = Chain(pool, pool_own)
                for a in range(2):
                    for c, src in enumerate((qk[:, :, 0:D], qk[:, :, D:2 * D], v[:, :, :])):
                        w = 2 * D if c < 2 else D
                        full = qk if c < 2 else v
                        flat = full[:, :, :].rearrange("p t n -> p (t n)")
                        off = a * H * w + (D if c == 1 else 0)
                        diag = flat[:, off:off + (H - 1) * (w + DH) + DH]
                        diag = bass.AP(diag.tensor, diag.offset, [diag.ap[0], [w + DH, H], [1, DH]])
                        pool.tensor_copy(far[:, a, :, c, :], diag).then_inc(far_done, 1)
                for r, rho, nh, ns, first in GROUPS:
                    out = pc[:, first * DH:(first + ns * 4 * nh) * DH].rearrange(
                        "p (s a b h d) -> p s a b h d", s=ns, a=2, b=2, h=nh)
                    for a in range(2):
                        for b in range(2):
                            pool.tensor_tensor(out[:, :, a, b, :, :], rows_of(qh, r, rho, ns, nh, a),
                                               key_rows(kh, r, rho, ns, b), ALU.mult).then_inc(pc_done, 1)
                pool.wait_ge(pc_done, 4 * len(GROUPS))
                pool.wait_ge(pv_go, 1)
                for r, rho, nh, ns, first in GROUPS:
                    out = pc[:, first * DH:(first + ns * 4 * nh) * DH].rearrange(
                        "p (s a b h d) -> p s a b h d", s=ns, a=2, b=2, h=nh)
                    wgt = sc[:, first:first + ns * 4 * nh].rearrange("p (s a b h) -> p s a b h", s=ns, a=2, b=2)
                    for a in range(2):
                        for b in range(2):
                            pool.tensor_tensor(out[:, :, a, b, :, :],
                                               wgt[:, :, a, b, :].unsqueeze(3).broadcast_to([P, ns, nh, DH]),
                                               key_rows(vh, r, rho, ns, b), ALU.mult).then_inc(pv_done, 1)

            @block.vector
            def _(dve):
                own = Chain(dve, own_sem)
                step = own.step
                tt = lambda out, a, b, op: step(dve.tensor_tensor(out, a, b, op))
                for s in range(NS):
                    for a in range(SEG):
                        n = (a + 1)
                        buf = prod[(s * SEG + a) % 2]
                        t = s * SEG
                        pr = buf[:, 0:n * D].rearrange("p (b x) -> p b x", b=n)
                        step(dve.tensor_tensor(pr, qk[:, t + a:t + a + 1, 0:D].broadcast_to([P, n, D]),
                                               qk[:, t:t + n, D:2 * D], ALU.mult))
                        own.mark(dve.tensor_reduce(s0[:, s, a * (a + 1) // 2:a * (a + 1) // 2 + n, :],
                                                   buf[:, 0:n * D].rearrange("p (b h d) -> p b h d", b=n, h=H),
                                                   AX.X, ALU.add))
                own.settle()
                dve.wait_ge(tabs, 48)
                s0f = s0[:, :, :, :].rearrange("p s n h -> p (s n h)")
                tt(s0f, s0f, cnt0[:, :], ALU.mult)
                dve.wait_ge(far_in, 16 * B)
                for r, ns, first in FGROUPS:
                    out = pf[:, first * DH:(first + ns * 4) * DH].rearrange("p (s a b d) -> p s a b d", s=ns, a=2, b=2)
                    for a in range(2):
                        qa = fq_[:, (2 + a) * r:(2 + a) * r + (ns - 1) * SEG * r + 1:SEG * r, :]
                        for b in range(2):
                            kb = fk_[:, b * r:b * r + (ns - 1) * SEG * r + 1:SEG * r, :]
                            own.mark(dve.tensor_tensor(out[:, :, a, b, :], qa, kb, ALU.mult))
                step(dve.memset(fo[:, :, DH:DH + 1], -1e30))
                step(dve.tensor_reduce(fs[:, :], pf[:, 0:NF * DH].rearrange("p (n d) -> p n d", d=DH), AX.X, ALU.add))
                tt(fs[:, :], fs[:, :], cntf[:, :], ALU.mult)
                step(dve.tensor_reduce(fx[:, :], fs[:, :].rearrange("p (n b) -> p n b", b=2), AX.X, ALU.max))

                def frows(c0, c1, r, ns):
                    return fo[:, :, c0:c1].rearrange("p (s q) c -> p s q c", q=SEG * r)[:, :, 2 * r:3 * r + 1:r, :]

                fxs = lambda buf, ns, first: buf[:, first // 2:(first + ns * 4) // 2].rearrange("p (s a c) -> p s a c", a=2, c=1)
                for r, ns, first in FGROUPS:
                    tt(frows(DH, DH + 1, r, ns), frows(DH, DH + 1, r, ns), fxs(fx, ns, first), ALU.max)
                for r, ns, first in FGROUPS:
                    own.mark(dve.tensor_copy(fxs(fm, ns, first), frows(DH, DH + 1, r, ns)))
                own.settle()
                dve.tensor_tensor(fs[:, :].rearrange("p (n b) -> p n b", b=2), fs[:, :].rearrange("p (n b) -> p n b", b=2),
                                  fm[:, :].unsqueeze(2).broadcast_to([HR, NF // 2, 2]), ALU.subtract).then_inc(e_req, 1)
                step(dve.memset(fo[:, :, 0:DH], 0.0))
                step(dve.memset(fo[:, :, DH + 1:DH + 2], 0.0))
                dve.wait_ge(e_done, 1)
                step(dve.tensor_reduce(fx[:, :], fs[:, :].rearrange("p (n b) -> p n b", b=2), AX.X, ALU.add))
                for r, ns, first in FGROUPS:
                    tt(frows(DH + 1, DH + 2, r, ns), frows(DH + 1, DH + 2, r, ns), fxs(fx, ns, first), ALU.add)
                for r, ns, first in FGROUPS:
                    out = pf[:, first * DH:(first + ns * 4) * DH].rearrange("p (s a b d) -> p s a b d", s=ns, a=2, b=2)
                    w = fs[:, first:first + ns * 4].rearrange("p (s a b) -> p s a b", a=2, b=2)
                    for a in range(2):
                        for b in range(2):
                            vb = fv_[:, b * r:b * r + (ns - 1) * SEG * r + 1:SEG * r, :]
                            own.mark(dve.tensor_tensor(out[:, :, a, b, :],
                                                       w[:, :, a, b].unsqueeze(2).broadcast_to([HR, ns, DH]), vb, ALU.mult))
                own.settle()
                pfh = pf[:, 0:NF * DH].rearrange("p (n b d) -> p n b d", b=2, d=DH)
                tt(pfh[:, :, 0, :], pfh[:, :, 0, :], pfh[:, :, 1, :], ALU.add)
                for i, (r, ns, first) in enumerate(FGROUPS):
                    part = pf[:, first * DH:(first + ns * 4) * DH].rearrange("p (s a b d) -> p s a b d", s=ns, a=2, b=2)
                    for a in range(2):
                        view = fo[:, :, 0:DH].rearrange("p (s q) c -> p s q c", q=SEG * r)[:, :, (2 + a) * r, :]
                        ins = dve.tensor_tensor(view, view, part[:, :, a, 0, :], ALU.add)
                        if i == len(FGROUPS) - 1 and a == 1:
                            ins.then_inc(fo_done, 1)
                        else:
                            step(ins)
                dve.wait_ge(pc_done, 4 * len(GROUPS))
                step(dve.tensor_reduce(sc[:, :], pc[:, 0:NC * DH].rearrange("p (n d) -> p n d", d=DH), AX.X, ALU.add))
                tt(sc[:, :], sc[:, :], cntc[:, :], ALU.mult)
                for a in range(SEG):
                    f = a * (a + 1) // 2
                    own.mark(dve.tensor_reduce(M[:, a:BL:SEG, :],
                                               s0[:, :, f:f + a + 1, :].rearrange("p s b h -> p s h b"), AX.X, ALU.max))
                own.settle()

                def parts(buf, r, rho, nh, ns, first):
                    return buf[:, first:first + ns * 4 * nh].rearrange("p (s a b h) -> p s a b h", s=ns, a=2, b=2)

                def halves(buf, r, rho, nh, ns, first):
                    return buf[:, first // 2:(first + ns * 4 * nh) // 2].rearrange("p (s a h) -> p s a h", s=ns, a=2)

                for g in GROUPS:
                    sp_ = parts(sc, *g)
                    hx = halves(scx, *g)
                    for a in range(2):
                        own.mark(dve.tensor_tensor(hx[:, :, a, :], sp_[:, :, a, 0, :], sp_[:, :, a, 1, :], ALU.max))
                own.settle()
                for gi, g in enumerate(GROUPS):
                    r, rho, nh, ns, first = g
                    if rho == 0:
                        own.settle()
                    for a in range(2):
                        m = rows_of(M, r, rho, ns, nh, a)
                        own.mark(dve.tensor_tensor(m, m, halves(scx, *g)[:, :, a, :], ALU.max))
                own.settle()
                dve.wait_ge(fb_in, 16 * B * 2)
                Mf = M[:, :, :].rearrange("p (a t) h -> p a (t h)", a=2)[:, :, 0:H * H:H + 1]
                Zf = Z[:, :, :].rearrange("p (a t) h -> p a (t h)", a=2)[:, :, 0:H * H:H + 1]
                tt(Mf, Mf, fb[:, :, :, DH], ALU.max)
                own.mark(dve.tensor_tensor(fg[:, :, :], fb[:, :, :, DH], Mf, ALU.subtract))
                for a in range(SEG):
                    f = a * (a + 1) // 2
                    for b in range(a + 1):
                        own.mark(dve.tensor_tensor(s0[:, :, f + b, :], s0[:, :, f + b, :], M[:, a:BL:SEG, :], ALU.subtract))
                for g in GROUPS:
                    r, rho, nh, ns, first = g
                    for a in range(2):
                        own.mark(dve.tensor_copy(halves(mc, *g)[:, :, a, :], rows_of(M, r, rho, ns, nh, a)))
                own.settle()
                for g in GROUPS:
                    for b in range(2):
                        own.mark(dve.tensor_tensor(parts(sc, *g)[:, :, :, b, :], parts(sc, *g)[:, :, :, b, :],
                                                   halves(mc, *g), ALU.subtract))
                own.settle()
                step(dve.tensor_copy(scx[:, 0:1], mc[:, 0:1]))
                dve.sem_inc(e_req, 1)
                dve.wait_ge(e_done, 4)
                for a in range(SEG):
                    f = a * (a + 1) // 2
                    own.mark(dve.tensor_reduce(Z[:, a:BL:SEG, :],
                                               s0[:, :, f:f + a + 1, :].rearrange("p s b h -> p s h b"), AX.X, ALU.add))
                for g in GROUPS:
                    sp_ = parts(sc, *g)
                    hx = halves(scx, *g)
                    for a in range(2):
                        own.mark(dve.tensor_tensor(hx[:, :, a, :], sp_[:, :, a, 0, :], sp_[:, :, a, 1, :], ALU.add))
                own.settle()
                for gi, g in enumerate(GROUPS):
                    r, rho, nh, ns, first = g
                    if rho == 0:
                        own.settle()
                    for a in range(2):
                        z = rows_of(Z, r, rho, ns, nh, a)
                        own.mark(dve.tensor_tensor(z, z, halves(scx, *g)[:, :, a, :], ALU.add))
                own.settle()
                fsum = fb[:, :, :, DH + 1]
                tt(fsum, fsum, fg[:, :, :], ALU.mult)
                tt(Zf, Zf, fsum, ALU.add)
                step(dve.reciprocal(Z[:, :, :], Z[:, :, :]))
                own.mark(dve.tensor_tensor(fg[:, :, :], fg[:, :, :], Zf, ALU.mult))
                for g in GROUPS:
                    r, rho, nh, ns, first = g
                    for a in range(2):
                        own.mark(dve.tensor_copy(halves(mc, *g)[:, :, a, :], rows_of(Z, r, rho, ns, nh, a)))
                own.settle()
                for gi, g in enumerate(GROUPS):
                    for b in range(2):
                        own.mark(dve.tensor_tensor(parts(sc, *g)[:, :, :, b, :], parts(sc, *g)[:, :, :, b, :],
                                                   halves(mc, *g), ALU.mult))
                own.settle()
                dve.tensor_copy(scx[:, 0:1], mc[:, 0:1]).then_inc(pv_go, 1)
                for a in range(SEG):
                    f = a * (a + 1) // 2
                    for b in range(a + 1):
                        own.mark(dve.tensor_tensor(s0[:, :, f + b, :], s0[:, :, f + b, :], Z[:, a:BL:SEG, :], ALU.mult))
                own.settle()
                for s in range(NS):
                    t = s * SEG
                    for a in range(SEG):
                        f, n = a * (a + 1) // 2, a + 1
                        buf = prod[(s * SEG + a) % 2]
                        if a == 0:
                            own.mark(dve.tensor_tensor(o[:, t, :].rearrange("p (h d) -> p h d", h=H),
                                                       s0[:, s, 0, :].unsqueeze(2).broadcast_to([P, H, DH]),
                                                       vh[:, t, :, :], ALU.mult))
                            continue
                        own.settle()
                        step(dve.tensor_tensor(buf[:, 0:n * D].rearrange("p (n d) -> p n d", d=DH),
                                               s0[:, s, f:f + n, :].rearrange("p b h -> p (b h)").unsqueeze(2).broadcast_to([P, n * H, DH]),
                                               v[:, t:t + n, :].rearrange("p b (h d) -> p (b h) d", h=H), ALU.mult))
                        own.mark(dve.tensor_reduce(o[:, t + a, :], buf[:, 0:n * D].rearrange("p (b x) -> p x b", b=n),
                                                   AX.X, ALU.add))
                own.settle()
                oh = o.rearrange("p t (h d) -> p t h d", h=H)
                dve.wait_ge(pv_done, 4 * len(GROUPS))
                for gi, g in enumerate(GROUPS):
                    r, rho, nh, ns, first = g
                    part = pc[:, first * DH:(first + ns * 4 * nh) * DH].rearrange(
                        "p (s a b h d) -> p s a b h d", s=ns, a=2, b=2, h=nh)
                    if rho == 0:
                        own.settle()
                    for a in range(2):
                        x = rows_of(oh, r, rho, ns, nh, a)
                        step(dve.tensor_tensor(x, x, part[:, :, a, 0, :, :], ALU.add))
                        own.mark(dve.tensor_tensor(x, x, part[:, :, a, 1, :, :], ALU.add))
                own.settle()
                tt(fb[:, :, :, 0:DH], fb[:, :, :, 0:DH], fg[:, :, :].unsqueeze(3).broadcast_to([P, 2, H, DH]), ALU.mult)
                for a in range(2):
                    x = T["o_diag"](a)
                    own.mark(dve.tensor_tensor(x, x, fb[:, a, :, 0:DH], ALU.add))
                own.settle()


def attend_out(nc, T, W):
    with ExitStack() as ctx:
        S = Sems(nc, ctx, "ao_")
        sb = lambda name, shape, dt=F32: ctx.enter_context(nc.sbuf_tensor("ao_" + name, shape, dt))
        w = sb("w", [P, KD, D])
        bias = sb("bias", [P, D])
        xb = [sb(f"xb{i}", [P, D]) for i in range(2)]
        oc = [sb(f"oc{i}", [P, D]) for i in range(2)]
        oT = [sb(f"oT{i}", [P, KD, P]) for i in range(2)]
        rs_ = [sb(f"res{i}", [P, D]) for i in range(2)]
        xo = [sb(f"xo{i}", [P, D]) for i in range(2)]
        xT = [sb(f"xT{i}", [P, KD, P]) for i in range(2)]
        st = [sb(f"st{i}", [P, 6]) for i in range(2)]
        mv = [sb(f"mv{i}", [P, 2]) for i in range(2)]
        var = [sb(f"var{i}", [P, 1]) for i in range(2)]
        rs = [sb(f"rs{i}", [P, 1]) for i in range(2)]
        o, x2b, x3, ident = T["o"], T["x2b"], T["x1"], T["ident"]
        x2_in, w_in = S("x2_in"), S("w_in")
        oc_done, oT_full, oT_done, y_full, res_done, own_sem = (S("oc"), S("oT_full"), S("oT"), S("y_full"), S("res"), S("own"))
        var_done, rs_done, xo_done, xT_full, xT_done, g_full, lg_done = (S("var"), S("rs"), S("xo"), S("xT_full"),
                                                                       S("xT"), S("g_full"), S("lg"))
        xb_done, x3_done, stored = S("xb"), S("x3"), [S(f"stored{i}") for i in range(2)]

        with ExitStack() as pctx, nc.Block() as block:
            pT, pO, pX, pG = ([pctx.enter_context(nc.psum_tensor(f"ao_{nm}{i}", [P, 512], F32)) for i in range(2)]
                              for nm in ("pT", "pO", "pX", "pG"))

            @block.sync
            def _(sp):
                sp.dma_start(w[:, :, :], W["woT"].rearrange("(k p) n -> p k n", p=P)).then_inc(w_in, 16)
                sp.dma_start(bias[:, :], W["bo"].partition_broadcast(P)).then_inc(w_in, 16)
                sp.dma_start(x2b, T["x2_d"].rearrange("(p i) d -> p i d", i=BL)).then_inc(x2_in, 16)
                for i in range(2):
                    sp.sem_inc(stored[i], 16)

                def body(s, h, q, on):
                    sp.wait_ge(xo_done, s + 3)
                    sp.dma_start(T["x3_d"].rearrange("(p i) d -> p i d", i=BL)[:, bass.ds(s, 1), :]
                                 .rearrange("p i d -> p (i d)"), xo[q][:, :]).then_inc(stored[q], 16)
                steps(sp, BL, 0, 2, body)
                for i in range(2):
                    sp.wait_ge(stored[i], 16 * (BL // 2 + 1))

            @block.gpsimd
            def _(pool):
                pool.wait_ge(x2_in, 16)
                pool.wait_ge(w_in, 32)

                def body(s, h, q, on):
                    if on(3):
                        t, r = s - 3, (q - 3) % 2
                        pool.wait_ge(var_done, t + 1)
                        pool.tensor_tensor(rs[r][:, :], var[r][:, :], T["half"][:, 0:1], ALU.pow).then_inc(rs_done, 1)
                    if on(0):
                        pool.wait_ge(res_done, s + 1)
                        hold(pool, T)
                        pool.tensor_tensor(xb[q][:, :], x2b[:, bass.ds(s, 1), :].rearrange("p a d -> p (a d)"),
                                           bias[:, :], ALU.add).then_inc(xb_done, 1)
                steps(pool, BL, 3, 2, body)

            @block.tensor
            def _(pe):
                pe.sem_inc(oT_full, 2)
                pe.sem_inc(y_full, 2)
                pe.sem_inc(xT_full, 2)
                pe.sem_inc(g_full, 2)
                pe.wait_ge(w_in, 32)

                def body(s, h, q, on):
                    if on(1):
                        t, r = s - 1, (q - 1) % 2
                        pe.wait_ge(oc_done, t + 1)
                        pe.wait_ge(oT_done, t + 1)
                        for k in range(KD):
                            mm = pe.transpose(pT[r][:, k * P:(k + 1) * P], oc[r][:, k * P:(k + 1) * P], ident[:, :])
                        mm.then_inc(oT_full, 1)
                    if on(2):
                        t, r = s - 2, q
                        pe.wait_ge(oT_done, t + 3)
                        pe.wait_ge(res_done, t + 1)
                        for k in range(KD):
                            mm = pe.matmul(pO[r][:, 0:D], oT[r][:, k, :], w[:, k, :], start=k == 0, stop=k == KD - 1)
                        mm.then_inc(y_full, 1)
                    if on(4):
                        t, r = s - 4, q
                        pe.wait_ge(xo_done, t + 3)
                        pe.wait_ge(xT_done, t + 1)
                        for k in range(KD):
                            mm = pe.transpose(pX[r][:, k * P:(k + 1) * P], xo[r][:, k * P:(k + 1) * P], ident[:, :])
                        mm.then_inc(xT_full, 1)
                    if on(5):
                        t, r = s - 5, (q - 5) % 2
                        pe.wait_ge(xT_done, t + 3)
                        pe.wait_ge(lg_done, t + 1)
                        for k in range(KD):
                            mm = pe.matmul(pG[r][:, 0:E_], xT[r][:, k, :], T["w_route"][:, k, :], start=k == 0, stop=k == KD - 1)
                        mm.then_inc(g_full, 1)
                steps(pe, BL, 5, 2, body)

            @block.scalar
            def _(act):
                act.sem_inc(oT_done, 2)
                act.sem_inc(xT_done, 2)

                def body(s, h, q, on):
                    if on(0):
                        act.wait_ge(oT_full, s + 1)
                        hold(act, T)
                        act.activation(oc[q][:, :], o[:, bass.ds(s, 1), :].rearrange("p a d -> p (a d)"),
                                       ACT.Identity).then_inc(oc_done, 1)
                    if on(1):
                        t, r = s - 1, (q - 1) % 2
                        act.wait_ge(oT_full, t + 3)
                        act.wait_ge(y_full, t + 1)
                        act.activation(oT[r][:, :, :].rearrange("p k n -> p (k n)"), pT[r][:, 0:D], ACT.Identity).then_inc(oT_done, 1)
                    if on(4):
                        t, r = s - 4, q
                        act.wait_ge(xT_full, t + 3)
                        act.wait_ge(g_full, t + 1)
                        act.activation(xT[r][:, :, :].rearrange("p k n -> p (k n)"), pX[r][:, 0:D], ACT.Identity).then_inc(xT_done, 1)
                steps(act, BL, 5, 2, body)

            @block.vector
            def _(dve):
                dve.sem_inc(res_done, 2)
                dve.sem_inc(xo_done, 2)
                dve.sem_inc(lg_done, 2)

                def body(s, h, q, on):
                    if on(2):
                        t, r = s - 2, q
                        own = Chain(dve, own_sem, t, 2)
                        dve.wait_ge(y_full, t + 3)
                        dve.wait_ge(xb_done, t + 1)
                        dve.wait_ge(xo_done, t + 1)
                        dve.tensor_tensor(rs_[r][:, :], pO[r][:, 0:D], xb[r][:, :], ALU.add).then_inc(res_done, 1)
                        dve.wait_ge(res_done, t + 3)
                        own.step(dve.bn_stats(st[r][:, :], rs_[r][:, :]))
                        hold(dve, T)
                        own.step(dve.bn_aggr(mv[r][:, :], st[r][:, :]))
                        dve.tensor_scalar(var[r][:, :], mv[r][:, 1:2], EPS, None, ALU.add).then_inc(var_done, 1)
                        own.close()
                    if on(3):
                        t, r = s - 3, (q - 3) % 2
                        dve.wait_ge(rs_done, t + 1)
                        dve.wait_ge(stored[r], (h + (q - 3) // 2 + 1) * 16)
                        dve.wait_ge(xT_full, t + 1)
                        dve.wait_ge(x3_done, t + 1)
                        dve.tensor_scalar(xo[r][:, :], rs_[r][:, :], mv[r][:, 0:1], rs[r][:, 0:1],
                                          ALU.subtract, ALU.mult).then_inc(xo_done, 1)
                        dve.wait_ge(xo_done, t + 3)
                        hold(dve, T)
                        dve.tensor_copy(x3[:, bass.ds(t, 1), :].rearrange("p a d -> p (a d)"), xo[r][:, :]).then_inc(x3_done, 1)
                    if on(5):
                        t, r = s - 5, (q - 5) % 2
                        dve.wait_ge(g_full, t + 3)
                        hold(dve, T)
                        dve.tensor_copy(T["logits"][:, bass.ds(t, 1), :].rearrange("p a e -> p (a e)"),
                                        pG[r][:, 0:E_]).then_inc(lg_done, 1)
                dve.sem_inc(x3_done, 2)
                steps(dve, BL, 5, 2, body)
                dve.wait_ge(lg_done, BL + 2)
                dve.wait_ge(x3_done, BL + 2)


def experts1(nc, T, n, pre):
    with ExitStack() as ctx:
        S = Sems(nc, ctx, pre)
        sb = lambda name, shape, dt=F32: ctx.enter_context(nc.sbuf_tensor(pre + name, shape, dt))
        ix = [sb(f"ix{i}", [P, 4], I32) for i in range(2)]
        xg = [sb(f"xg{i}", [P, D]) for i in range(8)]
        xT = [sb(f"xT{i}", [P, KD, P]) for i in range(2)]
        hb = [sb(f"hb{i}", [P, D]) for i in range(2)]
        hn = [sb(f"hn{i}", [P, D]) for i in range(2)]
        hT = [sb(f"hT{i}", [P, KD, P]) for i in range(2)]
        yo = [sb(f"yo{i}", [P, D]) for i in range(2)]
        st = [sb(f"st{i}", [P, 6]) for i in range(2)]
        mv = [sb(f"mv{i}", [P, 2]) for i in range(2)]
        var = [sb(f"var{i}", [P, 1]) for i in range(2)]
        rs = [sb(f"rs{i}", [P, 1]) for i in range(2)]
        ident, w1, w2, b1, b2, g1, be1 = (T[k] for k in ("ident", "w1", "w2b", "b1", "b2", "g1", "be1"))
        ix_done, xT_full, xT_done, h_full, hb_done = S("ix_done"), S("xT_full"), S("xT_done"), S("h_full"), S("hb_done")
        own_sem, var_done, rs_done, hn_done = S("own"), S("var_done"), S("rs_done"), S("hn_done")
        hT_full, hT_done, y_full, y_done = S("hT_full"), S("hT_done"), S("y_full"), S("y_done")
        x_in = [S(f"x_in{i}") for i in range(8)]
        y_stored = [S(f"y_stored{i}") for i in range(2)]
        row = lambda ap, e: ap[:, bass.ds(e, 1), :].rearrange("p a n -> p (a n)")

        with ExitStack() as pctx, nc.Block() as block:
            pX, pH, pHT, pY = ([pctx.enter_context(nc.psum_tensor(f"{pre}{nm}{i}", [P, 512], F32))
                                for i in range(2)] for nm in ("pX", "pH", "pHT", "pY"))

            @block.gpsimd
            def _(pool):
                def body(s, h, q, on):
                    if on(0):
                        if q % 4 == 0:
                            pool.wait_ge(xT_full, s + 4)
                            hold(pool, T)
                            pool.tensor_copy(ix[q // 4][:, :], T["slot_tok"][:, bass.ds(s, 4)]).then_inc(ix_done, 1)
                            pool.wait_ge(ix_done, h * 2 + q // 4 + 1)
                            hold(pool, T)
                        pool.indirect_dma_start(xg[q][:, :], None, T["x3_d"],
                                                bass.IndirectOffsetOnAxis(ap=ix[q // 4][:, q % 4:q % 4 + 1], axis=0)).then_inc(x_in[q], 16)
                    if on(6):
                        t, r = s - 6, q % 2
                        pool.wait_ge(var_done, t + 1)
                        pool.tensor_tensor(rs[r][:, :], var[r][:, :], T["half"][:, 0:1], ALU.pow).then_inc(rs_done, 1)
                steps(pool, n, 6, 8, body)

            @block.sync
            def _(sp):
                for i in range(2):
                    sp.sem_inc(y_stored[i], 16)

                def body(s, h, q, on):
                    sp.wait_ge(y_done, s + 3)
                    sp.dma_start(T["y_d"][bass.ds(s * P, P), :], yo[q % 2][:, :]).then_inc(y_stored[q % 2], 16)
                steps(sp, n, 0, 4, body)
                for i in range(2):
                    sp.wait_ge(y_stored[i], 16 * (n // 2 + 1))

            @block.tensor
            def _(pe):
                pe.sem_inc(xT_full, 8)
                pe.sem_inc(h_full, 2)
                pe.sem_inc(hT_full, 2)
                pe.sem_inc(y_full, 2)
                pe.wait_ge(T["w1_in"], T["w1_n"])
                experts = Experts(pe, T, n)

                def body(s, h, q, on):
                    if on(0):
                        pe.wait_ge(x_in[q], (h + 1) * 16)
                        pe.wait_ge(xT_done, s + 1)
                        for k in range(KD):
                            mm = pe.transpose(pX[q % 2][:, k * P:(k + 1) * P], xg[q][:, k * P:(k + 1) * P], ident[:, :])
                        mm.then_inc(xT_full, 1)
                    experts.before(h, q)
                    if on(1):
                        t, r = s - 1, (q - 1) % 2
                        e = experts.of(q, 1)
                        pe.wait_ge(xT_done, t + 3)
                        pe.wait_ge(hb_done, t + 1)
                        for k in range(KD):
                            mm = pe.matmul(pH[r][:, 0:D], xT[r][:, k, :], row(w1[:, :, k, :], e),
                                           start=k == 0, stop=k == KD - 1)
                        mm.then_inc(h_full, 1)
                    experts.after(h, q)
                    if on(3):
                        t, r = s - 3, (q - 3) % 2
                        pe.wait_ge(hn_done, t + 3)
                        pe.wait_ge(hT_done, t + 1)
                        for k in range(KD):
                            mm = pe.transpose(pHT[r][:, k * P:(k + 1) * P], hn[r][:, k * P:(k + 1) * P], ident[:, :])
                        mm.then_inc(hT_full, 1)
                    if on(4):
                        t, r = s - 4, q % 2
                        e = experts.of(q, 4)
                        pe.wait_ge(hT_done, t + 3)
                        pe.wait_ge(y_done, t + 1)
                        for k in range(KD):
                            mm = pe.matmul(pY[r][:, 0:D], hT[r][:, k, :], row(w2[:, :, k, :], e),
                                           start=k == 0, stop=k == KD - 1)
                        mm.then_inc(y_full, 1)
                steps(pe, n, 4, 8, body)

            @block.scalar
            def _(act):
                act.sem_inc(xT_done, 2)
                act.sem_inc(hT_done, 2)
                act.wait_ge(T["w1_in"], T["w1_n"])
                experts = Experts(act, T, n)

                def body(s, h, q, on):
                    if on(0):
                        act.wait_ge(xT_full, s + 9)
                        act.wait_ge(h_full, s + 1)
                        act.activation(xT[q % 2][:, :, :].rearrange("p k n -> p (k n)"), pX[q % 2][:, 0:D],
                                       ACT.Identity).then_inc(xT_done, 1)
                    experts.before(h, q)
                    experts.after(h, q)
                    if on(3):
                        t, r = s - 3, (q - 3) % 2
                        e = experts.of(q, 3)
                        act.wait_ge(hT_full, t + 3)
                        act.wait_ge(y_full, t + 1)
                        hold(act, T)
                        for k in range(KD):
                            ins = act.activation(hT[r][:, k, :], pHT[r][:, k * P:(k + 1) * P], ACT.Gelu,
                                                 scale=g1[:, k, bass.ds(e, 1)], bias=be1[:, k, bass.ds(e, 1)])
                        ins.then_inc(hT_done, 1)
                steps(act, n, 4, 8, body)

            @block.vector
            def _(dve):
                dve.sem_inc(hb_done, 2)
                dve.sem_inc(hn_done, 2)
                dve.sem_inc(y_done, 2)
                dve.wait_ge(T["w1_in"], T["w1_n"])
                experts = Experts(dve, T, n)

                def body(s, h, q, on):
                    experts.before(h, q)
                    if on(1):
                        t, r = s - 1, (q - 1) % 2
                        own = Chain(dve, own_sem, t, 2)
                        e = experts.of(q, 1)
                        dve.wait_ge(h_full, t + 3)
                        dve.wait_ge(hn_done, t + 1)
                        dve.tensor_tensor(hb[r][:, :], pH[r][:, 0:D], row(b1, e), ALU.add).then_inc(hb_done, 1)
                        dve.wait_ge(hb_done, t + 3)
                        own.step(dve.bn_stats(st[r][:, :], hb[r][:, :]))
                        hold(dve, T)
                        own.step(dve.bn_aggr(mv[r][:, :], st[r][:, :]))
                        dve.tensor_scalar(var[r][:, :], mv[r][:, 1:2], EPS, None, ALU.add).then_inc(var_done, 1)
                        own.close()
                    experts.after(h, q)
                    if on(2):
                        t, r = s - 2, q % 2
                        dve.wait_ge(rs_done, t + 1)
                        dve.wait_ge(hT_full, t + 1)
                        dve.tensor_scalar(hn[r][:, :], hb[r][:, :], mv[r][:, 0:1], rs[r][:, 0:1],
                                          ALU.subtract, ALU.mult).then_inc(hn_done, 1)
                    if on(4):
                        t, r = s - 4, q % 2
                        e = experts.of(q, 4)
                        dve.wait_ge(y_full, t + 3)
                        dve.wait_ge(y_stored[r], (h * 4 + (q - 4) // 2 + 1) * 16)
                        dve.tensor_tensor(yo[r][:, :], pY[r][:, 0:D], row(b2, e), ALU.add).then_inc(y_done, 1)
                steps(dve, n, 4, 8, body)


SLOTS0 = 4 * NT + E_
SLOTS1 = 2 * NT + E_


def shape_tables():
    p, t = np.arange(P), np.arange(NT)
    c32 = np.zeros((P, 256), np.float32)
    c32[:, 0:E_] = E_ - np.arange(E_)
    c32[:, 16:48] = P * t
    c32[:, 48:192] = np.arange(SLOTS0)
    c32[:, 192:224] = P * t[None, :] + p[:, None] - MID_ID
    c32[:, 224:256] = BL * p[:, None] + t[None, :] - MID_ID
    c16 = np.zeros((P, SLOTS0 + 2 * P), np.float16)
    c16[:, 0:SLOTS0] = np.arange(SLOTS0)
    c16[:, SLOTS0:SLOTS0 + P] = p[:, None] < p[None, :]
    c16[:, SLOTS0 + P:] = 1.0
    return c32, c16


def network(nc, W):
    with ExitStack() as ctx:
        def sb(name, shape, dt=F32):
            return ctx.enter_context(nc.sbuf_tensor(name, shape, dt))

        def sem(name):
            return ctx.enter_context(nc.semaphore(name))

        def dram(name, shape):
            return nc.dram_tensor(name, shape, F32, kind="Internal").ap()

        x = sb("x", [P, NT, D])
        R = sb("R", [P, CI * N])
        ident = sb("ident_sb", [P, P])
        half = sb("half", [P, NT])
        c32 = sb("c32_sb", [P, 256])
        c16 = sb("c16_sb", [P, SLOTS0 + 2 * P], F16)
        T = {
            "x1": x, "v": x, "ident": ident, "half": half, "zs": R[:, :].rearrange("p (c n) -> p c n", c=CI),
            "held": sem("held"), "w_ins": sem("ws_in"), "w_in0": sem("w0_in"), "w1_in": sem("w1_in"),
            "rope_in": sem("rope_in"), "w_ns": 32, "w_n0": 32, "w1_n": 96,
            "mixed": dram("mixed", [2, N]), "states": dram("states", [N]),
            "x1_d": dram("x1_d", [N, D]), "x2_d": dram("x2_d", [N, D]), "x3_d": dram("x3_d", [N, D]),
            "y_d": dram("y_d", [SLOTS0 * P, D]),
            "far_d": dram("far_d", [P, 2, H, 3, DH]), "fo_d": dram("fo_d", [B * H, NJ, DH + 2]),
            "w13s": sb("w13s", [P, KD, 2 * IN0]), "w2s": sb("w2s", [P, D]),
            "w_gate": sb("w_gate", [P, KD, E_]), "w_route": sb("w_route", [P, KD, E_]),
            "w130": R[:, 0:E_ * KD * 2 * IN0].rearrange("p (e k n) -> p e k n", e=E_, k=KD),
            "w20": R[:, E_ * KD * 2 * IN0:E_ * KD * 2 * IN0 + E_ * D].rearrange("p (e n) -> p e n", e=E_),
            "x2T": R[:, 0:KD * N].rearrange("p (k n) -> p k n", k=KD),
            "rope": R[:, KD * N:KD * N + BL * D].rearrange("p (t a n) -> p t a n", t=BL, a=2),
            "logits": sb("logits", [P, NT, E_]),
            "tile_exp": sb("tile_exp", [1, SLOTS0 // 4], I32), "slot_tok": sb("slot_tok", [P, SLOTS0], I32),
            "slot_of": sb("slot_of", [P, NT, 4], I32), "slot_w": sb("slot_w", [P, NT, 4]),
            "c32": {"rev": c32[:, 0:16], "thr": c32[:, 16:48], "iota": c32[:, 48:192]},
            "c16": {"iota": c16[:, 0:SLOTS0], "tri": c16[:, SLOTS0:SLOTS0 + P], "ones": c16[:, SLOTS0 + P:]},
        }
        route_b = [sb(f"route_b{i}", [P, E_]) for i in range(2)]
        T["route_b"] = route_b[0]
        early, half_done = sem("early"), sem("half_done")
        stage_sems = range(half_done.num + 1, 256)

        with nc.Block() as block:
            @block.gpsimd
            def _(pool):
                pool.memset(half[:, :], -0.5).then_inc(half_done, 1)
                for dst, src, s in (
                        (T["w13s"][:, :, :], W["w13s"].rearrange("(k p) n -> p k n", p=P), T["w_ins"]),
                        (T["w2s"][:, :], W["w2s"], T["w_ins"]),
                        (T["w_gate"][:, :, :], W["gateT"].rearrange("(k p) e -> p k e", p=P), early),
                        (T["w_route"][:, :, :], W["Wr"].rearrange("(k p) e -> p k e", p=P), early),
                        (route_b[0][:, :], W["gate_b"].partition_broadcast(P), early),
                        (route_b[1][:, :], W["br"].partition_broadcast(P), early),
                        (c32[:, :], W["c32"], early),
                        (c16[:, :], W["c16"], early)):
                    pool.dma_start(dst, src).then_inc(s, 16)
                pool.wait_ge(half_done, 1)

        mixer(nc, T, W)

        with nc.Block() as block:
            @block.gpsimd
            def _(pool):
                pool.sem_clear(stage_sems)

            @block.sync
            def _(sp):
                sp.wait_ge(early, 16 * 6)
                sp.dma_start(T["w130"], W["w13T"].rearrange("e (k p) n -> p e k n", p=P)).then_inc(T["w_in0"], 16)
                sp.dma_start(T["w20"], W["w2T"].rearrange("e p n -> p e n")).then_inc(T["w_in0"], 16)

        experts0(nc, T, False, NT, "sh_")
        dispatch(nc, T, 4, SLOTS0, True, c32[:, 192:224], "d0_")
        experts0(nc, T, True, SLOTS0, "e0_")

        with nc.Block() as block:
            @block.sync
            def _(sp):
                sp.dma_start(T["rope"], W["rope"]).then_inc(T["rope_in"], 16)

        combine(nc, T, 4, x, lambda s: T["x2_d"][bass.ds(s * P, P), :], True, "c0_")

        with ExitStack() as actx:
            qk = actx.enter_context(nc.sbuf_tensor("qk", [P, BL, 2 * D], F32))
            flat = qk[:, :, :].rearrange("p t n -> p (t n)")
            n_c, n_f, n_far = NC * DH, NF * DH, 2 * H * 3 * DH
            T.update({
                "qk": qk, "o": qk[:, :, 0:D], "x2b": qk[:, :, D:2 * D],
                "o_diag": lambda a: bass.AP(flat.tensor, a * H * 2 * D, [flat.ap[0], [2 * D + DH, H], [1, DH]]),
                "prodc": R[:, 0:n_c], "prodf": R[:, n_c:n_c + n_f],
                "far": R[:, n_c + n_f:n_c + n_f + n_far].rearrange("p (a h c d) -> p a h c d", a=2, h=H, c=3),
                "fq": R[0:B * H, n_c + n_f + n_far:n_c + n_f + n_far + NJ * 3 * DH]
                .rearrange("p (j c d) -> p j c d", j=NJ, c=3),
            })
            project_qkv(nc, T, W)
            attend(nc, T, W)
            T["w1"] = R[:, 0:E_ * KD * D].rearrange("p (e k n) -> p e k n", e=E_, k=KD)
            T["w2b"] = R[:, E_ * KD * D:2 * E_ * KD * D].rearrange("p (e k n) -> p e k n", e=E_, k=KD)
            with nc.Block() as block:
                @block.scalar
                def _(act):
                    for dst, src in ((T["w1"], W["W1"]), (T["w2b"], W["W2"])):
                        act.dma_start(dst, src.rearrange("e (k p) n -> p e k n", p=P)).then_inc(T["w1_in"], 16)
            attend_out(nc, T, W)

        T["b1"], T["b2"] = sb("b1", [P, E_, D]), sb("b2", [P, E_, D])
        T["g1"], T["be1"] = sb("g1", [P, KD, E_]), sb("be1", [P, KD, E_])
        T["route_b"] = route_b[1]
        with nc.Block() as block:
            @block.gpsimd
            def _(pool):
                pool.sem_clear(stage_sems)

            @block.sync
            def _(sp):
                for dst, src in ((T["b1"], W["b1"]), (T["b2"], W["b2"])):
                    sp.dma_start(dst[:, :, :].rearrange("p e n -> p (e n)"),
                                 src.rearrange("e n -> (e n)").partition_broadcast(P)).then_inc(T["w1_in"], 16)
                for dst, src in ((T["g1"], W["g1T"]), (T["be1"], W["be1T"])):
                    sp.dma_start(dst[:, :, :], src.rearrange("(k p) e -> p k e", p=P)).then_inc(T["w1_in"], 16)

        dispatch(nc, T, 2, SLOTS1, False, c32[:, 224:256], "d1_")
        experts1(nc, T, SLOTS1, "e1_")
        out = W["out"].rearrange("(p i) d -> p i d", i=BL)
        combine(nc, T, 2, x, lambda s: out[:, bass.ds(s, 1), :].rearrange("p i d -> p (i d)"), False, "c1_")


def layouts(inputs):
    a = {k: np.asarray(v) for k, v in inputs.items()}
    m, f, t, g = (lambda n, p=p: a[p + n] for p in ("L0_attn_", "L0_ffn_", "L1_attn_", "L1_ffn_"))
    cnt0, cntc, cntf = count_tables()
    c32, c16 = shape_tables()
    out = {"x": m("x").reshape(N, D), "xT": m("x").reshape(N, D).T}
    for n in ("W_in", "W_conv", "W_xproj", "W_dt", "b_dt", "W_out"):
        out[n] = m(n)
    out.update({
        "ln_g": m("ln_g").reshape(CI, P).T, "ln_b": m("ln_b").reshape(CI, P).T, "ident": np.eye(P, dtype=np.float32),
        "gateT": f("gate_w").T, "gate_b": f("gate_b"), "w13T": f("w13").transpose(0, 2, 1),
        "w2T": f("w2").transpose(0, 2, 1), "w13s": f("w13_s").T, "w2s": f("w2_s").T,
        "wqkvT": np.concatenate([t("Wq"), t("Wk"), t("Wv")]).T, "bqkv": np.concatenate([t("bq"), t("bk"), t("bv")]),
        "woT": t("Wo").T, "bo": t("bo"), "rope": rope_tables(), "cnt0": cnt0, "cntc": cntc, "cntf": cntf,
        "Wr": g("Wr"), "br": g("br"), "W1": g("W1"), "b1": g("b1"), "W2": g("W2"), "b2": g("b2"),
        "g1T": g("g1").T, "be1T": g("be1").T, "c32": c32, "c16": c16})
    return {k: np.ascontiguousarray(v) for k, v in out.items()}


def kernel(**inputs):
    import concourse.bacc as bacc
    from concourse.bass_utils import run_bass_kernel_spmd

    nc = bacc.Bacc("TRN2", target_bir_lowering=False, num_devices=1)
    arrays = layouts(inputs)
    W = {name: nc.dram_tensor("in_" + name, a.shape, mybir.dt.from_np(a.dtype), kind="ExternalInput").ap()
         for name, a in arrays.items()}
    W["out"] = nc.dram_tensor("out_x", (N, D), F32, kind="ExternalOutput").ap()
    network(nc, W)
    r = run_bass_kernel_spmd(nc, [{"in_" + name: a for name, a in arrays.items()}], core_ids=[0])
    return r.results[0]["out_x"].reshape(B, L, D)
```

```python
from contextlib import ExitStack

import concourse.bass as bass
import numpy as np
from concourse import mybir


ALU = mybir.AluOpType
ACT = mybir.ActivationFunctionType
AX = mybir.AxisListType
F32 = mybir.dt.float32
F16 = mybir.dt.float16
BF16 = mybir.dt.bfloat16
I32 = mybir.dt.int32

P = 128
D = 256
KD = D // P
B, L = 4, 1024
N = B * L
NT = N // P
TB = L // P
DI, DS, DTR = 512, 16, 64
SM = DTR
CI = DI // P
G = L // 512
EPS = 1e-5
E_ = 16
GT = 4
NG = NT // GT


class Chain:

    def __init__(self, eng, sem, it=0, per=0):
        self.eng, self.sem, self.it, self.per, self.n = eng, sem, it, per, 0

    def mark(self, ins):
        if ins is None:
            self.eng.sem_inc(self.sem, 1)
        else:
            ins.then_inc(self.sem, 1)
        self.n += 1

    def settle(self):
        self.eng.wait_ge(self.sem, self.it * self.per + self.n)

    def step(self, ins):
        self.mark(ins)
        self.settle()

    def close(self):
        assert self.n == self.per, (self.n, self.per)


def hold(eng, T):
    eng.sem_inc(T["held"], 1)


def mixer(nc, T, W):
    with ExitStack() as ctx:
        def sb(name, shape, dt=F32):
            return ctx.enter_context(nc.sbuf_tensor("mx_" + name, shape, dt))

        def sem(name):
            return ctx.enter_context(nc.semaphore("mx_" + name))

        ident = T["ident"]
        x1 = T["x1"]
        xin = x1[:, :, :].rearrange("p t d -> p (t d)").rearrange("p (k n) -> p k n", k=KD)
        w_in = sb("w_in", [P, KD, 2 * DI])
        w_conv = sb("w_conv", [P, CI, 3])
        w_x = sb("w_x", [P, CI, SM + DS + 2])
        w_b = sb("w_b", [P, CI, DS])
        w_dt = sb("w_dt", [DTR + 1, DI])
        w_dtsum = sb("w_dtsum", [DTR + 1, 1])
        w_out = sb("w_out", [P, CI, D])
        ln_g = sb("ln_g", [P, CI])
        ln_b = sb("ln_b", [P, CI])
        work = sb("work", [P, 4 * L + 4])
        xs_pad = [work[:, i * (L + 2):(i + 1) * (L + 2)] for i in range(2)]
        conv = [work[:, 2 * (L + 2) + i * L:2 * (L + 2) + (i + 1) * L] for i in range(2)]
        xs = sb("xs", [P, CI, L])
        zs = T["zs"]
        zsil = sb("zsil", [P, CI, L])
        yz = xs
        dtl_all = sb("dtl", [P, L])
        dtl = dtl_all[0:DTR + 1, :]
        small = sb("small", [P, NT, DS + 2])
        absu = sb("absu", [P, DI])
        expu = sb("expu", [P, DI])
        lnu = sb("lnu", [P, DI])
        sum_abs = sb("sum_abs", [P, TB])
        sum_ln = sb("sum_ln", [P, TB])
        sum_ua = sb("sum_ua", [P, TB])
        sum_dt = sb("sum_dt", [P, NT])
        dec_bx = sb("dec_bx", [P, 2, NT])
        dec_bxT = sb("dec_bxT", [NT, 2, P])
        rows = sb("rows", [B, 2, L])
        s_rows = sb("s_rows", [B, L])
        s_blk = sb("s_blk", [NT, P])
        s_tok = sb("s_tok", [P, NT])
        c_sum = sb("c_sum", [P, NT])
        cc = sb("cc", [P, NT, DS])
        csq = sb("csq", [P, NT, DS])
        c_var = sb("c_var", [P, NT])
        y_var = sb("y_var", [P, NT])
        y_rs = sb("y_rs", [P, NT])
        y_f = sb("y_f", [P, NT])
        yn = sb("yn", [P, NT, DS])
        yrep = sb("yrep", [P, TB, 8, DS])
        smT = yrep[0:DS + 2, :, :, :].rearrange("p t a s -> p (t a s)")
        res = work[:, 0:TB * D].rearrange("p (t d) -> p t d", t=TB)
        xo = work[:, TB * D:2 * TB * D].rearrange("p (t d) -> p t d", t=TB)
        xoT = dtl_all[:, :].rearrange("p (t k n) -> p t k n", t=GT, k=KD)
        stats = sb("stats", [P, TB, 6])
        mv = sb("mv", [P, TB, 2])
        x_var = sb("x_var", [P, TB])
        x_rs = sb("x_rs", [P, TB])
        SUMU = TB * (DS + 2)

        consts = sem("consts")
        w_in_in = sem("w_in_in")
        x_ready = sem("x_ready")
        x_in = [sem(f"x_in{b}") for b in range(B)]
        prep = sem("prep")
        xs_full = sem("xs_full")
        xs_evac = sem("xs_evac")
        z_full = sem("z_full")
        z_evac = sem("z_evac")
        conv_done = sem("conv_done")
        xs_done = sem("xs_done")
        rank_done = sem("rank_done")
        lo_full = sem("lo_full")
        lo_done = sem("lo_done")
        sm_done = sem("sm_done")
        small_done = sem("small_done")
        u_full = sem("u_full")
        u_free = sem("u_free")
        ln_done = sem("ln_done")
        dsum_done = sem("dsum_done")
        act_own = sem("act_own")
        dve_own = sem("dve_own")
        decay_done = sem("decay_done")
        bx_done = sem("bx_done")
        turned = sem("turned")
        turned_out = sem("turned_out")
        to_dram = sem("to_dram")
        rows_in = sem("rows_in")
        scanned = sem("scanned")
        s_dram = sem("s_dram")
        s_in = sem("s_in")
        s_turned = sem("s_turned")
        y_var_done = sem("y_var_done")
        y_rs_done = sem("y_rs_done")
        x_res = sem("x_res")

        mixed = T["mixed"]
        states = T["states"]

        with ExitStack() as pctx, nc.Block() as block:
            def ps(name):
                return pctx.enter_context(nc.psum_tensor("mx_" + name, [P, 512], F32))

            pA = [ps(f"pA{i}") for i in range(2)]
            pZ = [ps(f"pZ{i}") for i in range(2)]
            pU = [ps(f"pU{i}") for i in range(2)]
            pL = ps("pL")
            pS = ps("pS")

            @block.sync
            def _(sp):
                xT = W["xT"].rearrange("(k p) n -> p k n", p=P)
                w_x_d = W["W_xproj"].rearrange("(c p) n -> p c n", p=P)
                w_in_d = W["W_in"].rearrange("(k p) n -> p k n", p=P)
                sp.dma_start(w_in[:, :, 0:DI], w_in_d[:, :, 0:DI]).then_inc(w_in_in, 16)
                sp.dma_start(xin[:, :, 0:L], xT[:, :, 0:L]).then_inc(x_in[0], 16)
                sp.dma_start(w_in[:, :, DI:2 * DI], w_in_d[:, :, DI:2 * DI]).then_inc(consts, 16)
                for dst, src in ((w_conv[:], W["W_conv"].rearrange("(c p) a k -> p c (a k)", p=P)),
                                 (w_x[:, :, 0:SM], w_x_d[:, :, 0:DTR]),
                                 (w_x[:, :, SM:SM + DS], w_x_d[:, :, DTR + DS:DTR + 2 * DS]),
                                 (w_b[:], w_x_d[:, :, DTR:DTR + DS]),
                                 (w_dt[0:DTR, :], W["W_dt"]),
                                 (w_dt[DTR:DTR + 1, :], W["b_dt"].rearrange("(a n) -> a n", a=1)),
                                 (ident[:], W["ident"]),
                                 (ln_g[:], W["ln_g"]),
                                 (ln_b[:], W["ln_b"]),
                                 (w_out[:], W["W_out"].rearrange("(c p) n -> p c n", p=P))):
                    sp.dma_start(dst, src).then_inc(consts, 16)
                for b in range(1, B):
                    sp.dma_start(xin[:, :, b * L:(b + 1) * L], xT[:, :, b * L:(b + 1) * L]).then_inc(x_in[b], 16)
                T["early_loads"](sp)
                for b in range(1, B):
                    sp.wait_ge(x_in[b], 16)
                    sp.sem_inc(x_ready, 1)
                sp.wait_ge(turned_out, 1)
                sp.dma_start(mixed.rearrange("a (q p) -> q a p", p=P), dec_bxT[:, :, :]).then_inc(to_dram, 16)
                sp.wait_ge(to_dram, 16)
                sp.dma_start(rows[:, :, :], mixed.rearrange("a (b l) -> b a l", b=B)).then_inc(rows_in, 16)
                sp.wait_ge(scanned, 1)
                sp.dma_start(states.rearrange("(b l) -> b l", b=B), s_rows[:, :]).then_inc(s_dram, 16)
                sp.wait_ge(s_dram, 16)
                sp.dma_start(s_blk[:, :], states.rearrange("(q p) -> q p", p=P)).then_inc(s_in, 16)
                sp.wait_ge(z_full, B * CI * G)
                sp.dma_start(x1[:, :, :], W["x"].rearrange("(t p) d -> p t d", p=P)).then_inc(x_res, 16)

            @block.tensor
            def _(pe):
                pe.sem_inc(rank_done, 1)
                pe.sem_inc(lo_full, 1)
                pe.sem_inc(x_ready, 1)
                pe.wait_ge(w_in_in, 16)
                pe.wait_ge(x_in[0], 16)
                with pe.Fori(0, B) as b:
                    pe.wait_ge(x_ready, b + 1)

                    def proj(j, ring, full, evac, n):
                        m, g = j // G, j % G
                        pe.wait_ge(evac, b * 8 + n + 1)
                        for k in range(KD):
                            mm = pe.matmul(ring[n % 2][:, :], w_in[:, k, m * P:(m + 1) * P],
                                           xin[:, k, bass.ds(b * L + g * 512, 512)],
                                           start=k == 0, stop=k == KD - 1)
                        mm.then_inc(full, 1)

                    for j in range(8):
                        proj(j, pA, xs_full, xs_evac, j)
                    pe.wait_ge(consts, 16 * 11)
                    for j in range(2):
                        proj(8 + j, pZ, z_full, z_evac, j)
                    pe.wait_ge(prep, 8)
                    pe.wait_ge(xs_done, b * CI + 2 + CI)
                    for g in range(G):
                        pe.wait_ge(lo_done, b * G + g + 1)
                        if g > 0:
                            pe.wait_ge(sm_done, b * G + g)
                        for c in range(CI):
                            mm = pe.matmul(pL[0:SM + DS + 2, :], w_x[:, c, :], xs[:, c, g * 512:(g + 1) * 512],
                                           start=c == 0, stop=c == CI - 1)
                        mm.then_inc(lo_full, 1)
                        proj(10 + g, pZ, z_full, z_evac, 2 + g)
                    pe.wait_ge(dsum_done, b + 1)
                    pe.wait_ge(sm_done, b * G + G)
                    hold(pe, T)
                    for t in range(TB):
                        mm = pe.transpose(pS[:, t * (DS + 2):(t + 1) * (DS + 2)], smT[:, t * P:(t + 1) * P],
                                          ident[0:DS + 2, 0:DS + 2])
                    mm.then_inc(rank_done, 1)
                    pe.wait_ge(lo_done, b * G + G + 1)
                    pe.wait_ge(small_done, b + 1)
                    for t in range(TB):
                        pe.wait_ge(u_free, b * TB + t + 1)
                        pe.matmul(pS[:, SUMU + t:SUMU + t + 1], dtl[:, t * P:(t + 1) * P], w_dtsum[:, :],
                                  start=True, stop=True)
                        pe.matmul(pU[t % 2][:, :], dtl[:, t * P:(t + 1) * P], w_dt[:, :],
                                  start=True, stop=True).then_inc(u_full, 1)
                        if t % 2 == 0:
                            n = 4 + t // 2
                            proj(8 + n, pZ, z_full, z_evac, n)
                pe.wait_ge(decay_done, 1)
                pe.wait_ge(bx_done, 1)
                pe.wait_ge(small_done, B)
                pe.wait_ge(lo_done, B * G + 1)
                for a in range(2):
                    mm = pe.transpose(pL[0:NT, a * P:(a + 1) * P], dec_bx[:, a, :], ident[:, :])
                mm.then_inc(turned, 1)
                pe.wait_ge(s_in, 16)
                pe.wait_ge(turned_out, 1)
                pe.transpose(pL[:, 256:256 + NT], s_blk[:, :], ident[0:NT, 0:NT]).then_inc(s_turned, 1)

            @block.scalar
            def _(act):
                act.sem_inc(xs_evac, 2)
                act.sem_inc(xs_done, 2)
                act.sem_inc(u_free, 2)
                with act.Fori(0, B) as b:
                    def copy_xs(m):
                        act.wait_ge(conv_done, b * CI + m + 1)
                        for g in range(G):
                            act.wait_ge(xs_full, b * 8 + m * G + g + 1)
                            act.activation(xs_pad[m % 2][:, 1 + g * 512:1 + (g + 1) * 512],
                                           pA[g][:, :], ACT.Identity).then_inc(xs_evac, 1)

                    def silu_xs(m):
                        if m == 0:
                            act.wait_ge(lo_full, b * G + 1)
                        act.wait_ge(conv_done, b * CI + 2 + m + 1)
                        act.activation(xs[:, m, :], conv[m % 2][:, :], ACT.Silu).then_inc(xs_done, 1)

                    copy_xs(0)
                    for m in range(1, CI):
                        copy_xs(m)
                        silu_xs(m - 1)
                    silu_xs(CI - 1)
                    act.wait_ge(dsum_done, b + 1)
                    hold(act, T)
                    act.preload_act_table_set("natural_log_exp_and_others")
                    own = Chain(act, act_own, b, TB)
                    for t in range(TB):
                        act.wait_ge(u_full, b * TB + t + 1)
                        act.activation(absu[:, :], pU[t % 2][:, :], ACT.Abs,
                                       accum_out=sum_abs[:, t:t + 1]).then_inc(u_free, 1)
                        act.wait_ge(u_free, b * TB + t + 1 + 2)
                        own.step(act.activation(expu[:, :], absu[:, :], ACT.Exp, scale=-1.0))
                        act.activation(lnu[:, :], expu[:, :], ACT.Ln, bias=1.0,
                                       accum_out=sum_ln[:, t:t + 1]).then_inc(ln_done, 1)
                        act.wait_ge(ln_done, b * TB + t + 1)
                    own.close()
                act.wait_ge(dsum_done, B + 1)
                act.activation(dec_bx[:, 0, :], sum_dt[:, :], ACT.Exp, scale=-1.0 / DI).then_inc(decay_done, 1)

            @block.vector
            def _(dve):
                dve.sem_inc(z_evac, 2)
                dve.sem_inc(conv_done, 2)
                dve.sem_inc(lo_done, 1)
                dve.sem_inc(dsum_done, 1)
                dve.wait_ge(consts, 16 * 11)
                for i in range(2):
                    dve.memset(xs_pad[i][:, 0:1], 0.0).then_inc(prep, 1)
                    dve.memset(xs_pad[i][:, L + 1:L + 2], 0.0).then_inc(prep, 1)
                dve.memset(dtl[DTR:DTR + 1, :], 1.0).then_inc(prep, 1)
                dve.memset(w_x[:, :, SM + DS + 1:SM + DS + 2], 1.0).then_inc(prep, 1)
                dve.tensor_reduce(w_x[:, :, SM + DS], w_b[:, :, :], AX.X, ALU.add).then_inc(prep, 1)
                dve.tensor_reduce(w_dtsum[:, 0:1], w_dt[:, :], AX.X, ALU.add).then_inc(prep, 1)
                dve.wait_ge(prep, 8)
                with dve.Fori(0, B) as b:
                    own = Chain(dve, dve_own, b, 2 * CI + 1)

                    def copy_z(n):
                        c, g = n // G, n % G
                        dve.wait_ge(z_full, b * 8 + n + 1)
                        hold(dve, T)
                        dve.tensor_copy(zs[:, c, bass.ds(b * L + g * 512, 512)], pZ[n % 2][:, :]).then_inc(z_evac, 1)

                    for m in range(CI):
                        pad, out = xs_pad[m % 2], conv[m % 2]
                        dve.wait_ge(xs_evac, b * 8 + 2 + (m + 1) * G)
                        dve.wait_ge(xs_done, b * CI + m + 1)
                        own.step(dve.tensor_scalar(out[:, :], pad[:, 1:L + 1], w_conv[:, m, 1:2], None, ALU.mult))
                        own.step(dve.scalar_tensor_tensor(out=out[:, :], in0=pad[:, 0:L], scalar=w_conv[:, m, 0:1],
                                                          in1=out[:, :], op0=ALU.mult, op1=ALU.add))
                        dve.scalar_tensor_tensor(out=out[:, :], in0=pad[:, 2:L + 2], scalar=w_conv[:, m, 2:3],
                                                 in1=out[:, :], op0=ALU.mult, op1=ALU.add).then_inc(conv_done, 1)
                    copy_z(0)
                    copy_z(1)
                    for g in range(G):
                        dve.wait_ge(lo_full, b * G + g + 2)
                        dve.tensor_copy(dtl[0:DTR, g * 512:(g + 1) * 512], pL[0:DTR, :]).then_inc(lo_done, 1)
                        if g == 0:
                            dve.wait_ge(rank_done, b + 1)
                        dve.tensor_copy(smT[:, g * 512:(g + 1) * 512], pL[SM:SM + DS + 2, :]).then_inc(sm_done, 1)
                        copy_z(2 + g)
                    dve.wait_ge(rank_done, b + 2)
                    hold(dve, T)
                    dve.tensor_copy(small[:, bass.ds(b * TB, TB), :],
                                    pS[:, 0:SUMU].rearrange("p (t c) -> p t c", t=TB)).then_inc(small_done, 1)
                    for n in range(4, 8):
                        copy_z(n)
                    dve.wait_ge(u_full, b * TB + TB)
                    dve.wait_ge(ln_done, b * TB + TB)
                    own.step(dve.tensor_tensor(sum_ua[:, :], pS[:, SUMU:SUMU + TB], sum_abs[:, :], ALU.add))
                    dve.scalar_tensor_tensor(out=sum_dt[:, bass.ds(b * TB, TB)], in0=sum_ua[:, :], scalar=0.5,
                                             in1=sum_ln[:, :], op0=ALU.mult, op1=ALU.add).then_inc(dsum_done, 1)
                    own.close()
                own = Chain(dve, dve_own, B, 2 * CI + 1)
                dve.wait_ge(small_done, B)
                dve.scalar_tensor_tensor(out=dec_bx[:, 1, :], in0=small[:, :, DS], scalar=1.0 / DI,
                                         in1=small[:, :, DS + 1], op0=ALU.mult, op1=ALU.mult).then_inc(bx_done, 1)
                dve.wait_ge(turned, 1)
                dve.tensor_copy(dec_bxT[:, :, :], pL[0:NT, 0:2 * P].rearrange("q (a p) -> q a p", a=2)).then_inc(turned_out, 1)
                own.step(dve.tensor_reduce(c_sum[:, :], small[:, :, 0:DS], AX.X, ALU.add))
                own.step(dve.scalar_tensor_tensor(out=cc[:, :, :], in0=c_sum[:, :].unsqueeze(2).broadcast_to([P, NT, DS]),
                                                  scalar=-1.0 / DS, in1=small[:, :, 0:DS],
                                                  op0=ALU.mult, op1=ALU.add))
                own.step(dve.tensor_tensor(csq[:, :, :], cc[:, :, :], cc[:, :, :], ALU.mult))
                own.step(dve.tensor_reduce(c_var[:, :], csq[:, :, :], AX.X, ALU.add))
                dve.wait_ge(rows_in, 16)
                dve.tensor_tensor_scan(s_rows[:, :], rows[:, 0, :], rows[:, 1, :], 0.0,
                                       ALU.mult, ALU.add).then_inc(scanned, 1)
                dve.wait_ge(s_turned, 1)
                own.step(dve.tensor_copy(s_tok[:, :], pL[:, 256:256 + NT]))
                own.step(dve.tensor_tensor(y_var[:, :], s_tok[:, :], s_tok[:, :], ALU.mult))
                own.step(dve.tensor_tensor(y_var[:, :], y_var[:, :], c_var[:, :], ALU.mult))
                dve.tensor_scalar(y_var[:, :], y_var[:, :], 1.0 / DS, EPS, ALU.mult, ALU.add).then_inc(y_var_done, 1)
                dve.wait_ge(y_rs_done, 1)
                own.step(dve.tensor_tensor(y_f[:, :], s_tok[:, :], y_rs[:, :], ALU.mult))
                own.step(dve.tensor_tensor(yn[:, :, :], cc[:, :, :],
                                           y_f[:, :].unsqueeze(2).broadcast_to([P, NT, DS]), ALU.mult))

            @block.gpsimd
            def _(pool):
                pool.wait_ge(y_var_done, 1)
                pool.tensor_tensor(y_rs[:, :], y_var[:, :], T["half"][:, 0:NT], ALU.pow).then_inc(y_rs_done, 1)

        mixer_out(nc, T, ctx, sem, x_res, x1, ident, zs, zsil, yz, yn, yrep, w_out, ln_g, ln_b,
                  res, xo, xoT, stats, mv, x_var, x_rs)


def steps(eng, n, depth, unroll, body):
    first = -(-depth // unroll)
    loops = n // unroll - first
    for s in range(first * unroll):
        body(s, s // unroll, s % unroll, lambda k: 0 <= s - k < n)
    with eng.Fori(first, first + loops) as h:
        for q in range(unroll):
            body(h * unroll + q, h, q, lambda k: True)
    for s in range((first + loops) * unroll, n + depth):
        body(s, s // unroll, s % unroll, lambda k: 0 <= s - k < n)




def mixer_out(nc, T, ctx, sem, x_res, x1, ident, zs, zsil, yz, yn, yrep, w_out, ln_g, ln_b, res, xo, xoT,
              stats, mv, x_var, x_rs):
    yrep_done = sem("yrep_done")
    y_turned = sem("y_turned")
    y_scaled = sem("y_scaled")
    z_silu = sem("z_silu")
    yz_done = sem("yz_done")
    o_full = sem("o_full")
    o_evac = sem("o_evac")
    x_var_done = sem("x_var_done")
    x_rs_done = sem("x_rs_done")
    xo_done = sem("xo_done")
    xo_turned = sem("xo_turned")
    xoT_done = sem("xoT_done")
    g_full = sem("g_full")
    lg_done = sem("lg_done")
    x1_stored = [sem(f"x1_stored{i}") for i in range(2)]
    own_sem = sem("own2")
    GW = GT * P
    with ExitStack() as pctx, nc.Block() as block:
        pY = [pctx.enter_context(nc.psum_tensor(f"mx_pY{i}", [P, 512], F32)) for i in range(2)]
        pO = [pctx.enter_context(nc.psum_tensor(f"mx_pO{i}", [P, 512], F32)) for i in range(2)]
        pX = [pctx.enter_context(nc.psum_tensor(f"mx_pX{i}", [P, 512], F32)) for i in range(2)]
        pG = pctx.enter_context(nc.psum_tensor("mx_pG", [P, 512], F32))

        @block.tensor
        def _(pe):
            pe.wait_ge(T["early"], T["early_n"])
            pe.sem_inc(xo_turned, 2)
            pe.sem_inc(g_full, 1)
            pe.sem_inc(y_turned, 2)
            pe.sem_inc(o_full, 2 * GT)

            def body(s, h, q, on):
                if on(0):
                    pe.wait_ge(yrep_done, s + 1)
                    pe.wait_ge(y_scaled, (s + 1) * CI)
                    for t in range(GT):
                        mm = pe.transpose(pY[q][:, t * P:(t + 1) * P],
                                          yrep[:, q * GT + t, :, :].rearrange("p a s -> p (a s)"), ident[:, :])
                    mm.then_inc(y_turned, 1)
                def turn_x1():
                    g, r = s - 4, q
                    pe.wait_ge(xo_done, (g + 3) * GT)
                    if not isinstance(g, int) or g > 0:
                        pe.wait_ge(xoT_done, g)
                    for t in range(GT):
                        for k in range(KD):
                            at = (t % 2 * KD + k) * P
                            mm = pe.transpose(pX[t // 2][:, at:at + P], xo[:, r * GT + t, k * P:(k + 1) * P], ident[:, :])
                    mm.then_inc(xo_turned, 1)

                if on(4) and not on(2):
                    turn_x1()
                if on(2):
                    g = s - 2
                    pe.wait_ge(yz_done, g + 3)
                    for t in range(GT):
                        pe.wait_ge(o_evac, g * GT + t + 1)
                        for c in range(CI):
                            mm = pe.matmul(pO[t % 2][:, 0:D], yz[:, c, q * GW + t * P:q * GW + (t + 1) * P], w_out[:, c, :],
                                           start=c == 0, stop=c == CI - 1)
                        mm.then_inc(o_full, 1)
                        if t == 1 and on(4):
                            turn_x1()
                if on(4):
                    g = s - 4
                    pe.wait_ge(xoT_done, g + 1)
                    pe.wait_ge(lg_done, g + 1)
                    for t in range(GT):
                        for k in range(KD):
                            mm = pe.matmul(pG[:, t * E_:(t + 1) * E_], xoT[:, t, k, :], T["w_gate"][:, k, :],
                                           start=k == 0, stop=k == KD - 1)
                    mm.then_inc(g_full, 1)
            steps(pe, NG, 4, 2, body)

        @block.scalar
        def _(act):
            act.sem_inc(y_scaled, 2 * CI)
            act.sem_inc(lg_done, 1)

            def body(s, h, q, on):
                if on(0):
                    act.wait_ge(yz_done, s + 1)
                    hold(act, T)
                    act.activation(zsil[:, :, q * GW:(q + 1) * GW], zs[:, :, bass.ds(s * GW, GW)],
                                   ACT.Silu).then_inc(z_silu, 1)
                if on(1):
                    g, r = s - 1, (q - 1) % 2
                    act.wait_ge(y_turned, g + 3)
                    act.wait_ge(o_full, (g + 1) * GT)
                    for c in range(CI):
                        act.activation(yz[:, c, r * GW:(r + 1) * GW], pY[r][:, :], ACT.Identity,
                                       scale=ln_g[:, c:c + 1], bias=ln_b[:, c:c + 1]).then_inc(y_scaled, 1)
                if on(4):
                    g = s - 4
                    act.wait_ge(xo_turned, g + 3)
                    act.wait_ge(g_full, g + 1)
                    for i in range(2):
                        ins = act.activation(xoT[:, 2 * i:2 * i + 2, :, :].rearrange("p t k n -> p (t k n)"), pX[i][:, :],
                                             ACT.Identity)
                    ins.then_inc(xoT_done, 1)
                    act.wait_ge(g_full, g + 2)
                    hold(act, T)
                    act.activation(T["logits"][:, bass.ds(g * GT, GT), :],
                                   pG[:, 0:GT * E_].rearrange("p (t e) -> p t e", t=GT), ACT.Identity).then_inc(lg_done, 1)
            steps(act, NG, 4, 2, body)
            act.wait_ge(lg_done, NG + 1)

        @block.vector
        def _(dve):
            dve.sem_inc(o_evac, 2)
            dve.sem_inc(yz_done, 2)
            dve.sem_inc(xo_done, 2 * GT)
            dve.wait_ge(x_res, 16)

            def body(s, h, q, on):
                def gate():
                    g, r = s - 1, (q - 1) % 2
                    dve.wait_ge(z_silu, g + 1)
                    dve.wait_ge(y_scaled, (g + 3) * CI)
                    half = slice(r * GW, (r + 1) * GW)
                    dve.tensor_tensor(yz[:, :, half], yz[:, :, half], zsil[:, :, half], ALU.mult).then_inc(yz_done, 1)

                if on(1) and not on(2):
                    gate()
                if on(2):
                    g = s - 2
                    own = Chain(dve, own_sem, g, 2 * GT)
                    dve.wait_ge(xo_done, (g + 1) * GT)
                    for t in range(GT):
                        dve.wait_ge(o_full, (g + 2) * GT + t + 1)
                        dve.tensor_tensor(res[:, q * GT + t, :], pO[t % 2][:, 0:D],
                                          x1[:, bass.ds(g * GT + t, 1), :].rearrange("p a d -> p (a d)"),
                                          ALU.add).then_inc(o_evac, 1)
                        if t > 0:
                            dve.wait_ge(o_evac, g * GT + 2 + t)
                            own.mark(dve.bn_stats(stats[:, q * GT + t - 1, :], res[:, q * GT + t - 1, :]))
                        if t == 1 and on(1):
                            gate()
                    dve.wait_ge(o_evac, g * GT + 2 + GT)
                    own.mark(dve.bn_stats(stats[:, q * GT + GT - 1, :], res[:, q * GT + GT - 1, :]))
                    own.settle()
                    hold(dve, T)
                    for t in range(GT):
                        own.mark(dve.bn_aggr(mv[:, q * GT + t, :], stats[:, q * GT + t, :]))
                    own.settle()
                    dve.tensor_scalar(x_var[:, q * GT:(q + 1) * GT], mv[:, q * GT:(q + 1) * GT, 1], EPS, None,
                                      ALU.add).then_inc(x_var_done, 1)
                    own.close()
                if on(3):
                    g, r = s - 3, (q - 3) % 2
                    dve.wait_ge(x_rs_done, g + 1)
                    dve.wait_ge(x1_stored[r], (h + (q - 3) // 2 + 1) * 16)
                    dve.wait_ge(xo_turned, g + 1)
                    for t in range(GT):
                        i = r * GT + t
                        dve.tensor_scalar(xo[:, i, :], res[:, i, :], mv[:, i, 0:1], x_rs[:, i:i + 1],
                                          ALU.subtract, ALU.mult).then_inc(xo_done, 1)
            steps(dve, NG, 3, 2, body)

        @block.gpsimd
        def _(pool):
            def body(s, h, q, on):
                if on(0):
                    pool.wait_ge(y_turned, s + 1)
                    hold(pool, T)
                    pool.tensor_copy(yrep[:, q * GT:(q + 1) * GT, :, :],
                                     yn[:, bass.ds(s * GT, GT), :].unsqueeze(2).broadcast_to([P, GT, 8, DS])
                                     ).then_inc(yrep_done, 1)
                if on(3):
                    g, r = s - 3, (q - 3) % 2
                    pool.wait_ge(x_var_done, g + 1)
                    pool.tensor_tensor(x_rs[:, r * GT:(r + 1) * GT], x_var[:, r * GT:(r + 1) * GT], T["half"][:, 0:GT],
                                       ALU.pow).then_inc(x_rs_done, 1)
            steps(pool, NG, 3, 2, body)

        @block.sync
        def _(sp):
            for i in range(2):
                sp.sem_inc(x1_stored[i], 16)

            def body(s, h, q, on):
                if on(0):
                    sp.wait_ge(xo_done, (s + 3) * GT)
                    sp.dma_start(T["x1_d"].rearrange("(t p) d -> p t d", p=P)[:, bass.ds(s * GT, GT), :],
                                 xo[:, q * GT:(q + 1) * GT, :]).then_inc(x1_stored[q], 16)
                if on(2):
                    g = s - 2
                    sp.wait_ge(lg_done, g + 2)
                    sp.dma_start(T["logits_d"].rearrange("(t p) e -> p t e", p=P)[:, bass.ds(g * GT, GT), :],
                                 T["logits"][:, bass.ds(g * GT, GT), :]).then_inc(T["logits_out"], 16)
            steps(sp, NG, 2, 2, body)
            sp.wait_ge(T["logits_out"], 16 * NG)
            for i in range(2):
                sp.wait_ge(x1_stored[i], 16 * (NG // 2 + 1))


IN0 = 128
MID_ID = N // 2


class Experts:

    BACK, IN = 4, 6

    def __init__(self, eng, T, n):
        self.eng, self.words, self.n, self.loaded = eng, T["tile_exp"], n // 8, {}

    def load(self, h, i):
        if not isinstance(h, int) or h <= self.n:
            self.loaded[i] = self.eng.value_load(self.words[0:1, bass.ds(h * 2 + i, 1)], min_val=0,
                                                 max_val=E_ ** self.IN - 1)

    def before(self, h, q):
        if q == 0:
            self.load(h, 0)

    def after(self, h, q):
        if q == 1:
            self.load(h, 1)

    def of(self, q, k):
        j = q - k + self.BACK
        return (self.loaded[j // self.IN] >> (4 * (j % self.IN))) & (E_ - 1)


class Sems:

    def __init__(self, nc, ctx, prefix):
        self.make = lambda name: ctx.enter_context(nc.semaphore(prefix + name))
        self.made = {}

    def __call__(self, name):
        if name not in self.made:
            self.made[name] = self.make(name)
        return self.made[name]


def experts0(nc, T, n, pre):
    with ExitStack() as ctx:
        S = Sems(nc, ctx, pre)
        sb = lambda name, shape, dt=F32: ctx.enter_context(nc.sbuf_tensor(pre + name, shape, dt))
        xT = [sb(f"xT{i}", [P, KD, P]) for i in range(2)]
        sg = [sb(f"sg{i}", [P, IN0]) for i in range(2)]
        hh = [sb(f"hh{i}", [P, IN0]) for i in range(2)]
        hT = [sb(f"hT{i}", [P, P]) for i in range(2)]
        xg = [sb(f"xg{i}", [P, D]) for i in range(8)]
        ix = [sb(f"ix{i}", [P, 4], I32) for i in range(2)]
        yo = [sb(f"yo{i}", [P, D]) for i in range(2)]
        ident, w13, w2 = T["ident"], T["w13"], T["w2"]
        xT_full, xT_done = S("xT_full"), S("xT_done")
        h_full, sg_done, hh_done = S("h_full"), S("sg_done"), S("hh_done")
        ht_full, ht_done = S("ht_full"), S("ht_done")
        y_full, y_done = S("y_full"), S("y_done")
        x_in = [S(f"x_in{i}") for i in range(8)]
        y_stored = [S(f"y_stored{i}") for i in range(2)]
        ix_done = S("ix_done")

        with ExitStack() as pctx, nc.Block() as block:
            pX, pH, pHT, pY = ([pctx.enter_context(nc.psum_tensor(f"{pre}{nm}{i}", [P, 512], F32))
                                for i in range(2)] for nm in ("pX", "pH", "pHT", "pY"))

            @block.gpsimd
            def _(pool):
                def body(s, h, q, on):
                    if q % 4 == 0:
                        pool.wait_ge(xT_full, s + 4)
                        hold(pool, T)
                        pool.tensor_copy(ix[q // 4][:, :], T["slot_tok"][:, bass.ds(s, 4)]).then_inc(ix_done, 1)
                        pool.wait_ge(ix_done, h * 2 + q // 4 + 1)
                        hold(pool, T)
                    pool.indirect_dma_start(xg[q][:, :], None, T["x1_d"],
                                            bass.IndirectOffsetOnAxis(ap=ix[q // 4][:, q % 4:q % 4 + 1], axis=0)).then_inc(x_in[q], 16)
                steps(pool, n, 0, 8, body)

            @block.sync
            def _(sp):
                def body(s, h, q, on):
                    sp.wait_ge(y_done, s + 3)
                    sp.dma_start(T["y_d"][bass.ds(s * P, P), :], yo[q % 2][:, :]).then_inc(y_stored[q % 2], 16)
                steps(sp, n, 0, 4, body)
                for i in range(2):
                    sp.wait_ge(y_stored[i], 16 * (n // 2 + 1))

            @block.tensor
            def _(pe):
                pe.sem_inc(xT_full, 8)
                pe.sem_inc(h_full, 2)
                pe.sem_inc(ht_full, 2)
                pe.sem_inc(y_full, 2)
                pe.wait_ge(T["w0_in"], T["w0_n"])
                experts = Experts(pe, T, n)

                def body(s, h, q, on):
                    if on(0):
                        t = s
                        pe.wait_ge(x_in[q], (h + 1) * 16)
                        pe.wait_ge(xT_done, t + 1)
                        for k in range(KD):
                            mm = pe.transpose(pX[q % 2][:, k * P:(k + 1) * P], xg[q][:, k * P:(k + 1) * P],
                                              ident[:, :])
                        mm.then_inc(xT_full, 1)
                    experts.before(h, q)
                    if on(1):
                        t, r = s - 1, (q - 1) % 2
                        e = experts.of(q, 1)
                        pe.wait_ge(xT_done, t + 3)
                        pe.wait_ge(hh_done, t + 1)
                        for k in range(KD):
                            w = w13[:, bass.ds(e, 1), k, :].rearrange("p a n -> p (a n)")
                            mm = pe.matmul(pH[r][:, 0:D], xT[r][:, k, :], w, start=k == 0, stop=k == KD - 1)
                        mm.then_inc(h_full, 1)
                    experts.after(h, q)
                    if on(2):
                        t, r = s - 2, q % 2
                        pe.wait_ge(hh_done, t + 3)
                        pe.wait_ge(ht_done, t + 1)
                        pe.transpose(pHT[r][:, 0:P], hh[r][:, :], ident[:, :]).then_inc(ht_full, 1)
                    if on(3):
                        t, r = s - 3, (q - 3) % 2
                        e = experts.of(q, 3)
                        pe.wait_ge(ht_done, t + 3)
                        pe.wait_ge(y_done, t + 1)
                        w = w2[:, bass.ds(e, 1), :].rearrange("p a n -> p (a n)")
                        pe.matmul(pY[r][:, 0:D], hT[r][:, :], w, start=True, stop=True).then_inc(y_full, 1)
                steps(pe, n, 3, 8, body)

            @block.scalar
            def _(act):
                act.sem_inc(sg_done, 2)
                act.sem_inc(ht_done, 2)
                act.sem_inc(y_done, 2)
                for i in range(2):
                    act.sem_inc(y_stored[i], 16)

                def body(s, h, q, on):
                    if on(1):
                        t, r = s - 1, (q - 1) % 2
                        act.wait_ge(h_full, t + 3)
                        act.wait_ge(hh_done, t + 1)
                        act.activation(sg[r][:, :], pH[r][:, 0:IN0], ACT.Silu).then_inc(sg_done, 1)
                    if on(2):
                        t, r = s - 2, q % 2
                        act.wait_ge(ht_full, t + 3)
                        act.wait_ge(y_full, t + 1)
                        act.activation(hT[r][:, :], pHT[r][:, 0:P], ACT.Identity).then_inc(ht_done, 1)
                    if on(3):
                        t, r = s - 3, (q - 3) % 2
                        act.wait_ge(y_full, t + 3)
                        act.wait_ge(y_stored[r], (h * 2 + (q - 3) // 2 + 1) * 16)
                        act.activation(yo[r][:, :], pY[r][:, 0:D], ACT.Identity).then_inc(y_done, 1)
                steps(act, n, 3, 4, body)

            @block.vector
            def _(dve):
                dve.sem_inc(xT_done, 2)
                dve.sem_inc(hh_done, 2)

                def body(s, h, q, on):
                    if on(0):
                        t, r = s, q % 2
                        dve.wait_ge(xT_full, t + 9)
                        dve.wait_ge(h_full, t + 1)
                        dve.tensor_copy(xT[r][:, :, :].rearrange("p k n -> p (k n)"),
                                        pX[r][:, 0:D]).then_inc(xT_done, 1)
                    if on(1):
                        t, r = s - 1, (q - 1) % 2
                        dve.wait_ge(sg_done, t + 3)
                        dve.wait_ge(ht_full, t + 1)
                        dve.tensor_tensor(hh[r][:, :], sg[r][:, :], pH[r][:, IN0:2 * IN0], ALU.mult).then_inc(hh_done, 1)
                steps(dve, n, 3, 4, body)


def dispatch(nc, T, K, n_tiles, sigmoid, tok_id, pre):
    with ExitStack() as ctx:
        sb = lambda name, shape, dt=F32: ctx.enter_context(nc.sbuf_tensor(pre + name, shape, dt))
        sem = lambda name: ctx.enter_context(nc.semaphore(pre + name))
        TE = [P, NT, E_]
        score = sb("score", TE)
        work = sb("work", TE)
        cand = sb("cand", TE)
        oh = [sb(f"oh{k}", TE) for k in range(K)]
        top = sb("top", [P, NT])
        wsum = sb("wsum", [P, NT])
        mask = sb("mask", TE, F16)
        tot = sb("tot", [P, E_, NT])
        incl = sb("incl", [P, E_, NT])
        excl = sb("excl", [P, E_, NT])
        ones = sb("ones", [P, E_ * NT])
        cnt = sb("cnt", [P, E_])
        full = sb("full", [P, E_, NT])
        ntile = sb("ntile", [P, E_])
        tile_end = sb("tile_end", [P, E_])
        base = sb("base", [P, E_])
        place = sb("place", TE)
        pos = sb("pos", [P, NT, K])
        pos_lo = sb("pos_lo", [P, NT, K], I32)
        pos_hi = sb("pos_hi", [P, NT, K], I32)
        lo = sb("lo", [P, NT, K], F16)
        hi = sb("hi", [P, NT, K], F16)
        before = sb("before", [P, n_tiles, E_])
        texp = sb("texp", [P, n_tiles])
        padded = sb("padded", [1, n_tiles + 16])[:, :]
        word = sb("word", [1, n_tiles // 8 + 1, 2])[:, :, :]
        oh_lo = [sb(f"oh_lo{i}", [P, P, K], F16) for i in range(4)]
        oh_hi, oh_hw = ([sb(f"{nm}{i}", [P, n_tiles, K], F16) for i in range(4)] for nm in ("oh_hi", "oh_hw"))
        c32, c16 = T["c32"], T["c16"]
        rev, thr, iota = c32["rev"], c32["thr"], c32["iota"]
        io4, tri, one16 = c16["iota"], c16["tri"], c16["ones"]
        slot_w = T["slot_w"]

        dve_own, sig, mask_done, counted = sem("dve_own"), sem("sig"), sem("mask_done"), sem("counted")
        cent_done, exp_done = sem("cent_done"), sem("exp_done")
        lo_done, hi_done, hw_done = sem("lo_done"), sem("hi_done"), sem("hw_done")
        hot_used, inv_done = sem("hot_used"), sem("inv_done")

        bcE = lambda ap: ap.unsqueeze(2).broadcast_to(TE)
        bcT = lambda ap: ap.unsqueeze(1).broadcast_to(TE)

        with ExitStack() as pctx, nc.Block() as block:
            pW, pN, pI = (pctx.enter_context(nc.psum_tensor(pre + nm, [P, 512], F32)) for nm in ("pW", "pN", "pI"))

            @block.scalar
            def _(act):
                act.sem_inc(hw_done, 4)
                if sigmoid:
                    act.activation(score[:, :, :], T["logits"][:, :, :], ACT.Sigmoid).then_inc(exp_done, 1)
                else:
                    act.wait_ge(cent_done, 1)
                    act.activation(work[:, :, :], cand[:, :, :], ACT.Exp).then_inc(exp_done, 1)

                def body(t, h, q, on):
                    act.wait_ge(hi_done, t + 1)
                    act.wait_ge(hot_used, t + 1)
                    hold(act, T)
                    act.activation(oh_hw[q][:, :, :], oh_hi[q][:, :, :], ACT.Identity,
                                   scale=tok_id[:, bass.ds(t, 1)]).then_inc(hw_done, 1)
                steps(act, NT, 0, 4, body)

            @block.vector
            def _(dve):
                own = Chain(dve, dve_own)
                tt = lambda out, a, b, op: own.step(dve.tensor_tensor(out, a, b, op))
                if sigmoid:
                    dve.wait_ge(exp_done, 1)
                    tt(work[:, :, :], score[:, :, :], bcT(T["route_b"][:, :]), ALU.add)
                else:
                    lg = T["logits"]
                    tt(lg[:, :, :], lg[:, :, :], bcT(T["route_b"][:, :]), ALU.add)
                    own.step(dve.tensor_reduce(top[:, :], lg[:, :, :], AX.X, ALU.max))
                    dve.tensor_tensor(cand[:, :, :], lg[:, :, :], bcE(top[:, :]), ALU.subtract).then_inc(cent_done, 1)
                    dve.wait_ge(exp_done, 1)
                    own.step(dve.tensor_reduce(wsum[:, :], work[:, :, :], AX.X, ALU.add))
                    own.step(dve.reciprocal(wsum[:, :], wsum[:, :]))
                    tt(score[:, :, :], work[:, :, :], bcE(wsum[:, :]), ALU.mult)
                    own.step(dve.tensor_copy(work[:, :, :], score[:, :, :]))
                for k in range(K):
                    own.step(dve.tensor_reduce(top[:, :], work[:, :, :], AX.X, ALU.max))
                    tt(cand[:, :, :], work[:, :, :], bcE(top[:, :]), ALU.is_equal)
                    tt(cand[:, :, :], cand[:, :, :], bcT(rev), ALU.mult)
                    own.step(dve.tensor_reduce(top[:, :], cand[:, :, :], AX.X, ALU.max))
                    tt(oh[k][:, :, :], bcT(rev), bcE(top[:, :]), ALU.is_equal)
                    if k < K - 1:
                        own.step(dve.scalar_tensor_tensor(out=work[:, :, :], in0=oh[k][:, :, :], scalar=-1e30,
                                                          in1=work[:, :, :], op0=ALU.mult, op1=ALU.add))
                for k in range(1, K):
                    src = oh[0] if k <= 1 else cand
                    if k == K - 1:
                        dve.tensor_tensor(mask[:, :, :], src[:, :, :], oh[k][:, :, :], ALU.add).then_inc(mask_done, 1)
                    else:
                        tt(cand[:, :, :], src[:, :, :], oh[k][:, :, :], ALU.add)
                dve.wait_ge(mask_done, 1)
                for k in range(K):
                    tt(cand[:, :, :], oh[k][:, :, :], score[:, :, :], ALU.mult)
                    own.step(dve.tensor_reduce(slot_w[:, :, k], cand[:, :, :], AX.X, ALU.add))
                own.step(dve.tensor_reduce(wsum[:, :], slot_w[:, :, 0:K], AX.X, ALU.add))
                if not sigmoid:
                    own.step(dve.tensor_scalar(wsum[:, :], wsum[:, :], 1e-9, None, ALU.max))
                own.step(dve.reciprocal(wsum[:, :], wsum[:, :]))
                if sigmoid:
                    own.step(dve.tensor_scalar(wsum[:, :], wsum[:, :], 2.5, None, ALU.mult))
                tt(slot_w[:, :, 0:K], slot_w[:, :, 0:K], wsum[:, :].unsqueeze(2).broadcast_to([P, NT, K]), ALU.mult)
                own.step(dve.memset(ones[:, :], 1.0))
                own.step(dve.memset(padded, 0.0))
                dve.wait_ge(counted, 1)
                own.step(dve.tensor_copy(tot[:, :, :], pN[:, :].rearrange("p (t e) -> p e t", e=E_)))
                own.step(dve.tensor_tensor_scan(incl[:, :, :].rearrange("p e t -> p (e t)"), ones[:, :],
                                                tot[:, :, :].rearrange("p e t -> p (e t)"), 0.0, ALU.mult, ALU.add))
                tt(excl[:, :, :], incl[:, :, :], tot[:, :, :], ALU.subtract)
                tt(cnt[:, :], incl[:, :, NT - 1], excl[:, :, 0], ALU.subtract)
                tt(full[:, :, :], cnt[:, :].unsqueeze(2).broadcast_to([P, E_, NT]),
                   thr.unsqueeze(1).broadcast_to([P, E_, NT]), ALU.is_gt)
                own.step(dve.tensor_reduce(ntile[:, :], full[:, :, :], AX.X, ALU.add))
                own.step(dve.tensor_tensor_scan(tile_end[:, :], ones[:, 0:E_], ntile[:, :], 0.0, ALU.mult, ALU.add))
                tt(before[:, :, :], iota[:, 0:n_tiles].unsqueeze(2).broadcast_to([P, n_tiles, E_]),
                   tile_end[:, :].unsqueeze(1).broadcast_to([P, n_tiles, E_]), ALU.is_ge)
                own.step(dve.tensor_reduce(texp[:, :], before[:, :, :], AX.X, ALU.add))
                own.step(dve.tensor_scalar(padded[:, Experts.BACK:Experts.BACK + n_tiles], texp[0:1, :], float(E_ - 1), None, ALU.min))
                n_words, six = n_tiles // 8 + 1, Experts.IN
                at = [bass.AP(padded.tensor, padded.offset + j, [padded.ap[0], [8, n_words], [six, 2]]) for j in range(six)]
                for j in range(six - 2, -1, -1):
                    out = word if j else T["tile_exp"][:, 0:2 * n_words].rearrange("p (n w) -> p n w", w=2)
                    own.step(dve.scalar_tensor_tensor(out=out, in0=at[six - 1] if j == six - 2 else word, scalar=float(E_),
                                                      in1=at[j], op0=ALU.mult, op1=ALU.add))
                tt(base[:, :], tile_end[:, :], ntile[:, :], ALU.subtract)
                own.step(dve.scalar_tensor_tensor(out=base[:, :], in0=base[:, :], scalar=float(P),
                                                  in1=excl[:, :, 0], op0=ALU.mult, op1=ALU.subtract))
                tt(place[:, :, :], excl[:, :, :].rearrange("p e t -> p t e"), bcT(base[:, :]), ALU.add)
                tt(place[:, :, :], place[:, :, :], pW[:, :].rearrange("p (t e) -> p t e", e=E_), ALU.add)
                for k in range(K):
                    tt(cand[:, :, :], oh[k][:, :, :], place[:, :, :], ALU.mult)
                    own.step(dve.tensor_reduce(pos[:, :, k], cand[:, :, :], AX.X, ALU.add))
                pi = T["slot_of"][:, :, 0:K]
                own.step(dve.tensor_copy(pi, pos[:, :, :]))
                own.step(dve.tensor_scalar(pos_lo[:, :, :], pi, P - 1, None, ALU.bitwise_and))
                own.step(dve.tensor_scalar(pos_hi[:, :, :], pi, 7, None, ALU.logical_shift_right))
                own.step(dve.tensor_copy(lo[:, :, :], pos_lo[:, :, :]))
                own.step(dve.tensor_copy(hi[:, :, :], pos_hi[:, :, :]))
                def body(t, h, q, on):
                    dve.wait_ge(hot_used, t + 1)
                    dve.tensor_tensor(oh_lo[q][:, :, :], io4[:, 0:P, 0:K],
                                      lo[:, bass.ds(t, 1), :].broadcast_to([P, P, K]), ALU.is_equal).then_inc(lo_done, 1)
                    dve.wait_ge(hw_done, t + 1)
                    dve.tensor_tensor(oh_hi[q][:, :, :], io4[:, 0:n_tiles, 0:K],
                                      hi[:, bass.ds(t, 1), :].broadcast_to([P, n_tiles, K]), ALU.is_equal).then_inc(hi_done, 1)
                steps(dve, NT, 0, 4, body)
                dve.wait_ge(inv_done, 1)
                own.step(dve.tensor_scalar(T["slot_tok"][:, 0:n_tiles], pI[:, 0:n_tiles], float(MID_ID), None, ALU.add))

            @block.tensor
            def _(pe):
                pe.sem_inc(hot_used, 4)
                pe.wait_ge(mask_done, 1)
                m = mask[:, :, :].rearrange("p t e -> p (t e)")
                pe.matmul(pW[:, :], tri, m, start=True, stop=True)
                pe.matmul(pN[:, :], one16, m, start=True, stop=True).then_inc(counted, 1)

                def add(t, q, first=False, last=False):
                    pe.wait_ge(lo_done, t + 1)
                    pe.wait_ge(hw_done, t + 5)
                    for k in range(K):
                        mm = pe.matmul(pI[:, 0:n_tiles], oh_lo[q][:, :, k], oh_hw[q][:, :, k],
                                       start=first and k == 0, stop=last and k == K - 1)
                    mm.then_inc(inv_done if last else hot_used, 1)

                for q in range(4):
                    add(q, q, first=q == 0)
                with pe.Fori(1, NT // 4 - 1) as h:
                    for q in range(4):
                        add(h * 4 + q, q)
                for q in range(4):
                    add(NT - 4 + q, q, last=q == 3)


def combine(nc, T, K, acc, out_rows, first, pre):
    LAG = 4 if first else 5
    A = 3 if first else 0
    X = A + LAG + 1
    with ExitStack() as ctx:
        sb = lambda name, shape, dt=F32: ctx.enter_context(nc.sbuf_tensor(pre + name, shape, dt))
        S = Sems(nc, ctx, pre)
        ix = [sb(f"ix{i}", [P, 4, K], I32) for i in range(2)]
        if first:
            area = T["area"]
            yg = [area[:, i * K * D:(i + 1) * K * D].rearrange("p (k d) -> p k d", k=K) for i in range(4)]
            raw, tc_, ts_ = ([area[:, (4 * K + 4 * j + 2 * i) * D:(4 * K + 4 * j + 2 * i + 2) * D] for i in range(2)]
                             for j in range(3))
            lhs = [area[:, (4 * K + 12 + i) * D:(4 * K + 13 + i) * D].rearrange("p (k n) -> p k n", k=KD) for i in range(2)]
            w = T["w_qkv"][:, 0:KD * 3 * D].rearrange("p (k n) -> p k n", k=KD)
            bias = T["w_qkv"][:, KD * 3 * D:(KD + 1) * 3 * D]
            qk, v, cs = T["qk"], T["v"], T["rope"]
            qk_full, v_full, raw_done, v_done = S("qk_full"), S("v_full"), S("raw_done"), S("v_done")
            ts_done, rot0, rot1, rot_done = S("ts_done"), S("rot0"), S("rot1"), S("rot_done")
            ts0 = S("ts0")
            halves = lambda ap: ap.rearrange("p (a h n) -> p a h n", a=2, h=2)
        else:
            yg = [sb(f"yg{i}", [P, K, D]) for i in range(4)]
        sm = [sb(f"sm{i}", [P, D]) for i in range(8)]
        st = [sb(f"st{i}", [P, 6]) for i in range(2)]
        mv = sb("mv", [P, 8, 2])
        var = [sb(f"var{i}", [P, 4]) for i in range(2)]
        rs = [sb(f"rs{i}", [P, 4]) for i in range(2)]
        xo = [sb(f"xo{i}", [P, D]) for i in range(4)]
        ident = T["ident"]
        own_sem, ix_done, summed = S("own"), S("ix_done"), S("summed")
        y_in = [S(f"y_in{i}") for i in range(4)]
        var_done, rs_done = S("var"), S("rs")
        xo_done, xo_turned, xT_done = S("xo"), S("turned"), S("xT")
        stored = [S(f"stored{i}") for i in range(4)]
        if first:
            xc, sg, hh, hT = ([sb(f"{nm}{i}", [P, w]) for i in range(2)]
                              for nm, w in (("xc", D), ("sg", IN0), ("hh", IN0), ("hT", P)))
            xcT = [sb(f"xcT{i}", [P, KD, P]) for i in range(2)]
            xc_done, xc_turned, xcT_done = S("xc"), S("xc_turned"), S("xcT")
            h_full, sg_done, hh_done = S("h_full"), S("sg"), S("hh")
            hh_turned, hT_done, y_full, y_added = S("hh_turned"), S("hT"), S("y_full"), S("y_added")

        with ExitStack() as pctx, nc.Block() as block:
            ps = lambda nm, n: [pctx.enter_context(nc.psum_tensor(f"{pre}{nm}{i}", [P, 512], F32)) for i in range(n)]
            if first:
                (pX,), (pC,), pQ = ps("pX", 1), ps("pC", 1), ps("pQ", 2)
                (pH,), (pHT,), (pY,), (pV,) = (ps(nm, 1) for nm in ("pH", "pHT", "pY", "pV"))

            @block.gpsimd
            def _(pool):
                if first:
                    pool.sem_inc(ts_done, 2)

                def body(s, h, q, on):
                    g = h * 2 + q // 4
                    if on(0):
                        if q % 4 == 0:
                            pool.wait_ge(summed, s)
                            hold(pool, T)
                            pool.tensor_copy(ix[q // 4][:, :, :], T["slot_of"][:, bass.ds(s, 4), 0:K]).then_inc(ix_done, 1)
                            pool.wait_ge(ix_done, g + 1)
                        pool.wait_ge(summed, s + 1)
                        hold(pool, T)
                        for k in range(K):
                            pool.indirect_dma_start(yg[q % 4][:, k, :], None, T["y_d"],
                                                    bass.IndirectOffsetOnAxis(ap=ix[q // 4][:, q % 4, k:k + 1], axis=0)
                                                    ).then_inc(y_in[q % 4], 16)
                    if q % 4 == 2 and on(4):
                        pool.wait_ge(var_done, g)
                        r = (q // 4 - 1) % 2
                        pool.tensor_tensor(rs[r][:, :], var[r][:, :], T["half"][:, 0:4], ALU.pow).then_inc(rs_done, 1)
                    if first and on(X + 3):
                        t, r = s - X - 3, (q - X - 3) % 2
                        pool.wait_ge(T["rope_in"], T["rope_n"])
                        pool.wait_ge(raw_done, t + 3)
                        pool.wait_ge(rot_done, t + 1)
                        hold(pool, T)
                        x, o = halves(raw[r]), halves(ts_[r])
                        sin = cs[:, bass.ds(t, 1), 1, :].broadcast_to([P, 2, D // 2])
                        pool.tensor_tensor(o[:, :, 0, :], x[:, :, 1, :], sin, ALU.mult).then_inc(ts0, 1)
                        pool.tensor_tensor(o[:, :, 1, :], x[:, :, 0, :], sin, ALU.mult).then_inc(ts_done, 1)
                        pool.wait_ge(ts0, t + 1)
                        pool.wait_ge(ts_done, t + 3)
                steps(pool, NT, X + 3 if first else LAG, 8, body)

            @block.vector
            def _(dve):
                dve.sem_inc(summed, 4)
                dve.sem_inc(xo_done, 8)
                if first:
                    dve.sem_inc(hh_done, 2)
                    dve.sem_inc(y_added, 2)

                    for sm_ in (raw_done, v_done, rot0, rot1, rot_done):
                        dve.sem_inc(sm_, 2)
                    dve.wait_ge(T["x1_in"], 16)

                def normalised(s, h, q, on):
                    if on(A + LAG):
                        t, r, g = s - A - LAG, (q - A - LAG) % 8, (q - A - LAG) // 4
                        dve.wait_ge(rs_done, h * 2 + g + 1)
                        dve.wait_ge(stored[r % 4], (h * 2 + g + 1) * 16)
                        if first:
                            dve.wait_ge(xo_turned, t + 1)
                        dve.tensor_scalar(xo[r % 4][:, :], sm[r][:, :], mv[:, r, 0:1], rs[r // 4][:, r % 4:r % 4 + 1],
                                          ALU.subtract, ALU.mult).then_inc(xo_done, 1)

                def attention_part(i, s, q, on):
                    if i in (1, 3) and on(X + 4):
                        t, r = s - X - 4, (q - X - 4) % 2
                        c, x = halves(tc_[r]), halves(ts_[r])
                        if i == 1:
                            dve.wait_ge(T["rope_in"], T["rope_n"])
                            dve.wait_ge(raw_done, t + 3)
                            dve.wait_ge(rot_done, t + 1)
                            dve.wait_ge(rot1, t + 1)
                            cos = cs[:, bass.ds(t, 1), 0, :].broadcast_to([P, 4, D // 2])
                            dve.tensor_tensor(tc_[r].rearrange("p (a n) -> p a n", a=4),
                                              raw[r].rearrange("p (a n) -> p a n", a=4), cos, ALU.mult).then_inc(rot0, 1)
                        else:
                            dve.wait_ge(rot0, t + 3)
                            dve.wait_ge(ts_done, t + 3)
                            o = qk[:, bass.ds(t, 1), :].rearrange("p b (a h n) -> p (b a) h n", a=2, h=2)
                            dve.tensor_tensor(o[:, :, 0, :], c[:, :, 0, :], x[:, :, 0, :], ALU.subtract).then_inc(rot1, 1)
                            dve.tensor_tensor(o[:, :, 1, :], c[:, :, 1, :], x[:, :, 1, :], ALU.add).then_inc(rot_done, 1)
                    if i in (0, 2) and on(X + 2):
                        t, r = s - X - 2, (q - X - 2) % 2
                        dve.wait_ge(T["w_qkv_in"], 32)
                        if i == 2:
                            dve.wait_ge(qk_full, t + 3)
                            dve.wait_ge(rot0, t + 1)
                            dve.wait_ge(ts_done, t + 1)
                            dve.tensor_tensor(raw[r], pQ[r][:, :], bias[:, 0:2 * D], ALU.add).then_inc(raw_done, 1)
                        else:
                            dve.wait_ge(v_full, t + 3)
                            dve.tensor_tensor(v[:, bass.ds(t, 1), :].rearrange("p a d -> p (a d)"), pV[:, 0:D],
                                              bias[:, 2 * D:3 * D], ALU.add).then_inc(v_done, 1)

                def body(s, h, q, on):
                    if first and on(1):
                        t, r = s - 1, (q - 1) % 2
                        dve.wait_ge(sg_done, t + 3)
                        dve.wait_ge(hh_turned, t + 1)
                        dve.tensor_tensor(hh[r][:, :], sg[r][:, :], pH[:, IN0:2 * IN0], ALU.mult).then_inc(hh_done, 1)
                    if on(A):
                        t, r = s - A, (q - A) % 8
                        own = Chain(dve, own_sem, t, K + 1)
                        g = (q - A) // 4
                        dve.wait_ge(xo_done, t + 1)
                        src = acc[:, bass.ds(t, 1), :].rearrange("p a d -> p (a d)")
                        if first:
                            dve.wait_ge(y_full, t + 3)
                            dve.tensor_tensor(sm[r][:, :], pY[:, 0:D], src, ALU.add).then_inc(y_added, 1)
                            attention_part(0, s, q, on)
                            dve.wait_ge(y_added, t + 3)
                            src = sm[r][:, :]
                        dve.wait_ge(y_in[r % 4], (h * 2 + g + 1) * 16 * K)
                        for k in range(K):
                            ins = dve.scalar_tensor_tensor(
                                out=sm[r][:, :], in0=yg[r % 4][:, k, :],
                                scalar=T["slot_w"][:, bass.ds(t, 1), k:k + 1].rearrange("p a k -> p (a k)"),
                                in1=src, op0=ALU.mult, op1=ALU.add)
                            src = sm[r][:, :]
                            if k < K - 1:
                                own.mark(ins)
                            else:
                                ins.then_inc(summed, 1)
                            if first and k + 1 in (1, 2, 3):
                                attention_part(k + 1, s, q, on)
                            if k < K - 1:
                                own.settle()
                        dve.wait_ge(summed, t + 5)
                        own.mark(dve.bn_stats(st[r % 2][:, :], sm[r][:, :]))
                        normalised(s, h, q, on)
                        own.settle()
                        hold(dve, T)
                        own.step(dve.bn_aggr(mv[:, r, :], st[r % 2][:, :]))
                        if r % 4 == 3:
                            n = r // 4
                            dve.tensor_scalar(var[n][:, :], mv[:, n * 4:n * 4 + 4, 1], EPS, None, ALU.add).then_inc(var_done, 1)
                    if not on(A):
                        normalised(s, h, q, on)
                    if first and not on(A):
                        for i in range(4):
                            attention_part(i, s, q, on)
                steps(dve, NT, X + 4 if first else A + LAG, 8, body)
                if first:
                    dve.wait_ge(rot1, BL + 2)
                    dve.wait_ge(v_done, BL + 2)
                    dve.wait_ge(rot_done, BL + 2)

            @block.sync
            def _(sp):
                for i in range(4):
                    sp.sem_inc(stored[i], 16)
                if first:
                    n = KD * 3 * D
                    sp.dma_start(T["w_qkv"][:, 0:n].rearrange("p (k n) -> p k n", k=KD), T["w_qkv_d"].rearrange("(k p) n -> p k n", p=P)
                                 ).then_inc(T["w_qkv_in"], 16)
                    sp.dma_start(T["w_qkv"][:, n:n + 3 * D], T["b_qkv_d"].partition_broadcast(P)).then_inc(T["w_qkv_in"], 16)
                    for i in range(0, BL, 8):
                        sp.dma_start(T["rope"][:, i:i + 8, :, :], T["rope_d"][:, i:i + 8, :, :]).then_inc(T["rope_in"], 16)

                def body(s, h, q, on):
                    sp.wait_ge(xo_done, s + 9)
                    sp.dma_start(out_rows(s), xo[q][:, :]).then_inc(stored[q], 16)
                steps(sp, NT, 0, 4, body)
                for i in range(4):
                    sp.wait_ge(stored[i], 16 * (NT // 4 + 1))

            if first:
                @block.tensor
                def _(pe):
                    pe.sem_inc(xo_turned, 4)
                    for s in (xc_turned, h_full, hh_turned, y_full, qk_full, v_full):
                        pe.sem_inc(s, 2)
                    pe.wait_ge(T["w_ins"], T["w_ns"])

                    def body(s, h, q, on):
                        if on(0):
                            pe.wait_ge(xc_done, s + 1)
                            pe.wait_ge(xcT_done, s + 1)
                            for k in range(KD):
                                mm = pe.transpose(pC[:, k * P:(k + 1) * P], xc[q % 2][:, k * P:(k + 1) * P], ident[:, :])
                            mm.then_inc(xc_turned, 1)
                        if on(1):
                            t, r = s - 1, (q - 1) % 2
                            pe.wait_ge(xcT_done, t + 2)
                            pe.wait_ge(hh_done, t + 2)
                            for k in range(KD):
                                mm = pe.matmul(pH[:, 0:D], xcT[r][:, k, :], T["w13s"][:, k, :], start=k == 0, stop=k == KD - 1)
                            mm.then_inc(h_full, 1)
                        if on(2):
                            t, r = s - 2, q % 2
                            pe.wait_ge(hh_done, t + 3)
                            pe.wait_ge(hT_done, t + 2)
                            pe.transpose(pHT[:, 0:P], hh[r][:, :], ident[:, :]).then_inc(hh_turned, 1)
                        if on(3):
                            t, r = s - 3, (q - 3) % 2
                            pe.wait_ge(hT_done, t + 3)
                            pe.wait_ge(y_added, t + 2)
                            pe.matmul(pY[:, 0:D], hT[r][:, :], T["w2s"][:, :], start=True, stop=True).then_inc(y_full, 1)
                        if on(A + LAG + 1):
                            t, r = s - A - LAG - 1, (q - A - LAG - 1) % 4
                            pe.wait_ge(xo_done, t + 9)
                            pe.wait_ge(xT_done, t + 1)
                            for k in range(KD):
                                mm = pe.transpose(pX[:, k * P:(k + 1) * P], xo[r][:, k * P:(k + 1) * P], ident[:, :])
                            mm.then_inc(xo_turned, 1)
                        if on(X + 1):
                            t, r = s - X - 1, (q - X - 1) % 2
                            pe.wait_ge(T["w_qkv_in"], 32)
                            pe.wait_ge(xT_done, t + 2)
                            pe.wait_ge(raw_done, t + 1)
                            for k in range(KD):
                                mm = pe.matmul(pQ[r][:, :], lhs[r][:, k, :], w[:, k, 0:2 * D], start=k == 0, stop=k == KD - 1)
                            mm.then_inc(qk_full, 1)
                            pe.wait_ge(v_done, t + 2)
                            for k in range(KD):
                                mm = pe.matmul(pV[:, 0:D], lhs[r][:, k, :], w[:, k, 2 * D:3 * D], start=k == 0, stop=k == KD - 1)
                            mm.then_inc(v_full, 1)
                    steps(pe, NT, X + 1, 4, body)

                @block.scalar
                def _(act):
                    for s, n in ((xcT_done, 1), (sg_done, 2), (hT_done, 2), (xT_done, 1)):
                        act.sem_inc(s, n)
                    act.wait_ge(T["x1_in"], 16)

                    def body(s, h, q, on):
                        if on(0):
                            act.wait_ge(xc_turned, s + 1)
                            hold(act, T)
                            act.activation(xc[q % 2][:, :], acc[:, bass.ds(s, 1), :].rearrange("p a d -> p (a d)"),
                                           ACT.Identity).then_inc(xc_done, 1)
                            act.wait_ge(xc_turned, s + 3)
                            act.wait_ge(h_full, s + 1)
                            act.activation(xcT[q % 2][:, :, :].rearrange("p k n -> p (k n)"), pC[:, 0:D],
                                           ACT.Identity).then_inc(xcT_done, 1)
                        if on(1):
                            t, r = s - 1, (q - 1) % 2
                            act.wait_ge(h_full, t + 3)
                            act.wait_ge(hh_done, t + 1)
                            act.activation(sg[r][:, :], pH[:, 0:IN0], ACT.Silu).then_inc(sg_done, 1)
                        if on(2):
                            t, r = s - 2, q % 2
                            act.wait_ge(hh_turned, t + 3)
                            act.wait_ge(y_full, t + 1)
                            act.activation(hT[r][:, :], pHT[:, 0:P], ACT.Identity).then_inc(hT_done, 1)
                        if on(A + LAG + 1):
                            t, r = s - A - LAG - 1, (q - A - LAG - 1) % 2
                            act.wait_ge(xo_turned, t + 5)
                            act.wait_ge(v_full, t + 1)
                            hold(act, T)
                            act.activation(lhs[r][:, :, :],
                                           pX[:, 0:D].rearrange("p (k n) -> p k n", k=KD), ACT.Identity).then_inc(xT_done, 1)
                    steps(act, NT, A + LAG + 1, 4, body)
                    act.wait_ge(xT_done, NT + 1)


H, DH = 16, 16
BL = 32
SEG = 4
LOCAL = (1, 2, 3)
FAR = tuple(range(5))
POOL_SEGS = 3
N0 = 10
PAIRS0 = [(a, b) for a in range(SEG) for b in range(a + 1)]


def far_count(t, s, h):
    return sum(1 for x in range(L.bit_length() - 1)
               if t // 2 ** (x + 2) == s // 2 ** (x + 2) and t % 2 ** x == h % 2 ** x == s % 2 ** x)


def local_groups():
    out, first = [], 0
    for lv in LOCAL:
        r = 2 ** lv
        for rho in range(r):
            nh, ns = H // r, BL // (SEG * r)
            out.append((r, rho, nh, ns, first))
            first += ns * 4 * nh
    return out, first


GROUPS, NC = local_groups()


def far_groups():
    out, first = [], 0
    for lv in FAR:
        r = 2 ** lv
        ns = (L // H) // (SEG * r)
        out.append((r, ns, first))
        first += ns * 4
    return out, first


FGROUPS, NF = far_groups()
NJ = L // H


def count_tables():
    c0 = np.zeros((P, BL // SEG, N0, H), np.float32)
    cc = np.zeros((P, NC), np.float32)
    for p in range(L // BL):
        for s in range(BL // SEG):
            for n, (a, b) in enumerate(PAIRS0):
                for h in range(H):
                    t = BL * p + SEG * s
                    c0[p, s, n, h] = far_count(t + a, t + b, h)
        for r, rho, nh, ns, first in GROUPS:
            v = cc[p, first:first + ns * 4 * nh].reshape(ns, 2, 2, nh)
            for s in range(ns):
                for a in range(2):
                    for b in range(2):
                        for k in range(nh):
                            t = BL * p + s * SEG * r + rho
                            v[s, a, b, k] = far_count(t + (2 + a) * r, t + b * r, rho + r * k)
    for q in range(1, B):
        n = L // BL
        c0[q * n:(q + 1) * n], cc[q * n:(q + 1) * n] = c0[:n], cc[:n]
    cf = np.zeros((B * H, NF), np.float32)
    for h in range(H):
        for r, ns, first in FGROUPS:
            v = cf[h, first:first + ns * 4].reshape(ns, 2, 2)
            for s in range(ns):
                for a in range(2):
                    for b in range(2):
                        j = s * SEG * r
                        v[s, a, b] = far_count(H * (j + (2 + a) * r) + h, H * (j + b * r) + h, h)
    for q in range(1, B):
        cf[q * H:(q + 1) * H] = cf[:H]
    return c0.reshape(P, -1), cc, cf


def rope_tables():
    freq = (1.0 / np.float32(15000.0) ** (np.arange(0, D, 2, dtype=np.float32) / np.float32(D))).astype(np.float32)
    ang = np.arange(L, dtype=np.float32)[:, None] * freq[None, :]
    both = np.stack([np.cos(ang), np.sin(ang)], 1).astype(np.float32)
    return np.tile(both.reshape(L // BL, BL, 2, D // 2), (B, 1, 1, 1)).copy()


def attend(nc, T, W):
    with ExitStack() as ctx:
        sb = lambda name, shape, dt=F32: ctx.enter_context(nc.sbuf_tensor("at_" + name, shape, dt))
        sem = lambda name: ctx.enter_context(nc.semaphore("at_" + name))
        NS = BL // SEG
        HR = B * H
        qk, v = T["qk"], T["v"]
        n0 = NS * N0 * H
        cnt0, cntc, sc = T["w_qkv"][:, 0:n0], T["w_qkv"][:, n0:n0 + NC], T["w_qkv"][:, n0 + NC:n0 + 2 * NC]
        cntf = sb("cntf", [HR, NF])
        s0 = sb("s0", [P, NS, N0, H])
        scx = sb("scx", [P, NC // 2])
        M = sb("M", [P, BL, H])
        Z = sb("Z", [P, BL, H])
        prod = [sb(f"prod{i}", [P, SEG * D]) for i in range(2)]
        prod_p = [T["prodp"][:, i * SEG * D:(i + 1) * SEG * D] for i in range(2)]
        mc = sb("mc", [P, NC // 2])
        far = T["far"]
        fq = T["fq"]
        fs = sb("fs", [HR, NF])
        fx = sb("fx", [HR, NF // 2])
        fm = sb("fm", [HR, NF // 2])
        fo = sb("fo", [HR, NJ, DH + 2])
        fb = sb("fb", [P, 2, H, DH + 2])
        fg = sb("fg", [P, 2, H])
        pc = T["prodc"]
        pf = T["prodf"][0:HR, :]
        o = T["o"]
        tabs, own_sem, pool_own = sem("tabs"), sem("own"), sem("pool_own")
        far_done, far_st, far_in, fo_done, fo_st, fb_in = (sem("far_done"), sem("far_st"), sem("far_in"),
                                                           sem("fo_done"), sem("fo_st"), sem("fb_in"))
        pc_done, pv_go, pv_done = sem("pc_done"), sem("pv_go"), sem("pv_done")
        p_done, p_used, s0_go, q_done, q_used = (sem("p_done"), sem("p_used"), sem("s0_go"), sem("q_done"), sem("q_used"))
        e_req, e_done, k_read = sem("e_req"), sem("e_done"), sem("k_read")
        fq_, fk_, fv_ = (fq[:, :, i, :] for i in range(3))

        def rows_of(ap, r, rho, ns, nh, a):
            t0 = (2 + a) * r + rho
            return ap[:, t0:t0 + (ns - 1) * SEG * r + 1:SEG * r, rho:H:r]

        with nc.Block() as block:
            @block.sync
            def _(sp):
                for dst, src in ((cnt0[:, :], W["cnt0"]), (cntc[:, :], W["cntc"]), (cntf[:, :], W["cntf"])):
                    sp.dma_start(dst, src).then_inc(tabs, 16)
                sp.wait_ge(far_done, 6)
                sp.dma_start(T["far_d"].rearrange("p a h c d -> p (a h c d)"),
                             far[:, :, :, :, :].rearrange("p a h c d -> p (a h c d)")).then_inc(far_st, 16)
                sp.wait_ge(far_st, 16)
                src = T["far_d"].rearrange("(b n) a h c d -> b h n a (c d)", b=B)
                for b in range(B):
                    sp.dma_start(fq[b * H:(b + 1) * H, :, :, :].rearrange("h (n a) c d -> h n a (c d)", a=2),
                                 src[b]).then_inc(far_in, 16)
                sp.wait_ge(fo_done, 1)
                sp.dma_start(T["fo_d"].rearrange("h j c -> h (j c)"), fo[:, :, :].rearrange("h j c -> h (j c)")).then_inc(fo_st, 16)
                sp.wait_ge(fo_st, 16)
                back = T["fo_d"].rearrange("(b h) (n a) c -> b n a h c", b=B, a=2)
                n = L // BL
                for b in range(B):
                    for a in range(2):
                        sp.dma_start(fb[b * n:(b + 1) * n, a, :, :], back[b][:, a]).then_inc(fb_in, 16)
                sp.wait_ge(k_read, 1)
                sp.wait_ge(pc_done, 4 * len(GROUPS))
                sp.dma_start(T["x2b"], T["x2_d"].rearrange("(p i) d -> p i d", i=BL)).then_inc(T["x2_in"], 16)
                sp.wait_ge(fb_in, 16 * B * 2)

            @block.scalar
            def _(act):
                act.wait_ge(e_req, 1)
                act.activation(fs[:, :], fs[:, :], ACT.Exp).then_inc(e_done, 1)
                act.wait_ge(e_req, 2)
                act.activation(fg[:, :, :], fg[:, :, :], ACT.Exp).then_inc(e_done, 1)
                act.activation(s0[:, :, :, :], s0[:, :, :, :], ACT.Exp).then_inc(e_done, 1)
                act.wait_ge(e_req, 3)
                act.activation(sc[:, :], sc[:, :], ACT.Exp).then_inc(e_done, 1)

            qh = qk[:, :, 0:D].rearrange("p t (h d) -> p t h d", h=H)
            kh = qk[:, :, D:2 * D].rearrange("p t (h d) -> p t h d", h=H)
            vh = v[:, :, :].rearrange("p t (h d) -> p t h d", h=H)

            dve_rows = [(g, a) for g in range(NS - POOL_SEGS) for a in range(SEG)]
            pool_rows = [(g, a) for g in range(NS - POOL_SEGS, NS) for a in range(SEG)]

            def score_product(eng, buf, g, a):
                n, t = a + 1, g * SEG
                return eng.tensor_tensor(buf[:, 0:n * D].rearrange("p (b x) -> p b x", b=n),
                                         qk[:, t + a:t + a + 1, 0:D].broadcast_to([P, n, D]),
                                         qk[:, t:t + n, D:2 * D], ALU.mult)

            def value_product(eng, buf, g, a):
                f, n, t = a * (a + 1) // 2, a + 1, g * SEG
                out = o[:, t, :] if a == 0 else buf[:, 0:n * D]
                return eng.tensor_tensor(out.rearrange("p (n d) -> p n d", d=DH),
                                         s0[:, g, f:f + n, :].rearrange("p b h -> p (b h)").unsqueeze(2).broadcast_to([P, n * H, DH]),
                                         v[:, t:t + n, :].rearrange("p b (h d) -> p (b h) d", h=H), ALU.mult)

            def key_rows(ap, r, rho, ns, b):
                t0 = b * r + rho
                return ap[:, t0:t0 + (ns - 1) * SEG * r + 1:SEG * r, rho:H:r]

            @block.gpsimd
            def _(pool):
                own = Chain(pool, pool_own)
                for a in range(2):
                    for c, src in enumerate((qk[:, :, 0:D], qk[:, :, D:2 * D], v[:, :, :])):
                        w = 2 * D if c < 2 else D
                        full = qk if c < 2 else v
                        flat = full[:, :, :].rearrange("p t n -> p (t n)")
                        off = a * H * w + (D if c == 1 else 0)
                        diag = flat[:, off:off + (H - 1) * (w + DH) + DH]
                        diag = bass.AP(diag.tensor, diag.offset, [diag.ap[0], [w + DH, H], [1, DH]])
                        pool.tensor_copy(far[:, a, :, c, :], diag).then_inc(far_done, 1)
                for i, (g, a) in enumerate(pool_rows):
                    if i >= 2:
                        pool.wait_ge(p_used, i - 1)
                    score_product(pool, prod_p[i % 2], g, a).then_inc(p_done, 1)
                for r, rho, nh, ns, first in GROUPS:
                    out = pc[:, first * DH:(first + ns * 4 * nh) * DH].rearrange(
                        "p (s a b h d) -> p s a b h d", s=ns, a=2, b=2, h=nh)
                    for a in range(2):
                        for b in range(2):
                            pool.tensor_tensor(out[:, :, a, b, :, :], rows_of(qh, r, rho, ns, nh, a),
                                               key_rows(kh, r, rho, ns, b), ALU.mult).then_inc(pc_done, 1)
                pool.wait_ge(pc_done, 4 * len(GROUPS))
                pool.wait_ge(pv_go, 1)
                for r, rho, nh, ns, first in GROUPS:
                    out = pc[:, first * DH:(first + ns * 4 * nh) * DH].rearrange(
                        "p (s a b h d) -> p s a b h d", s=ns, a=2, b=2, h=nh)
                    wgt = sc[:, first:first + ns * 4 * nh].rearrange("p (s a b h) -> p s a b h", s=ns, a=2, b=2)
                    for a in range(2):
                        for b in range(2):
                            pool.tensor_tensor(out[:, :, a, b, :, :],
                                               wgt[:, :, a, b, :].unsqueeze(3).broadcast_to([P, ns, nh, DH]),
                                               key_rows(vh, r, rho, ns, b), ALU.mult).then_inc(pv_done, 1)
                pool.wait_ge(s0_go, 1)
                for i, (g, a) in enumerate(pool_rows):
                    if i >= 2:
                        pool.wait_ge(q_used, i - 1)
                    value_product(pool, prod_p[i % 2], g, a).then_inc(q_done, 1)

            @block.vector
            def _(dve):
                own = Chain(dve, own_sem)
                step = own.step
                tt = lambda out, a, b, op: step(dve.tensor_tensor(out, a, b, op))
                def reduce_scores(buf, g, a):
                    f, n = a * (a + 1) // 2, a + 1
                    return dve.tensor_reduce(s0[:, g, f:f + n, :],
                                             buf[:, 0:n * D].rearrange("p (b h d) -> p b h d", b=n, h=H), AX.X, ALU.add)

                def reduce_values(buf, g, a):
                    n = a + 1
                    return dve.tensor_reduce(o[:, g * SEG + a, :], buf[:, 0:n * D].rearrange("p (b x) -> p x b", b=n),
                                             AX.X, ALU.add)

                def level0(product, reduce, done, used, first):
                    i = 0
                    base = own.n
                    for j in range(len(dve_rows) + 1):
                        if j < len(dve_rows):
                            if j >= 2:
                                dve.wait_ge(own_sem, base + 2 * j - 1)
                            own.mark(product(dve, prod[j % 2], *dve_rows[j]))
                        if j > 0:
                            dve.wait_ge(own_sem, base + max(1, 2 * j - 2))
                            if reduce is reduce_values and dve_rows[j - 1][1] == 0:
                                own.settle()
                                own.mark(None)
                            else:
                                own.mark(reduce(prod[(j - 1) % 2], *dve_rows[j - 1]))
                        while i < len(pool_rows) * (j - first) // (len(dve_rows) - first):
                            dve.wait_ge(done, i + 1)
                            if reduce is reduce_values and pool_rows[i][1] == 0:
                                if i:
                                    dve.wait_ge(used, i)
                                dve.sem_inc(used, 1)
                            else:
                                reduce(prod_p[i % 2], *pool_rows[i]).then_inc(used, 1)
                            i += 1
                    own.settle()
                    dve.wait_ge(used, len(pool_rows))

                level0(score_product, reduce_scores, p_done, p_used, 2)
                dve.sem_inc(k_read, 1)
                dve.wait_ge(tabs, 48)
                s0f = s0[:, :, :, :].rearrange("p s n h -> p (s n h)")
                tt(s0f, s0f, cnt0[:, :], ALU.mult)
                dve.wait_ge(far_in, 16 * B)
                for r, ns, first in FGROUPS:
                    out = pf[:, first * DH:(first + ns * 4) * DH].rearrange("p (s a b d) -> p s a b d", s=ns, a=2, b=2)
                    for a in range(2):
                        qa = fq_[:, (2 + a) * r:(2 + a) * r + (ns - 1) * SEG * r + 1:SEG * r, :]
                        for b in range(2):
                            kb = fk_[:, b * r:b * r + (ns - 1) * SEG * r + 1:SEG * r, :]
                            own.mark(dve.tensor_tensor(out[:, :, a, b, :], qa, kb, ALU.mult))
                step(dve.memset(fo[:, :, DH:DH + 1], -1e30))
                step(dve.tensor_reduce(fs[:, :], pf[:, 0:NF * DH].rearrange("p (n d) -> p n d", d=DH), AX.X, ALU.add))
                tt(fs[:, :], fs[:, :], cntf[:, :], ALU.mult)
                step(dve.tensor_reduce(fx[:, :], fs[:, :].rearrange("p (n b) -> p n b", b=2), AX.X, ALU.max))

                def frows(c0, c1, r, ns):
                    return fo[:, :, c0:c1].rearrange("p (s q) c -> p s q c", q=SEG * r)[:, :, 2 * r:3 * r + 1:r, :]

                fxs = lambda buf, ns, first: buf[:, first // 2:(first + ns * 4) // 2].rearrange("p (s a c) -> p s a c", a=2, c=1)
                for r, ns, first in FGROUPS:
                    tt(frows(DH, DH + 1, r, ns), frows(DH, DH + 1, r, ns), fxs(fx, ns, first), ALU.max)
                for r, ns, first in FGROUPS:
                    own.mark(dve.tensor_copy(fxs(fm, ns, first), frows(DH, DH + 1, r, ns)))
                own.settle()
                dve.tensor_tensor(fs[:, :].rearrange("p (n b) -> p n b", b=2), fs[:, :].rearrange("p (n b) -> p n b", b=2),
                                  fm[:, :].unsqueeze(2).broadcast_to([HR, NF // 2, 2]), ALU.subtract).then_inc(e_req, 1)
                step(dve.memset(fo[:, :, 0:DH], 0.0))
                step(dve.memset(fo[:, :, DH + 1:DH + 2], 0.0))
                dve.wait_ge(e_done, 1)
                step(dve.tensor_reduce(fx[:, :], fs[:, :].rearrange("p (n b) -> p n b", b=2), AX.X, ALU.add))
                for r, ns, first in FGROUPS:
                    tt(frows(DH + 1, DH + 2, r, ns), frows(DH + 1, DH + 2, r, ns), fxs(fx, ns, first), ALU.add)
                for r, ns, first in FGROUPS:
                    out = pf[:, first * DH:(first + ns * 4) * DH].rearrange("p (s a b d) -> p s a b d", s=ns, a=2, b=2)
                    w = fs[:, first:first + ns * 4].rearrange("p (s a b) -> p s a b", a=2, b=2)
                    for a in range(2):
                        for b in range(2):
                            vb = fv_[:, b * r:b * r + (ns - 1) * SEG * r + 1:SEG * r, :]
                            own.mark(dve.tensor_tensor(out[:, :, a, b, :],
                                                       w[:, :, a, b].unsqueeze(2).broadcast_to([HR, ns, DH]), vb, ALU.mult))
                own.settle()
                pfh = pf[:, 0:NF * DH].rearrange("p (n b d) -> p n b d", b=2, d=DH)
                tt(pfh[:, :, 0, :], pfh[:, :, 0, :], pfh[:, :, 1, :], ALU.add)
                for i, (r, ns, first) in enumerate(FGROUPS):
                    part = pf[:, first * DH:(first + ns * 4) * DH].rearrange("p (s a b d) -> p s a b d", s=ns, a=2, b=2)
                    for a in range(2):
                        view = fo[:, :, 0:DH].rearrange("p (s q) c -> p s q c", q=SEG * r)[:, :, (2 + a) * r, :]
                        ins = dve.tensor_tensor(view, view, part[:, :, a, 0, :], ALU.add)
                        if i == len(FGROUPS) - 1 and a == 1:
                            ins.then_inc(fo_done, 1)
                        else:
                            step(ins)
                dve.wait_ge(pc_done, 4 * len(GROUPS))
                step(dve.tensor_reduce(sc[:, :], pc[:, 0:NC * DH].rearrange("p (n d) -> p n d", d=DH), AX.X, ALU.add))
                tt(sc[:, :], sc[:, :], cntc[:, :], ALU.mult)
                for a in range(SEG):
                    f = a * (a + 1) // 2
                    own.mark(dve.tensor_reduce(M[:, a:BL:SEG, :],
                                               s0[:, :, f:f + a + 1, :].rearrange("p s b h -> p s h b"), AX.X, ALU.max))
                own.settle()

                def parts(buf, r, rho, nh, ns, first):
                    return buf[:, first:first + ns * 4 * nh].rearrange("p (s a b h) -> p s a b h", s=ns, a=2, b=2)

                def halves(buf, r, rho, nh, ns, first):
                    return buf[:, first // 2:(first + ns * 4 * nh) // 2].rearrange("p (s a h) -> p s a h", s=ns, a=2)

                for g in GROUPS:
                    sp_ = parts(sc, *g)
                    hx = halves(scx, *g)
                    for a in range(2):
                        own.mark(dve.tensor_tensor(hx[:, :, a, :], sp_[:, :, a, 0, :], sp_[:, :, a, 1, :], ALU.max))
                own.settle()
                for gi, g in enumerate(GROUPS):
                    r, rho, nh, ns, first = g
                    if rho == 0:
                        own.settle()
                    for a in range(2):
                        m = rows_of(M, r, rho, ns, nh, a)
                        own.mark(dve.tensor_tensor(m, m, halves(scx, *g)[:, :, a, :], ALU.max))
                own.settle()
                dve.wait_ge(fb_in, 16 * B * 2)
                Mf = M[:, :, :].rearrange("p (a t) h -> p a (t h)", a=2)[:, :, 0:H * H:H + 1]
                Zf = Z[:, :, :].rearrange("p (a t) h -> p a (t h)", a=2)[:, :, 0:H * H:H + 1]
                tt(Mf, Mf, fb[:, :, :, DH], ALU.max)
                own.mark(dve.tensor_tensor(fg[:, :, :], fb[:, :, :, DH], Mf, ALU.subtract))
                for a in range(SEG):
                    f = a * (a + 1) // 2
                    for b in range(a + 1):
                        own.mark(dve.tensor_tensor(s0[:, :, f + b, :], s0[:, :, f + b, :], M[:, a:BL:SEG, :], ALU.subtract))
                own.settle()
                dve.sem_inc(e_req, 1)
                for g in GROUPS:
                    r, rho, nh, ns, first = g
                    for a in range(2):
                        own.mark(dve.tensor_copy(halves(mc, *g)[:, :, a, :], rows_of(M, r, rho, ns, nh, a)))
                own.settle()
                for g in GROUPS:
                    for b in range(2):
                        own.mark(dve.tensor_tensor(parts(sc, *g)[:, :, :, b, :], parts(sc, *g)[:, :, :, b, :],
                                                   halves(mc, *g), ALU.subtract))
                own.settle()
                dve.sem_inc(e_req, 1)
                dve.wait_ge(e_done, 3)
                for a in range(SEG):
                    f = a * (a + 1) // 2
                    own.mark(dve.tensor_reduce(Z[:, a:BL:SEG, :],
                                               s0[:, :, f:f + a + 1, :].rearrange("p s b h -> p s h b"), AX.X, ALU.add))
                dve.wait_ge(e_done, 4)
                for g in GROUPS:
                    sp_ = parts(sc, *g)
                    hx = halves(scx, *g)
                    for a in range(2):
                        own.mark(dve.tensor_tensor(hx[:, :, a, :], sp_[:, :, a, 0, :], sp_[:, :, a, 1, :], ALU.add))
                own.settle()
                for gi, g in enumerate(GROUPS):
                    r, rho, nh, ns, first = g
                    if rho == 0:
                        own.settle()
                    for a in range(2):
                        z = rows_of(Z, r, rho, ns, nh, a)
                        own.mark(dve.tensor_tensor(z, z, halves(scx, *g)[:, :, a, :], ALU.add))
                own.settle()
                fsum = fb[:, :, :, DH + 1]
                tt(fsum, fsum, fg[:, :, :], ALU.mult)
                tt(Zf, Zf, fsum, ALU.add)
                step(dve.reciprocal(Z[:, :, :], Z[:, :, :]))
                own.mark(dve.tensor_tensor(fg[:, :, :], fg[:, :, :], Zf, ALU.mult))
                for g in GROUPS:
                    r, rho, nh, ns, first = g
                    for a in range(2):
                        own.mark(dve.tensor_copy(halves(mc, *g)[:, :, a, :], rows_of(Z, r, rho, ns, nh, a)))
                own.settle()
                for gi, g in enumerate(GROUPS):
                    for b in range(2):
                        own.mark(dve.tensor_tensor(parts(sc, *g)[:, :, :, b, :], parts(sc, *g)[:, :, :, b, :],
                                                   halves(mc, *g), ALU.mult))
                own.settle()
                dve.sem_inc(pv_go, 1)
                for a in range(SEG):
                    f = a * (a + 1) // 2
                    for b in range(a + 1):
                        own.mark(dve.tensor_tensor(s0[:, :, f + b, :], s0[:, :, f + b, :], Z[:, a:BL:SEG, :], ALU.mult))
                own.settle()
                dve.sem_inc(s0_go, 1)
                level0(value_product, reduce_values, q_done, q_used, 8)
                oh = o.rearrange("p t (h d) -> p t h d", h=H)
                dve.wait_ge(pv_done, 4 * len(GROUPS))
                for lv in LOCAL:
                    for b in range(2):
                        own.settle()
                        for r, rho, nh, ns, first in GROUPS:
                            if r != 2 ** lv:
                                continue
                            part = pc[:, first * DH:(first + ns * 4 * nh) * DH].rearrange(
                                "p (s a b h d) -> p s a b h d", s=ns, a=2, b=2, h=nh)
                            for a in range(2):
                                x = rows_of(oh, r, rho, ns, nh, a)
                                own.mark(dve.tensor_tensor(x, x, part[:, :, a, b, :, :], ALU.add))
                own.settle()
                tt(fb[:, :, :, 0:DH], fb[:, :, :, 0:DH], fg[:, :, :].unsqueeze(3).broadcast_to([P, 2, H, DH]), ALU.mult)
                for a in range(2):
                    x = T["o_diag"](a)
                    own.mark(dve.tensor_tensor(x, x, fb[:, a, :, 0:DH], ALU.add))
                own.settle()


def attend_out(nc, T, W):
    with ExitStack() as ctx:
        S = Sems(nc, ctx, "ao_")
        sb = lambda name, shape, dt=F32: ctx.enter_context(nc.sbuf_tensor("ao_" + name, shape, dt))
        w = sb("w", [P, KD, D])
        bias = sb("bias", [P, D])
        xb = [sb(f"xb{i}", [P, D]) for i in range(2)]
        oc = [sb(f"oc{i}", [P, D]) for i in range(2)]
        oT = [sb(f"oT{i}", [P, KD, P]) for i in range(2)]
        rs_ = [sb(f"res{i}", [P, D]) for i in range(2)]
        xo = [sb(f"xo{i}", [P, D]) for i in range(2)]
        xT = [sb(f"xT{i}", [P, KD, P]) for i in range(2)]
        st = [sb(f"st{i}", [P, 6]) for i in range(2)]
        mv = [sb(f"mv{i}", [P, 2]) for i in range(2)]
        var = [sb(f"var{i}", [P, 1]) for i in range(2)]
        rs = [sb(f"rs{i}", [P, 1]) for i in range(2)]
        o, x2b, x3, ident = T["o"], T["x2b"], T["x1"], T["ident"]
        x2_in, w_in = T["x2_in"], S("w_in")
        oc_done, oT_full, oT_done, y_full, res_done, own_sem = (S("oc"), S("oT_full"), S("oT"), S("y_full"), S("res"), S("own"))
        var_done, rs_done, xo_done, xT_full, xT_done, g_full, lg_done = (S("var"), S("rs"), S("xo"), S("xT_full"),
                                                                       S("xT"), S("g_full"), S("lg"))
        xb_done, x3_done, stored = S("xb"), S("x3"), [S(f"stored{i}") for i in range(2)]

        with ExitStack() as pctx, nc.Block() as block:
            pT, pO, pX, pG = ([pctx.enter_context(nc.psum_tensor(f"ao_{nm}{i}", [P, 512], F32)) for i in range(2)]
                              for nm in ("pT", "pO", "pX", "pG"))

            @block.sync
            def _(sp):
                sp.dma_start(w[:, :, :], W["woT"].rearrange("(k p) n -> p k n", p=P)).then_inc(w_in, 16)
                sp.dma_start(bias[:, :], W["bo"].partition_broadcast(P)).then_inc(w_in, 16)
                sp.wait_ge(w_in, 32)
                for i in range(2):
                    sp.sem_inc(stored[i], 16)

                def body(s, h, q, on):
                    for dst, src in (((T["w1"], W["W1"]), (T["w2b"], W["W2"]))[q],):
                        sp.dma_start(dst[:, bass.ds(h, 1), :, :], src.rearrange("e (k p) n -> p e k n", p=P)[:, bass.ds(h, 1), :, :]
                                     ).then_inc(T["w1_in"], 16)
                    sp.wait_ge(xo_done, s + 3)
                    sp.dma_start(T["x3_d"].rearrange("(p i) d -> p i d", i=BL)[:, bass.ds(s, 1), :]
                                 .rearrange("p i d -> p (i d)"), xo[q][:, :]).then_inc(stored[q], 16)
                steps(sp, BL, 0, 2, body)
                for i in range(2):
                    sp.wait_ge(stored[i], 16 * (BL // 2 + 1))

            @block.gpsimd
            def _(pool):
                pool.wait_ge(x2_in, 16)
                pool.wait_ge(w_in, 32)

                def body(s, h, q, on):
                    if on(3):
                        t, r = s - 3, (q - 3) % 2
                        pool.wait_ge(var_done, t + 1)
                        pool.tensor_tensor(rs[r][:, :], var[r][:, :], T["half"][:, 0:1], ALU.pow).then_inc(rs_done, 1)
                    if on(0):
                        pool.wait_ge(res_done, s + 1)
                        hold(pool, T)
                        pool.tensor_tensor(xb[q][:, :], x2b[:, bass.ds(s, 1), :].rearrange("p a d -> p (a d)"),
                                           bias[:, :], ALU.add).then_inc(xb_done, 1)
                steps(pool, BL, 3, 2, body)

            @block.tensor
            def _(pe):
                pe.sem_inc(oT_full, 2)
                pe.sem_inc(y_full, 2)
                pe.sem_inc(xT_full, 2)
                pe.sem_inc(g_full, 2)
                pe.wait_ge(w_in, 32)

                def body(s, h, q, on):
                    if on(1):
                        t, r = s - 1, (q - 1) % 2
                        pe.wait_ge(oc_done, t + 1)
                        pe.wait_ge(oT_done, t + 1)
                        for k in range(KD):
                            mm = pe.transpose(pT[r][:, k * P:(k + 1) * P], oc[r][:, k * P:(k + 1) * P], ident[:, :])
                        mm.then_inc(oT_full, 1)
                    if on(2):
                        t, r = s - 2, q
                        pe.wait_ge(oT_done, t + 3)
                        pe.wait_ge(res_done, t + 1)
                        for k in range(KD):
                            mm = pe.matmul(pO[r][:, 0:D], oT[r][:, k, :], w[:, k, :], start=k == 0, stop=k == KD - 1)
                        mm.then_inc(y_full, 1)
                    if on(4):
                        t, r = s - 4, q
                        pe.wait_ge(xo_done, t + 3)
                        pe.wait_ge(xT_done, t + 1)
                        for k in range(KD):
                            mm = pe.transpose(pX[r][:, k * P:(k + 1) * P], xo[r][:, k * P:(k + 1) * P], ident[:, :])
                        mm.then_inc(xT_full, 1)
                    if on(5):
                        t, r = s - 5, (q - 5) % 2
                        pe.wait_ge(xT_done, t + 3)
                        pe.wait_ge(lg_done, t + 1)
                        for k in range(KD):
                            mm = pe.matmul(pG[r][:, 0:E_], xT[r][:, k, :], T["w_route"][:, k, :], start=k == 0, stop=k == KD - 1)
                        mm.then_inc(g_full, 1)
                steps(pe, BL, 5, 2, body)

            @block.scalar
            def _(act):
                act.sem_inc(oT_done, 2)
                act.sem_inc(xT_done, 2)
                act.sem_inc(x3_done, 2)
                act.sem_inc(lg_done, 2)

                def body(s, h, q, on):
                    if on(0):
                        act.wait_ge(oT_full, s + 1)
                        hold(act, T)
                        act.activation(oc[q][:, :], o[:, bass.ds(s, 1), :].rearrange("p a d -> p (a d)"),
                                       ACT.Identity).then_inc(oc_done, 1)
                    if on(1):
                        t, r = s - 1, (q - 1) % 2
                        act.wait_ge(oT_full, t + 3)
                        act.wait_ge(y_full, t + 1)
                        act.activation(oT[r][:, :, :].rearrange("p k n -> p (k n)"), pT[r][:, 0:D], ACT.Identity).then_inc(oT_done, 1)
                    if on(4):
                        t, r = s - 4, q
                        act.wait_ge(xT_full, t + 3)
                        act.wait_ge(g_full, t + 1)
                        act.activation(xT[r][:, :, :].rearrange("p k n -> p (k n)"), pX[r][:, 0:D], ACT.Identity).then_inc(xT_done, 1)
                        hold(act, T)
                        act.activation(x3[:, bass.ds(t, 1), :].rearrange("p a d -> p (a d)"), xo[r][:, :],
                                       ACT.Identity).then_inc(x3_done, 1)
                    if on(6):
                        t, r = s - 6, q
                        act.wait_ge(g_full, t + 3)
                        hold(act, T)
                        act.activation(T["logits"][:, bass.ds(t, 1), :].rearrange("p a e -> p (a e)"),
                                       pG[r][:, 0:E_], ACT.Identity).then_inc(lg_done, 1)
                steps(act, BL, 6, 2, body)
                act.wait_ge(lg_done, BL + 2)
                act.wait_ge(x3_done, BL + 2)

            @block.vector
            def _(dve):
                dve.sem_inc(res_done, 2)
                dve.sem_inc(xo_done, 2)

                def body(s, h, q, on):
                    if on(2):
                        t, r = s - 2, q
                        own = Chain(dve, own_sem, t, 2)
                        dve.wait_ge(y_full, t + 3)
                        dve.wait_ge(xb_done, t + 1)
                        dve.wait_ge(xo_done, t + 1)
                        dve.tensor_tensor(rs_[r][:, :], pO[r][:, 0:D], xb[r][:, :], ALU.add).then_inc(res_done, 1)
                        dve.wait_ge(res_done, t + 3)
                        own.step(dve.bn_stats(st[r][:, :], rs_[r][:, :]))
                        hold(dve, T)
                        own.step(dve.bn_aggr(mv[r][:, :], st[r][:, :]))
                        dve.tensor_scalar(var[r][:, :], mv[r][:, 1:2], EPS, None, ALU.add).then_inc(var_done, 1)
                        own.close()
                    if on(3):
                        t, r = s - 3, (q - 3) % 2
                        dve.wait_ge(rs_done, t + 1)
                        dve.wait_ge(stored[r], (h + (q - 3) // 2 + 1) * 16)
                        dve.wait_ge(xT_full, t + 1)
                        dve.wait_ge(x3_done, t + 1)
                        dve.tensor_scalar(xo[r][:, :], rs_[r][:, :], mv[r][:, 0:1], rs[r][:, 0:1],
                                          ALU.subtract, ALU.mult).then_inc(xo_done, 1)
                steps(dve, BL, 5, 2, body)


def experts1(nc, T, n, pre):
    with ExitStack() as ctx:
        S = Sems(nc, ctx, pre)
        sb = lambda name, shape, dt=F32: ctx.enter_context(nc.sbuf_tensor(pre + name, shape, dt))
        ix = [sb(f"ix{i}", [P, 4], I32) for i in range(2)]
        xg = [sb(f"xg{i}", [P, D]) for i in range(8)]
        xT = [sb(f"xT{i}", [P, KD, P]) for i in range(2)]
        hb = [sb(f"hb{i}", [P, D]) for i in range(2)]
        hn = [sb(f"hn{i}", [P, D]) for i in range(2)]
        hT = [sb(f"hT{i}", [P, KD, P]) for i in range(2)]
        yo = [sb(f"yo{i}", [P, D]) for i in range(2)]
        st = [sb(f"st{i}", [P, 6]) for i in range(2)]
        mv = [sb(f"mv{i}", [P, 2]) for i in range(2)]
        var = [sb(f"var{i}", [P, 1]) for i in range(2)]
        rs = [sb(f"rs{i}", [P, 1]) for i in range(2)]
        ident, w1, w2, b1, b2, g1, be1 = (T[k] for k in ("ident", "w1", "w2b", "b1", "b2", "g1", "be1"))
        ix_done, xT_full, xT_done, h_full, hb_done = S("ix_done"), S("xT_full"), S("xT_done"), S("h_full"), S("hb_done")
        own_sem, var_done, rs_done, hn_done = S("own"), S("var_done"), S("rs_done"), S("hn_done")
        hT_full, hT_done, y_full, y_done = S("hT_full"), S("hT_done"), S("y_full"), S("y_done")
        x_in = [S(f"x_in{i}") for i in range(8)]
        y_stored = [S(f"y_stored{i}") for i in range(2)]
        row = lambda ap, e: ap[:, bass.ds(e, 1), :].rearrange("p a n -> p (a n)")

        with ExitStack() as pctx, nc.Block() as block:
            pX, pH, pHT, pY = ([pctx.enter_context(nc.psum_tensor(f"{pre}{nm}{i}", [P, 512], F32))
                                for i in range(2)] for nm in ("pX", "pH", "pHT", "pY"))

            @block.gpsimd
            def _(pool):
                def body(s, h, q, on):
                    if on(0):
                        if q % 4 == 0:
                            pool.wait_ge(xT_full, s + 4)
                            hold(pool, T)
                            pool.tensor_copy(ix[q // 4][:, :], T["slot_tok"][:, bass.ds(s, 4)]).then_inc(ix_done, 1)
                            pool.wait_ge(ix_done, h * 2 + q // 4 + 1)
                            hold(pool, T)
                        pool.indirect_dma_start(xg[q][:, :], None, T["x3_d"],
                                                bass.IndirectOffsetOnAxis(ap=ix[q // 4][:, q % 4:q % 4 + 1], axis=0)).then_inc(x_in[q], 16)
                    if on(6):
                        t, r = s - 6, q % 2
                        pool.wait_ge(var_done, t + 1)
                        pool.tensor_tensor(rs[r][:, :], var[r][:, :], T["half"][:, 0:1], ALU.pow).then_inc(rs_done, 1)
                steps(pool, n, 6, 8, body)

            @block.sync
            def _(sp):
                for i in range(2):
                    sp.sem_inc(y_stored[i], 16)

                def body(s, h, q, on):
                    sp.wait_ge(y_done, s + 3)
                    sp.dma_start(T["y_d"][bass.ds(s * P, P), :], yo[q % 2][:, :]).then_inc(y_stored[q % 2], 16)
                steps(sp, n, 0, 4, body)
                for i in range(2):
                    sp.wait_ge(y_stored[i], 16 * (n // 2 + 1))

            @block.tensor
            def _(pe):
                pe.sem_inc(xT_full, 8)
                pe.sem_inc(h_full, 2)
                pe.sem_inc(hT_full, 2)
                pe.sem_inc(y_full, 2)
                pe.wait_ge(T["w1_in"], T["w1_n"])
                experts = Experts(pe, T, n)

                def body(s, h, q, on):
                    if on(0):
                        pe.wait_ge(x_in[q], (h + 1) * 16)
                        pe.wait_ge(xT_done, s + 1)
                        for k in range(KD):
                            mm = pe.transpose(pX[q % 2][:, k * P:(k + 1) * P], xg[q][:, k * P:(k + 1) * P], ident[:, :])
                        mm.then_inc(xT_full, 1)
                    experts.before(h, q)
                    if on(1):
                        t, r = s - 1, (q - 1) % 2
                        e = experts.of(q, 1)
                        pe.wait_ge(xT_done, t + 3)
                        pe.wait_ge(hb_done, t + 1)
                        for k in range(KD):
                            mm = pe.matmul(pH[r][:, 0:D], xT[r][:, k, :], row(w1[:, :, k, :], e),
                                           start=k == 0, stop=k == KD - 1)
                        mm.then_inc(h_full, 1)
                    experts.after(h, q)
                    if on(3):
                        t, r = s - 3, (q - 3) % 2
                        pe.wait_ge(hn_done, t + 3)
                        pe.wait_ge(hT_done, t + 1)
                        for k in range(KD):
                            mm = pe.transpose(pHT[r][:, k * P:(k + 1) * P], hn[r][:, k * P:(k + 1) * P], ident[:, :])
                        mm.then_inc(hT_full, 1)
                    if on(4):
                        t, r = s - 4, q % 2
                        e = experts.of(q, 4)
                        pe.wait_ge(hT_done, t + 3)
                        pe.wait_ge(y_done, t + 1)
                        for k in range(KD):
                            mm = pe.matmul(pY[r][:, 0:D], hT[r][:, k, :], row(w2[:, :, k, :], e),
                                           start=k == 0, stop=k == KD - 1)
                        mm.then_inc(y_full, 1)
                steps(pe, n, 4, 8, body)

            @block.scalar
            def _(act):
                act.sem_inc(xT_done, 2)
                act.sem_inc(hT_done, 2)
                act.wait_ge(T["w1_in"], T["w1_n"])
                experts = Experts(act, T, n)

                def body(s, h, q, on):
                    if on(0):
                        act.wait_ge(xT_full, s + 9)
                        act.wait_ge(h_full, s + 1)
                        act.activation(xT[q % 2][:, :, :].rearrange("p k n -> p (k n)"), pX[q % 2][:, 0:D],
                                       ACT.Identity).then_inc(xT_done, 1)
                    experts.before(h, q)
                    experts.after(h, q)
                    if on(3):
                        t, r = s - 3, (q - 3) % 2
                        e = experts.of(q, 3)
                        act.wait_ge(hT_full, t + 3)
                        act.wait_ge(y_full, t + 1)
                        hold(act, T)
                        for k in range(KD):
                            ins = act.activation(hT[r][:, k, :], pHT[r][:, k * P:(k + 1) * P], ACT.Gelu,
                                                 scale=g1[:, k, bass.ds(e, 1)], bias=be1[:, k, bass.ds(e, 1)])
                        ins.then_inc(hT_done, 1)
                steps(act, n, 4, 8, body)

            @block.vector
            def _(dve):
                dve.sem_inc(hb_done, 2)
                dve.sem_inc(hn_done, 2)
                dve.sem_inc(y_done, 2)
                dve.wait_ge(T["w1_in"], T["w1_n"])
                experts = Experts(dve, T, n)

                def body(s, h, q, on):
                    experts.before(h, q)
                    if on(1):
                        t, r = s - 1, (q - 1) % 2
                        own = Chain(dve, own_sem, t, 2)
                        e = experts.of(q, 1)
                        dve.wait_ge(h_full, t + 3)
                        dve.wait_ge(hn_done, t + 1)
                        dve.tensor_tensor(hb[r][:, :], pH[r][:, 0:D], row(b1, e), ALU.add).then_inc(hb_done, 1)
                        dve.wait_ge(hb_done, t + 3)
                        own.step(dve.bn_stats(st[r][:, :], hb[r][:, :]))
                        hold(dve, T)
                        own.step(dve.bn_aggr(mv[r][:, :], st[r][:, :]))
                        dve.tensor_scalar(var[r][:, :], mv[r][:, 1:2], EPS, None, ALU.add).then_inc(var_done, 1)
                        own.close()
                    experts.after(h, q)
                    if on(2):
                        t, r = s - 2, q % 2
                        dve.wait_ge(rs_done, t + 1)
                        dve.wait_ge(hT_full, t + 1)
                        dve.tensor_scalar(hn[r][:, :], hb[r][:, :], mv[r][:, 0:1], rs[r][:, 0:1],
                                          ALU.subtract, ALU.mult).then_inc(hn_done, 1)
                    if on(4):
                        t, r = s - 4, q % 2
                        e = experts.of(q, 4)
                        dve.wait_ge(y_full, t + 3)
                        dve.wait_ge(y_stored[r], (h * 4 + (q - 4) // 2 + 1) * 16)
                        dve.tensor_tensor(yo[r][:, :], pY[r][:, 0:D], row(b2, e), ALU.add).then_inc(y_done, 1)
                steps(dve, n, 4, 8, body)


SLOTS0 = 4 * NT + E_
SLOTS1 = 2 * NT + E_


def shape_tables():
    p, t = np.arange(P), np.arange(NT)
    c32 = np.zeros((P, 224), np.float32)
    c32[:, 0:E_] = E_ - np.arange(E_)
    c32[:, 16:48] = P * t
    c32[:, 48:192] = np.arange(SLOTS0)
    c32[:, 192:224] = BL * p[:, None] + t[None, :] - MID_ID
    c16 = np.zeros((P, 4 * SLOTS0 + 2 * P), np.float16)
    c16[:, 0:4 * SLOTS0] = np.repeat(np.arange(SLOTS0), 4)
    c16[:, 4 * SLOTS0:4 * SLOTS0 + P] = p[:, None] < p[None, :]
    c16[:, 4 * SLOTS0 + P:] = 1.0
    return c32, c16


def network(nc, W):
    with ExitStack() as ctx:
        def sb(name, shape, dt=F32):
            return ctx.enter_context(nc.sbuf_tensor(name, shape, dt))

        def sem(name):
            return ctx.enter_context(nc.semaphore(name))

        def dram(name, shape):
            return nc.dram_tensor(name, shape, F32, kind="Internal").ap()

        x = sb("x", [P, NT, D])
        R = sb("R", [P, CI * N])
        ident = sb("ident_sb", [P, P])
        half = sb("half", [P, NT])
        c32 = sb("c32_sb", [P, 224])
        c16 = sb("c16_sb", [P, 4 * SLOTS0 + 2 * P], F16)
        T = {
            "x1": x, "v": x, "ident": ident, "half": half, "zs": R[:, :].rearrange("p (c n) -> p c n", c=CI),
            "held": sem("held"), "w_ins": sem("ws_in"), "w0_in": sem("w0_in"), "w1_in": sem("w1_in"),
            "rope_in": sem("rope_in"), "x2_in": sem("x2_in"), "w_ns": 32, "w0_n": 32, "w1_n": 16 * (2 * E_ + 4),
            "mixed": dram("mixed", [2, N]), "states": dram("states", [N]),
            "x1_d": dram("x1_d", [N, D]), "x2_d": dram("x2_d", [N, D]), "x3_d": dram("x3_d", [N, D]),
            "y_d": dram("y_d", [SLOTS0 * P, D]),
            "far_d": dram("far_d", [P, 2, H, 3, DH]), "fo_d": dram("fo_d", [B * H, NJ, DH + 2]),
            "w13s": sb("w13s", [P, KD, 2 * IN0]), "w2s": sb("w2s", [P, D]),
            "w_gate": sb("w_gate", [P, KD, E_]), "w_route": sb("w_route", [P, KD, E_]),
            "w13": R[:, 0:E_ * KD * 2 * IN0].rearrange("p (e k n) -> p e k n", e=E_, k=KD),
            "w2": R[:, E_ * KD * 2 * IN0:E_ * KD * 2 * IN0 + E_ * D].rearrange("p (e n) -> p e n", e=E_),
            "area": R[:, 0:KD * N], "rope_n": 16 * BL // 8,
            "rope": R[:, KD * N:KD * N + BL * D].rearrange("p (t a n) -> p t a n", t=BL, a=2),
            "logits": sb("logits", [P, NT, E_]),
            "tile_exp": sb("tile_exp", [1, 2 * (SLOTS0 // 8 + 1)], I32), "slot_tok": sb("slot_tok", [P, SLOTS0], I32),
            "slot_of": sb("slot_of", [P, NT, 4], I32), "slot_w": sb("slot_w", [P, NT, 4]),
            "c32": {"rev": c32[:, 0:16], "thr": c32[:, 16:48], "iota": c32[:, 48:192]},
            "c16": {"iota": c16[:, 0:4 * SLOTS0].rearrange("p (n k) -> p n k", k=4),
                    "tri": c16[:, 4 * SLOTS0:4 * SLOTS0 + P], "ones": c16[:, 4 * SLOTS0 + P:]},
        }
        route_b = [sb(f"route_b{i}", [P, E_]) for i in range(2)]
        T["route_b"] = route_b[0]
        T["w_qkv_in"], T["x1_in"] = sem("w_qkv_in"), sem("x1_in")
        T["logits_out"], T["logits_in"] = sem("logits_out"), sem("logits_in")
        T["logits_d"] = dram("logits_d", [N, E_])
        early, half_done = sem("early"), sem("half_done")
        T["early"], T["early_n"] = early, 16 * 6
        stage_sems = range(half_done.num + 1, 256)

        with nc.Block() as block:
            @block.gpsimd
            def _(pool):
                pool.memset(half[:, :], -0.5).then_inc(half_done, 1)
                pool.wait_ge(half_done, 1)

        def early_loads(sp):
            for dst, src, s in (
                    (T["w13s"][:, :, :], W["w13s"].rearrange("(k p) n -> p k n", p=P), T["w_ins"]),
                    (T["w2s"][:, :], W["w2s"], T["w_ins"]),
                    (T["w_gate"][:, :, :], W["gateT"].rearrange("(k p) e -> p k e", p=P), early),
                    (T["w_route"][:, :, :], W["Wr"].rearrange("(k p) e -> p k e", p=P), early),
                    (route_b[0][:, :], W["gate_b"].partition_broadcast(P), early),
                    (route_b[1][:, :], W["br"].partition_broadcast(P), early),
                    (c32[:, :], W["c32"], early),
                    (c16[:, :], W["c16"], early)):
                sp.dma_start(dst, src).then_inc(s, 16)

        T["early_loads"] = early_loads
        mixer(nc, T, W)

        with nc.Block() as block:
            @block.gpsimd
            def _(pool):
                pool.sem_clear(stage_sems)

            @block.sync
            def _(sp):
                sp.dma_start(T["logits"][:, :, :], T["logits_d"].rearrange("(p i) e -> p i e", i=BL)).then_inc(T["logits_in"], 16)
                sp.wait_ge(T["logits_in"], 16)
                sp.dma_start(x[:, :, :], T["x1_d"].rearrange("(p i) d -> p i d", i=BL)).then_inc(T["x1_in"], 16)
                sp.dma_start(T["w13"], W["w13T"].rearrange("e (k p) n -> p e k n", p=P)).then_inc(T["w0_in"], 16)
                sp.dma_start(T["w2"], W["w2T"].rearrange("e p n -> p e n")).then_inc(T["w0_in"], 16)

        dispatch(nc, T, 4, SLOTS0, True, c32[:, 192:224], "d0_")
        experts0(nc, T, SLOTS0, "e0_")

        T.update({"rope_d": W["rope"], "w_qkv_d": W["wqkvT"], "b_qkv_d": W["bqkv"]})
        with ExitStack() as actx:
            T["w_qkv"] = actx.enter_context(nc.sbuf_tensor("w_qkv", [P, (KD + 1) * 3 * D], F32))

            qk = actx.enter_context(nc.sbuf_tensor("qk", [P, BL, 2 * D], F32))
            flat = qk[:, :, :].rearrange("p t n -> p (t n)")
            n_c, n_f, n_far = NC * DH, NF * DH, 2 * H * 3 * DH
            T.update({
                "qk": qk, "o": qk[:, :, 0:D], "x2b": qk[:, :, D:2 * D],
                "o_diag": lambda a: bass.AP(flat.tensor, a * H * 2 * D, [flat.ap[0], [2 * D + DH, H], [1, DH]]),
                "prodc": R[:, 0:n_c], "prodf": R[:, n_c:n_c + n_f],
                "far": R[:, n_c + n_f:n_c + n_f + n_far].rearrange("p (a h c d) -> p a h c d", a=2, h=H, c=3),
                "fq": R[0:B * H, n_c + n_f + n_far:n_c + n_f + n_far + NJ * 3 * DH]
                .rearrange("p (j c d) -> p j c d", j=NJ, c=3),
                "prodp": R[:, n_c + n_f + n_far + NJ * 3 * DH:],
            })
            x2_rows = T["x2_d"].rearrange("(p i) d -> p i d", i=BL)
            combine(nc, T, 4, x, lambda s: x2_rows[:, bass.ds(s, 1), :].rearrange("p i d -> p (i d)"), True, "c0_")
            attend(nc, T, W)
            T["w1"] = R[:, 0:E_ * KD * D].rearrange("p (e k n) -> p e k n", e=E_, k=KD)
            T["w2b"] = R[:, E_ * KD * D:2 * E_ * KD * D].rearrange("p (e k n) -> p e k n", e=E_, k=KD)
            attend_out(nc, T, W)

        T["b1"], T["b2"] = sb("b1", [P, E_, D]), sb("b2", [P, E_, D])
        T["g1"], T["be1"] = sb("g1", [P, KD, E_]), sb("be1", [P, KD, E_])
        T["route_b"] = route_b[1]
        with nc.Block() as block:
            @block.gpsimd
            def _(pool):
                pool.sem_clear(stage_sems)

            @block.sync
            def _(sp):
                for dst, src in ((T["b1"], W["b1"]), (T["b2"], W["b2"])):
                    sp.dma_start(dst[:, :, :].rearrange("p e n -> p (e n)"),
                                 src.rearrange("e n -> (e n)").partition_broadcast(P)).then_inc(T["w1_in"], 16)
                for dst, src in ((T["g1"], W["g1T"]), (T["be1"], W["be1T"])):
                    sp.dma_start(dst[:, :, :], src.rearrange("(k p) e -> p k e", p=P)).then_inc(T["w1_in"], 16)

        dispatch(nc, T, 2, SLOTS1, False, c32[:, 192:224], "d1_")
        experts1(nc, T, SLOTS1, "e1_")
        out = W["out"].rearrange("(p i) d -> p i d", i=BL)
        combine(nc, T, 2, x, lambda s: out[:, bass.ds(s, 1), :].rearrange("p i d -> p (i d)"), False, "c1_")


def layouts(inputs):
    a = {k: np.asarray(v) for k, v in inputs.items()}
    m, f, t, g = (lambda n, p=p: a[p + n] for p in ("L0_attn_", "L0_ffn_", "L1_attn_", "L1_ffn_"))
    cnt0, cntc, cntf = count_tables()
    c32, c16 = shape_tables()
    out = {"x": m("x").reshape(N, D), "xT": m("x").reshape(N, D).T}
    for n in ("W_in", "W_conv", "W_xproj", "W_dt", "b_dt", "W_out"):
        out[n] = m(n)
    out.update({
        "ln_g": m("ln_g").reshape(CI, P).T, "ln_b": m("ln_b").reshape(CI, P).T, "ident": np.eye(P, dtype=np.float32),
        "gateT": f("gate_w").T, "gate_b": f("gate_b"), "w13T": f("w13").transpose(0, 2, 1),
        "w2T": f("w2").transpose(0, 2, 1), "w13s": f("w13_s").T, "w2s": f("w2_s").T,
        "wqkvT": np.concatenate([t("Wq"), t("Wk"), t("Wv")]).T, "bqkv": np.concatenate([t("bq"), t("bk"), t("bv")]),
        "woT": t("Wo").T, "bo": t("bo"), "rope": rope_tables(), "cnt0": cnt0, "cntc": cntc, "cntf": cntf,
        "Wr": g("Wr"), "br": g("br"), "W1": g("W1"), "b1": g("b1"), "W2": g("W2"), "b2": g("b2"),
        "g1T": g("g1").T, "be1T": g("be1").T, "c32": c32, "c16": c16})
    return {k: np.ascontiguousarray(v) for k, v in out.items()}


def kernel(**inputs):
    import concourse.bacc as bacc
    from concourse.bass_utils import run_bass_kernel_spmd

    nc = bacc.Bacc("TRN2", target_bir_lowering=False, num_devices=1)
    arrays = layouts(inputs)
    W = {name: nc.dram_tensor("in_" + name, a.shape, mybir.dt.from_np(a.dtype), kind="ExternalInput").ap()
         for name, a in arrays.items()}
    W["out"] = nc.dram_tensor("out_x", (N, D), F32, kind="ExternalOutput").ap()
    network(nc, W)
    r = run_bass_kernel_spmd(nc, [{"in_" + name: a for name, a in arrays.items()}], core_ids=[0])
    return r.results[0]["out_x"].reshape(B, L, D)
```
